# Optimizing a Trainium2 kernel written in Bass

```python
import numpy as np
import jax
import jax.numpy as jnp

def _softmax(x, axis=-1):
    return jax.nn.softmax(x, axis=axis)

def _gelu(x):
    return jax.nn.gelu(x, approximate=True)

def _silu(x):
    return jax.nn.silu(x)

def _sigmoid(x):
    return jax.nn.sigmoid(x)

def _layernorm(x, axis=-1, eps=1e-05):
    m = jnp.mean(x, axis=axis, keepdims=True)
    v = jnp.var(x, axis=axis, keepdims=True)
    return (x - m) / jnp.sqrt(v + eps)

def _scatter_add(tgt, idx, src, axis=0):
    return tgt.at[idx].add(src)

def _segment_sum(src, seg, n):
    return jax.ops.segment_sum(src, seg, n)
kernel_name = 'mk_flamingo_gated_d2_seqx_r8_eeee47'

def setup_inputs(seed: int=0):
    np.random.seed(seed)
    _w = jnp.asarray

    def _rec_inputs():
        import jax
        import jax.numpy as jnp
        _rk = jax.random.key(seed)
        x = -0.000125 + 0.9999 * jax.random.normal(jax.random.fold_in(_rk, 1), (16, 128, 128), jnp.float32)
        _lenS = 128 - jax.random.randint(jax.random.fold_in(_rk, 7), (16,), 0, max(1, 128 // 4) + 1, jnp.int32)
        _lenS2 = 77 - jax.random.randint(jax.random.fold_in(_rk, 8), (16,), 0, max(1, 77 // 4) + 1, jnp.int32)
        _ctx_768P = jax.random.normal(jax.random.fold_in(_rk, 11), (16, 16, 96), jnp.float32)
        _ctx_768c = jax.random.dirichlet(jax.random.fold_in(_rk, 511), 0.3 * jnp.ones((16,), jnp.float32), (16, 77))
        _ctx_768t = jnp.einsum('bsk,bkd->bsd', _ctx_768c, _ctx_768P)
        _ctx_768t = _ctx_768t * jax.lax.rsqrt(jnp.mean(jnp.square(_ctx_768t)) + 1e-12) * 0.953939
        ctx_768 = 0.00272024 + 0.999456 * (_ctx_768t + 0.3 * jax.random.normal(jax.random.fold_in(_rk, 611), (16, 77, 96), jnp.float32))
        _validS = jnp.arange(128)[None, :] < _lenS[:, None]
        _validS2 = jnp.arange(77)[None, :] < _lenS2[:, None]
        _causal = jnp.tril(jnp.ones((128, 128), dtype=bool))
        mask_BxS_bk0 = jnp.logical_not(jnp.broadcast_to(_validS[:, :], (16, 128)))
        _g = jax.random.normal(jax.random.fold_in(_rk, 9001), (2, 2), jnp.float32)
        _g = jnp.sign(_g) * jnp.maximum(jnp.abs(_g), 1.0) + (_g == 0) * 1.0
        g_xattn = _g[0]
        g_ffn = _g[1]
        return (x, ctx_768, mask_BxS_bk0, g_xattn, g_ffn)
    x, ctx_768, mask_BxS_bk0, g_xattn, g_ffn = _rec_inputs()

    def _L0_xattn_setup():
        import jax, jax.numpy as jnp
        import numpy as np
        N_HEADS = 16
        DIM_EMBED = 128
        DIM_CROSS = 96
        DIM_HEAD = DIM_EMBED // N_HEADS
        key = jax.random.key(seed)
        ks = jax.random.split(key, 10)
        B, Sq, Sk = (8, 512, 77)
        s_e = 1.0 / np.sqrt(DIM_EMBED)
        s_c = 1.0 / np.sqrt(DIM_CROSS)
        return {'x': jax.random.normal(ks[0], (B, Sq, DIM_EMBED), jnp.float32), 'y': jax.random.normal(ks[1], (B, Sk, DIM_CROSS), jnp.float32), 'wq': jax.random.normal(ks[2], (DIM_EMBED, DIM_EMBED), jnp.float32) * s_e, 'bq': jax.random.normal(ks[3], (DIM_EMBED,), jnp.float32) * 0.01, 'wk': jax.random.normal(ks[4], (DIM_CROSS, DIM_EMBED), jnp.float32) * s_c, 'bk': jax.random.normal(ks[5], (DIM_EMBED,), jnp.float32) * 0.01, 'wv': jax.random.normal(ks[6], (DIM_CROSS, DIM_EMBED), jnp.float32) * s_c, 'bv': jax.random.normal(ks[7], (DIM_EMBED,), jnp.float32) * 0.01, 'wo': jax.random.normal(ks[8], (DIM_EMBED, DIM_EMBED), jnp.float32) * s_e, 'bo': jax.random.normal(ks[9], (DIM_EMBED,), jnp.float32) * 0.01}
    _L0_xattn_all = _L0_xattn_setup()
    _L0_xattn_in = {k: v for k, v in _L0_xattn_all.items() if k in ('wq', 'bq', 'wk', 'bk', 'wv', 'bv', 'wo', 'bo')}
    del _L0_xattn_all

    def _L0_ffn_setup():
        import jax, jax.numpy as jnp
        import numpy as np
        HIDDEN = 128
        INTER = 256
        NUM_EXPERTS = 8
        TOPK = 2
        STD = 0.02
        key = jax.random.key(seed)
        k1, k2, k3, k4 = jax.random.split(key, 4)
        return {'hidden_states': jax.random.normal(k1, (1, 256, HIDDEN), dtype=jnp.float32), 'w1': jax.random.normal(k2, (NUM_EXPERTS, 2 * INTER, HIDDEN), dtype=jnp.float32) * STD, 'w2': jax.random.normal(k3, (NUM_EXPERTS, HIDDEN, INTER), dtype=jnp.float32) * STD, 'router_w': jax.random.normal(k4, (NUM_EXPERTS, HIDDEN), dtype=jnp.float32) * STD}
    _L0_ffn_all = _L0_ffn_setup()
    _L0_ffn_in = {k: v for k, v in _L0_ffn_all.items() if k in ('w1', 'w2', 'router_w')}
    del _L0_ffn_all

    def _L1_xattn_setup():
        import jax, jax.numpy as jnp
        import numpy as np
        NUM_HEADS = 16
        key = jax.random.key(seed)
        k1, k2, k3, k4, k5 = jax.random.split(key, 5)
        B, N, C = (4, 256, 128)
        N2, Cy = (128, 96)
        x = jax.random.normal(k1, (B, N, C), dtype=jnp.float32)
        y = jax.random.normal(k2, (B, N2, Cy), dtype=jnp.float32)
        pad_mask = jax.random.randint(k3, (B, N), 0, 2).astype(jnp.bool_)
        Wq = jax.random.normal(k4, (C, C), dtype=jnp.float32) * C ** (-0.5)
        Wkv = jax.random.normal(k5, (2 * C, Cy), dtype=jnp.float32) * Cy ** (-0.5)
        return {'x': x, 'y': y, 'pad_mask': pad_mask, 'Wq': Wq, 'Wkv': Wkv}
    _L1_xattn_all = _L1_xattn_setup()
    _L1_xattn_in = {k: v for k, v in _L1_xattn_all.items() if k in ('Wq', 'Wkv')}
    del _L1_xattn_all

    def _L1_ffn_setup():
        import jax, jax.numpy as jnp
        import numpy as np
        DIM = 128

        def _reference_tuple_inner(x, W_r, W_k, W_v, mu_r, mu_k):
            B, T, C = x.shape
            x_prev = jnp.concatenate([jnp.zeros((B, 1, C), x.dtype), x[:, :-1, :]], axis=1)
            xr = mu_r * x + (1.0 - mu_r) * x_prev
            xk = mu_k * x + (1.0 - mu_k) * x_prev
            r = jax.nn.sigmoid(jnp.einsum('btc,dc->btd', xr, W_r))
            k = jnp.einsum('btc,dc->btd', xk, W_k)
            k_act = jnp.square(jax.nn.relu(k))
            out = r * jnp.einsum('btc,dc->btd', k_act, W_v)
            new_state = x[:, -1, :]
            return (out, new_state)
        key = jax.random.key(seed)
        ks = jax.random.split(key, 6)
        B, T, C = (8, 256, DIM)
        x = jax.random.normal(ks[0], (B, T, C), dtype=jnp.float32)
        s = 1.0 / np.sqrt(C)
        W_r = jax.random.uniform(ks[1], (C, C), jnp.float32, -s, s)
        W_k = jax.random.uniform(ks[2], (C, C), jnp.float32, -s, s)
        W_v = jax.random.uniform(ks[3], (C, C), jnp.float32, -s, s)
        mu_r = jax.random.uniform(ks[4], (C,), jnp.float32)
        mu_k = jax.random.uniform(ks[5], (C,), jnp.float32)
        return {'x': x, 'W_r': W_r, 'W_k': W_k, 'W_v': W_v, 'mu_r': mu_r, 'mu_k': mu_k}
    _L1_ffn_all = _L1_ffn_setup()
    _L1_ffn_in = {k: v for k, v in _L1_ffn_all.items() if k in ('W_r', 'W_k', 'W_v', 'mu_r', 'mu_k')}
    del _L1_ffn_all
    return {'x': x, 'ctx_768': ctx_768, 'mask_BxS_bk0': mask_BxS_bk0, 'g_xattn': g_xattn, 'g_ffn': g_ffn, 'L0_xattn_wq': _L0_xattn_in['wq'], 'L0_xattn_bq': _L0_xattn_in['bq'], 'L0_xattn_wk': _L0_xattn_in['wk'], 'L0_xattn_bk': _L0_xattn_in['bk'], 'L0_xattn_wv': _L0_xattn_in['wv'], 'L0_xattn_bv': _L0_xattn_in['bv'], 'L0_xattn_wo': _L0_xattn_in['wo'], 'L0_xattn_bo': _L0_xattn_in['bo'], 'L0_ffn_w1': _L0_ffn_in['w1'], 'L0_ffn_w2': _L0_ffn_in['w2'], 'L0_ffn_router_w': _L0_ffn_in['router_w'], 'L1_xattn_Wq': _L1_xattn_in['Wq'], 'L1_xattn_Wkv': _L1_xattn_in['Wkv'], 'L1_ffn_W_r': _L1_ffn_in['W_r'], 'L1_ffn_W_k': _L1_ffn_in['W_k'], 'L1_ffn_W_v': _L1_ffn_in['W_v'], 'L1_ffn_mu_r': _L1_ffn_in['mu_r'], 'L1_ffn_mu_k': _L1_ffn_in['mu_k']}

def reference(x, ctx_768, mask_BxS_bk0, g_xattn, g_ffn, L0_xattn_wq, L0_xattn_bq, L0_xattn_wk, L0_xattn_bk, L0_xattn_wv, L0_xattn_bv, L0_xattn_wo, L0_xattn_bo, L0_ffn_w1, L0_ffn_w2, L0_ffn_router_w, L1_xattn_Wq, L1_xattn_Wkv, L1_ffn_W_r, L1_ffn_W_k, L1_ffn_W_v, L1_ffn_mu_r, L1_ffn_mu_k):
    import jax
    import jax.numpy as jnp

    def _L0_xattn_ref(x, y, wq, bq, wk, bk, wv, bv, wo, bo):
        import jax, jax.numpy as jnp
        import numpy as np
        N_HEADS = 16
        DIM_EMBED = 128
        DIM_CROSS = 96
        DIM_HEAD = DIM_EMBED // N_HEADS
        B, Sq, E = x.shape
        H, D = (N_HEADS, DIM_HEAD)
        q = (x @ wq + bq).reshape(B, Sq, H, D).transpose(0, 2, 1, 3)
        k = (y @ wk + bk).reshape(B, -1, H, D).transpose(0, 2, 1, 3)
        v = (y @ wv + bv).reshape(B, -1, H, D).transpose(0, 2, 1, 3)
        scores = jnp.einsum('bhqd,bhkd->bhqk', q, k) / jnp.sqrt(jnp.asarray(D, x.dtype))
        attn = jax.nn.softmax(scores, axis=-1)
        out = jnp.einsum('bhqk,bhkd->bhqd', attn, v)
        out = out.transpose(0, 2, 1, 3).reshape(B, Sq, E)
        return out @ wo + bo

    def _L0_ffn_ref(hidden_states, w1, w2, router_w):
        import jax, jax.numpy as jnp
        import numpy as np
        HIDDEN = 128
        INTER = 256
        NUM_EXPERTS = 8
        TOPK = 2
        STD = 0.02
        orig_shape = hidden_states.shape
        dtype = hidden_states.dtype
        x = hidden_states.reshape(-1, orig_shape[-1])
        E = w1.shape[0]
        gating = x @ router_w.T
        probs = jax.nn.softmax(gating.astype(jnp.float32), axis=-1)
        topk_w, sel = jax.lax.top_k(probs, TOPK)
        topk_w = topk_w.astype(dtype)
        combine = (jax.nn.one_hot(sel, E, dtype=dtype) * topk_w[..., None]).sum(axis=1)
        h = jnp.einsum('td,eid->tei', x, w1)
        gate = jax.nn.silu(h[..., :INTER])
        y = h[..., INTER:] * gate
        out = jnp.einsum('tei,ehi,te->th', y, w2, combine)
        return out.reshape(orig_shape)

    def _L1_xattn_ref(x, y, pad_mask, Wq, Wkv):
        import jax, jax.numpy as jnp
        import numpy as np
        NUM_HEADS = 16
        B, N, C = x.shape
        N2 = y.shape[1]
        H = NUM_HEADS
        d = C // H
        scale = d ** (-0.5)
        q = (x @ Wq.T).reshape(B, N, H, d).transpose(0, 2, 1, 3)
        kv = (y @ Wkv.T).reshape(B, N2, 2, H, d).transpose(2, 0, 3, 1, 4)
        k, v = (kv[0], kv[1])
        attn = jnp.einsum('bhnd,bhmd->bhnm', q * scale, k)
        attn = jnp.where(pad_mask[:, None, :, None], attn, jnp.float32(-1000000000.0))
        attn = jax.nn.softmax(attn, axis=-1)
        out = jnp.einsum('bhnm,bhmd->bhnd', attn, v)
        return out.transpose(0, 2, 1, 3).reshape(B, N, C)

    def _L1_ffn_ref(x, W_r, W_k, W_v, mu_r, mu_k):
        import jax, jax.numpy as jnp
        import numpy as np
        DIM = 128

        def _reference_tuple_inner(x, W_r, W_k, W_v, mu_r, mu_k):
            B, T, C = x.shape
            x_prev = jnp.concatenate([jnp.zeros((B, 1, C), x.dtype), x[:, :-1, :]], axis=1)
            xr = mu_r * x + (1.0 - mu_r) * x_prev
            xk = mu_k * x + (1.0 - mu_k) * x_prev
            r = jax.nn.sigmoid(jnp.einsum('btc,dc->btd', xr, W_r))
            k = jnp.einsum('btc,dc->btd', xk, W_k)
            k_act = jnp.square(jax.nn.relu(k))
            out = r * jnp.einsum('btc,dc->btd', k_act, W_v)
            new_state = x[:, -1, :]
            return (out, new_state)
        return _reference_tuple_inner(x, W_r, W_k, W_v, mu_r, mu_k)[0]
    x = x + jnp.tanh(g_xattn[0]) * _L0_xattn_ref(_layernorm(x, axis=-1), ctx_768, L0_xattn_wq, L0_xattn_bq, L0_xattn_wk, L0_xattn_bk, L0_xattn_wv, L0_xattn_bv, L0_xattn_wo, L0_xattn_bo)
    x = x + jnp.tanh(g_ffn[0]) * _L0_ffn_ref(_layernorm(x, axis=-1), L0_ffn_w1, L0_ffn_w2, L0_ffn_router_w)
    x = x + jnp.tanh(g_xattn[1]) * _L1_xattn_ref(_layernorm(x, axis=-1), ctx_768, mask_BxS_bk0, L1_xattn_Wq, L1_xattn_Wkv)
    x = x + jnp.tanh(g_ffn[1]) * _L1_ffn_ref(_layernorm(x, axis=-1), L1_ffn_W_r, L1_ffn_W_k, L1_ffn_W_v, L1_ffn_mu_r, L1_ffn_mu_k)
    return x

_drawn_inputs = setup_inputs


def setup_inputs(seed=0):
    import zlib

    import numpy as np

    out = dict(_drawn_inputs(seed))
    spreads = {'g_ffn': (-1.0, 0.6)}
    factors = {'L0_xattn_bq': 8.0,
     'L0_xattn_bk': 64.0,
     'L0_xattn_bv': 8.0,
     'L0_xattn_bo': 7.837,
     'L0_ffn_w1': 8.0,
     'L0_ffn_w2': 8.0,
     'L0_ffn_router_w': 8.0,
     'L1_ffn_W_r': 3.77,
     'L1_ffn_mu_r': 26.313,
     'L1_ffn_mu_k': 2.727}
    for name, (base, spread) in spreads.items():
        noise = np.random.default_rng([zlib.crc32(name.encode()), seed]).standard_normal(out[name].shape)
        drawn = base * np.exp(spread * noise) if base else spread * noise
        out[name] = jnp.asarray(drawn.astype(out[name].dtype))
    for name, factor in factors.items():
        out[name] = (out[name] * factor).astype(out[name].dtype)
    return out
```

```python
from contextlib import ExitStack

import concourse.bass as bass
from concourse import mybir

F32 = mybir.dt.float32
F32R = mybir.dt.float32r
U8 = mybir.dt.uint8
ALU = mybir.AluOpType
ACT = mybir.ActivationFunctionType
AX = mybir.AxisListType

P = 128
KM = 64
KR = 16
LN_EPS = 1e-5


def flamingo_kernel(nc, x, ctx_768, mask_BxS_bk0, g_xattn, g_ffn, wq0, bq0, wk0, bk0, wv0, bv0, wo0, bo0,
                    w1, w2, router_w, wq1, wkv1, w_r, w_k, w_v, mu_r, mu_k, out):
    B, S, D = x.shape
    _, S2, DC = ctx_768.shape
    E, I2, _ = w1.shape
    I = I2 // 2
    H = 16
    DH = D // H
    SCALE = float(DH) ** -0.5
    NR = S2 - KM
    MAIN, REST = H * KM, H * KR
    COLS = MAIN + REST
    CH = COLS // P
    CM = MAIN // P
    NQ = B // 4
    assert S == P and D == P and H * DH == P and 0 < NR <= KR and B % 4 == 0 and E == 8 and I == 2 * P

    with ExitStack() as ctx:
        def sb(name, shape, dt=F32, stack=ctx):
            return stack.enter_context(nc.sbuf_tensor(name, shape, dt))

        def sem(name, stack=ctx):
            return stack.enter_context(nc.semaphore(name))

        bank = [ctx.enter_context(nc.psum_tensor(f"bank{i}", [P, 512], F32)) for i in range(5)]
        scores_ps = ctx.enter_context(nc.psum_tensor("scores_ps", [P, 3 * 512], F32))

        def pbank(i):
            return bank[i][:, :] if i < 5 else scores_ps[:, (i - 5) * 512:(i - 4) * 512]

        xs = sb("xs", [P, B, D])
        mv = sb("mv", [P, B, 2])
        rstd = sb("rstd", [P, B])
        veps = sb("veps", [P, B])
        neg_half = sb("neg_half", [P, B])
        bns = sb("bns", [P, B, 2, 3])
        st = sb("st", [P, 3, B])
        ident = sb("ident", [P, P])
        tg = sb("tg", [P, 4])
        kT = sb("kT", [P, 2, B, S2])
        vc = sb("vc", [P, B, 2, 2, D])
        head_mask = sb("head_mask", [P, H])
        main_mask = sb("main_mask", [P, 2 * DH])
        rest_mask = sb("rest_mask", [P, 8])
        wq0_sb = sb("wq0_sb", [P, D])
        bq_col = sb("bq_col", [P, 1])
        wo_tg = sb("wo_tg", [P, D])
        bias_bc = sb("bias_bc", [P, D])
        wq1T = sb("wq1T", [P, D])
        valid = sb("valid", [P, B])
        w_rT = sb("w_rT", [P, D])
        w_kT = sb("w_kT", [P, D])
        w_vT = sb("w_vT", [P, D])
        mus = sb("mus", [P, 4])
        routerT = sb("routerT", [P, E])
        w1h = sb("w1h", [P, E, I2], F32R)
        w1l = sb("w1l", [P, E, I2], F32R)
        w2h = sb("w2h", [P, E, 2, D], F32R)
        w2l = sb("w2l", [P, E, 2, D], F32R)

        x_loaded = [sem(f"x_loaded{q}") for q in range(NQ)]
        out_stored = sem("out_stored")

        def finish_stats(dve, stats_step):
            even, odd = bns[:, :, 0, :], bns[:, :, 1, :]
            dve.tensor_tensor(st[:, 0, :], even[:, :, 1], odd[:, :, 1], ALU.subtract).then_inc(stats_step, 1)
            dve.tensor_tensor(st[:, 1, :], even[:, :, 1], odd[:, :, 1], ALU.add).then_inc(stats_step, 1)
            dve.tensor_tensor(st[:, 2, :], even[:, :, 2], odd[:, :, 2], ALU.add).then_inc(stats_step, 1)
            dve.wait_ge(stats_step, 3)
            dve.tensor_scalar(mv[:, :, 0], st[:, 1, :], 0.5, None, ALU.mult).then_inc(stats_step, 1)
            dve.scalar_tensor_tensor(st[:, 0, :], st[:, 0, :], 0.25, st[:, 0, :], ALU.mult, ALU.mult
                                     ).then_inc(stats_step, 1)
            dve.wait_ge(stats_step, 5)
            dve.scalar_tensor_tensor(mv[:, :, 1], st[:, 2, :], 1.0 / D, st[:, 0, :], ALU.mult, ALU.add
                                     ).then_inc(stats_step, 1)

        def finish_rstd(pool, stats_step, eps_added):
            pool.wait_ge(stats_step, 6)
            pool.tensor_scalar(veps[:], mv[:, :, 1], LN_EPS, 1.0, ALU.add, ALU.mult).then_inc(eps_added, 1)
            pool.wait_ge(eps_added, 1)
            pool.tensor_tensor(rstd[:], veps[:], neg_half[:], ALU.pow)

        x_dram = x.rearrange("b t d -> t b d")
        out_dram = out.rearrange("b t d -> t b d")

        with ExitStack() as su:
            y_sb = sb("y_sb", [S2, B, DC], stack=su)
            yT = sb("yT", [DC, B, S2], stack=su)
            yrep = sb("yrep", [DC, B, 2, P], stack=su)
            w1_sb = sb("w1_sb", [P, E, 4, P], stack=su)
            wk01 = sb("wk01", [DC, 2, D], stack=su)
            wv01 = sb("wv01", [DC, 2, D], stack=su)
            w2_sb = sb("w2_sb", [P, E, I], stack=su)
            wq1_sb = sb("wq1_sb", [P, D], stack=su)
            wkv_sb = sb("wkv_sb", [P, 2, DC], stack=su)
            ffn_sb = sb("ffn_sb", [P, 3, D], stack=su)
            router_sb = sb("router_sb", [E, D], stack=su)
            wo_sb = sb("wo_sb", [P, D], stack=su)
            bk_col = sb("bk_col", [P, 1], stack=su)
            bv_col = sb("bv_col", [P, 1], stack=su)
            bv_bc = sb("bv_bc", [P, P], stack=su)
            ones_pp = sb("ones_pp", [P, P], stack=su)
            bo_row = sb("bo_row", [1, D], stack=su)
            bo_tg = sb("bo_tg", [1, D], stack=su)
            ones_row = sb("ones_row", [1, P], stack=su)
            g_sb = sb("g_sb", [P, 4], stack=su)
            mask_u8 = sb("mask_u8", [B, P], U8, stack=su)
            mask_f = sb("mask_f", [B, P], stack=su)

            y_loaded = sem("y_loaded", su)
            small_loaded = sem("small_loaded", su)
            w_loaded = [sem(f"w_loaded{i}", su) for i in range(E // 2)]
            zeroed = sem("zeroed", su)
            ident_ready = sem("ident_ready", su)
            masks_step = sem("masks_step", su)
            yT_done = sem("yT_done", su)
            yT_copied = sem("yT_copied", su)
            yrep_ready = sem("yrep_ready", su)
            small_T = sem("small_T", su)
            small_copied = sem("small_copied", su)
            tg_ready = sem("tg_ready", su)
            scaled = sem("scaled", su)
            mask_float = sem("mask_float", su)
            k_done = sem("k_done", su)
            k_copied = sem("k_copied", su)
            v_done = sem("v_done", su)
            v_copied_act = sem("v_copied_act", su)
            v_copied_dve = sem("v_copied_dve", su)
            wT_done = sem("wT_done", su)
            wT_high = sem("wT_high", su)
            wT_low = sem("wT_low", su)
            stats = sem("stats", su)
            stats_step = sem("stats_step", su)
            eps_added = sem("eps_added", su)
            bias_done = sem("bias_done", su)

            SMALL = 19
            YG = [range(0, 6), range(6, 12), range(12, B)]

            with nc.Block() as block:
                @block.sync
                def _(sp):
                    sp.dma_start(y_sb[:], ctx_768.rearrange("b k c -> k b c")).then_inc(y_loaded, 16)
                    for dst, src in (
                        (wk01[:, 0, :], wk0), (wv01[:, 0, :], wv0), (wq0_sb[:], wq0), (wo_sb[:], wo0),
                        (wq1_sb[:], wq1), (wkv_sb[:], wkv1.rearrange("(l o) c -> o l c", l=2)),
                        (ffn_sb[:, 0, :], w_r), (ffn_sb[:, 1, :], w_k), (ffn_sb[:, 2, :], w_v),
                        (router_sb[:], router_w), (mask_u8[:], mask_BxS_bk0),
                        (bq_col[:], bq0.rearrange("(d o) -> d o", o=1)),
                        (bk_col[:], bk0.rearrange("(d o) -> d o", o=1)),
                        (bv_col[:], bv0.rearrange("(d o) -> d o", o=1)),
                        (bo_row[:], bo0.rearrange("(o d) -> o d", o=1)),
                        (mus[:, 0:1], mu_r.rearrange("(d o) -> d o", o=1)),
                        (mus[:, 1:2], mu_k.rearrange("(d o) -> d o", o=1)),
                        (g_sb[:, 0:2], g_xattn.partition_broadcast(P)), (g_sb[:, 2:4], g_ffn.partition_broadcast(P)),
                    ):
                        sp.dma_start(dst, src).then_inc(small_loaded, 16)
                    for q in range(NQ):
                        sp.dma_start(xs[:, 4 * q:4 * q + 4, :], x_dram[:, 4 * q:4 * q + 4, :]).then_inc(x_loaded[q], 16)
                    for pair in range(E // 2):
                        es = slice(2 * pair, 2 * pair + 2)
                        sp.dma_start(w1_sb[:, es], w1[es].rearrange("e (k o) i -> o e k i", o=P)
                                     ).then_inc(w_loaded[pair], 16)
                        sp.dma_start(w2_sb[:, es], w2[es].rearrange("e h i -> h e i")).then_inc(w_loaded[pair], 16)

                @block.gpsimd
                def _(pool):
                    pool.memset(ident[:], 0.0).then_inc(zeroed, 1)
                    pool.memset(head_mask[:], 1.0).then_inc(zeroed, 1)
                    pool.memset(main_mask[:], 1.0).then_inc(zeroed, 1)
                    pool.memset(rest_mask[:], 1.0).then_inc(zeroed, 1)
                    pool.memset(yrep[:], 0.0).then_inc(zeroed, 1)
                    pool.memset(ones_pp[:], 1.0).then_inc(zeroed, 1)
                    pool.memset(ones_row[:], 1.0).then_inc(zeroed, 1)
                    pool.memset(neg_half[:], -0.5).then_inc(zeroed, 1)
                    pool.wait_ge(zeroed, 8)
                    pool.affine_select(out=ident[:], in_=ident[:], compare_op=ALU.not_equal, fill=1.0, base=0,
                                       pattern=[[-1, P]], channel_multiplier=1).then_inc(ident_ready, 1)
                    n = 0
                    for mask, step, pat in ((head_mask, DH, [[-DH, H]]), (main_mask, P // 2, [[-P // 2, 2], [0, DH]]),
                                            (rest_mask, KR, [[-KR, 8]])):
                        pool.affine_select(out=mask[:], in_=mask[:], compare_op=ALU.is_ge, fill=0.0, base=0,
                                           pattern=pat, channel_multiplier=1).then_inc(masks_step, 1)
                        n += 1
                        pool.wait_ge(masks_step, n)
                        pool.affine_select(out=mask[:], in_=mask[:], compare_op=ALU.is_ge, fill=0.0, base=step - 1,
                                           pattern=[[-s, c] for s, c in pat], channel_multiplier=-1
                                           ).then_inc(masks_step, 1)
                        n += 1
                    finish_rstd(pool, stats_step, eps_added)

                @block.tensor
                def _(pe):
                    pe.wait_ge(ident_ready, 1)
                    pe.wait_ge(y_loaded, 16)
                    for n, group in enumerate(YG):
                        for i, b in enumerate(group):
                            mm = pe.transpose(pbank(n)[0:DC, i * S2:(i + 1) * S2], y_sb[:, b, :], ident[0:S2, 0:S2])
                        mm.then_inc(yT_done, 1)
                    pe.wait_ge(small_loaded, 16 * SMALL)
                    pe.wait_ge(mask_float, 1)
                    pe.transpose(pbank(3)[:, 0:128], wq1_sb[:], ident[:])
                    for i in range(2):
                        pe.transpose(pbank(3)[0:DC, 128 + 128 * i:256 + 128 * i], wkv_sb[:, i, :], ident[:])
                    pe.transpose(pbank(3)[:, 384:384 + B], mask_f[:], ident[0:B, 0:B])
                    pe.transpose(pbank(3)[:, 400:400 + E], router_sb[:], ident[0:E, 0:E]).then_inc(small_T, 1)
                    for i in range(3):
                        mm = pe.transpose(pbank(4)[:, 128 * i:128 * i + 128], ffn_sb[:, i, :], ident[:])
                    mm.then_inc(small_T, 1)
                    pe.wait_ge(yT_copied, 3)
                    pe.wait_ge(small_copied, 2)
                    n = 0
                    for layer in range(2):
                        for group in YG:
                            if n >= 3:
                                pe.wait_ge(k_copied, n - 2)
                            w = len(group) * S2
                            pe.matmul(pbank(5 + n % 3)[:, 0:w], wk01[:, layer, :],
                                      yT[:, group[0]:group[-1] + 1, :], start=True, stop=True).then_inc(k_done, 1)
                            n += 1
                    pe.wait_ge(yrep_ready, 2)
                    for b in range(B):
                        if b >= 2:
                            pe.wait_ge(v_copied_dve if b % 2 else v_copied_act, b // 2)
                        for part in range(2):
                            mm = pe.matmul(pbank(b % 2)[:, 256 * part:256 * part + 256], yrep[:, b, part, :],
                                           wv01[:], start=True, stop=True)
                        mm.then_inc(v_done, 1)
                    pe.wait_ge(scaled, 3)
                    pe.matmul(pbank(2)[:, 0:D], bv_bc[:], wo_tg[:], start=True, stop=False)
                    pe.matmul(pbank(2)[:, 0:D], ones_row[:], bo_tg[:], start=False, stop=True).then_inc(bias_done, 1)
                    n = 0
                    for pair in range(E // 2):
                        pe.wait_ge(w_loaded[pair], 32)
                        for g in range(3):
                            if n >= 2:
                                pe.wait_ge(wT_low, n - 1)
                            else:
                                pe.wait_ge(small_copied, 4)
                            for i in range(4):
                                src = (w1_sb[:, 2 * pair + g, i, :] if g < 2 else
                                       w2_sb[:, 2 * pair + i // 2, P * (i % 2):P * (i % 2) + P])
                                mm = pe.transpose(pbank(3 + n % 2)[:, P * i:P * i + P], src, ident[:])
                            mm.then_inc(wT_done, 1)
                            n += 1

                @block.scalar
                def _(act):
                    act.wait_ge(small_loaded, 16 * SMALL)
                    act.activation(tg[:], g_sb[:], ACT.Tanh).then_inc(tg_ready, 1)
                    for n, group in enumerate(YG):
                        act.wait_ge(yT_done, n + 1)
                        act.copy(yT[:, group[0]:group[-1] + 1, :],
                                 pbank(n)[0:DC, 0:len(group) * S2]).then_inc(yT_copied, 1)
                    act.wait_ge(small_T, 1)
                    act.copy(wk01[:, 1, :], pbank(3)[0:DC, 128:256]).then_inc(small_copied, 1)
                    act.copy(wv01[:, 1, :], pbank(3)[0:DC, 256:384]).then_inc(small_copied, 1)
                    act.copy(wq1T[:], pbank(3)[:, 0:128]).then_inc(small_copied, 1)
                    act.copy(valid[:], pbank(3)[:, 384:384 + B])
                    act.copy(routerT[:], pbank(3)[:, 400:400 + E])
                    act.wait_ge(small_T, 2)
                    act.copy(w_rT[:], pbank(4)[:, 0:128])
                    act.copy(w_kT[:], pbank(4)[:, 128:256])
                    act.copy(w_vT[:], pbank(4)[:, 256:384]).then_inc(small_copied, 1)
                    n = 0
                    for layer in range(2):
                        for group in YG:
                            act.wait_ge(k_done, n + 1)
                            act.activation(kT[:, layer, group[0]:group[-1] + 1, :],
                                           pbank(5 + n % 3)[:, 0:len(group) * S2], ACT.Identity,
                                           bias=bk_col[:] if layer == 0 else 0.0).then_inc(k_copied, 1)
                            n += 1
                    for b in range(0, B, 2):
                        act.wait_ge(v_done, b + 1)
                        act.copy(vc[:, b].rearrange("p a l d -> p (a l d)"), pbank(0)).then_inc(v_copied_act, 1)
                    act.wait_ge(bias_done, 1)
                    act.copy(bias_bc[:], pbank(2)[:, 0:D])
                    for n in range(3 * E // 2):
                        pair, g = n // 3, n % 3
                        act.wait_ge(wT_done, n + 1)
                        act.copy(w1h[:, 2 * pair + g, :] if g < 2 else
                                 w2h[:, 2 * pair:2 * pair + 2].rearrange("p e k d -> p (e k d)"),
                                 pbank(3 + n % 2)).then_inc(wT_high, 1)

                @block.vector
                def _(dve):
                    dve.wait_ge(small_loaded, 16 * SMALL)
                    dve.tensor_copy(mask_f[:], mask_u8[:]).then_inc(mask_float, 1)
                    dve.tensor_scalar(mus[:, 2:4], mus[:, 0:2], -1.0, 1.0, ALU.mult, ALU.add)
                    dve.wait_ge(tg_ready, 1)
                    dve.wait_ge(zeroed, 8)
                    dve.tensor_scalar(wo_tg[:], wo_sb[:], tg[:, 0:1], None, ALU.mult).then_inc(scaled, 1)
                    dve.tensor_scalar(bo_tg[:], bo_row[:], tg[0:1, 0:1], None, ALU.mult).then_inc(scaled, 1)
                    dve.tensor_scalar(bv_bc[:], ones_pp[:], bv_col[:, 0:1], None, ALU.mult).then_inc(scaled, 1)
                    dve.wait_ge(yT_copied, 3)
                    dve.tensor_copy(yrep[:, :, 0, :].rearrange("c b (r k) -> c b r k", r=2),
                                    yT[:, :, 0:KM].unsqueeze(2).to_broadcast([DC, B, 2, KM])).then_inc(yrep_ready, 1)
                    dve.tensor_copy(yrep[:, :, 1, :].rearrange("c b (r k) -> c b r k", r=8)[:, :, :, 0:NR],
                                    yT[:, :, KM:S2].unsqueeze(2).to_broadcast([DC, B, 8, NR])).then_inc(yrep_ready, 1)
                    for b in range(B):
                        if b % 4 == 0:
                            dve.wait_ge(x_loaded[b // 4], 16)
                        if b % 2:
                            dve.wait_ge(v_done, b + 1)
                            dve.tensor_copy(vc[:, b].rearrange("p a l d -> p (a l d)"),
                                            pbank(1)).then_inc(v_copied_dve, 1)
                        dve.bn_stats(bns[:, b].rearrange("p a s -> p (a s)"), xs[:, b, :]).then_inc(stats, 1)
                    dve.wait_ge(stats, B)
                    finish_stats(dve, stats_step)
                    for n in range(3 * E // 2):
                        pair, g = n // 3, n % 3
                        dve.wait_ge(wT_high, n + 1)
                        hi, lo = ((w1h[:, 2 * pair + g, :], w1l[:, 2 * pair + g, :]) if g < 2 else
                                  [w[:, 2 * pair:2 * pair + 2].rearrange("p e k d -> p (e k d)") for w in (w2h, w2l)])
                        dve.tensor_tensor(lo, pbank(3 + n % 2), hi.bitcast(F32), ALU.subtract).then_inc(wT_low, 1)

        def attention(layer):
            with ExitStack() as at:
                kbd = sb(f"kbd{layer}", [P, 2, COLS], stack=at)
                vbd = sb(f"vbd{layer}", [P, 2, COLS + P], stack=at)
                pr = sb(f"pr{layer}", [P, 2, COLS], stack=at)
                pT = sb(f"pT{layer}", [P, COLS], stack=at)
                xn = sb(f"xn{layer}", [P, 2, D], stack=at)
                xnT = sb(f"xnT{layer}", [P, 2, D], stack=at)
                qT = sb(f"qT{layer}", [P, 2, D], stack=at)
                oT = sb(f"oT{layer}", [P, 2, P], stack=at)
                rT = sb(f"rT{layer}", [P, 2, P], stack=at)
                mxm = sb(f"mxm{layer}", [P, 2, H], stack=at)
                mxr = sb(f"mxr{layer}", [P, 2, H], stack=at)
                mx = sb(f"mx{layer}", [P, 2, H], stack=at)
                smm = sb(f"smm{layer}", [P, 2, H], stack=at)
                smr = sb(f"smr{layer}", [P, 2, H], stack=at)
                sm = sb(f"sm{layer}", [P, 2, H], stack=at)
                rc = sb(f"rc{layer}", [P, 2, H], stack=at)
                rx = sb(f"rx{layer}", [P, 2, P], stack=at)
                tmp = sb(f"tmp{layer}", [P, 2, P], stack=at)

                def s_(name):
                    return sem(f"{name}{layer}", at)

                cleared = s_("cleared")
                xn_ready = s_("xn_ready")
                bias_added = s_("bias_added")
                xnT_done = s_("xnT_done")
                xnT_ready = s_("xnT_ready")
                q_done = s_("q_done")
                q_ready = s_("q_ready")
                kbd_ready = s_("kbd_ready")
                vbd_ready = s_("vbd_ready")
                scored = s_("scored")
                part_max = s_("part_max")
                max_ready = s_("max_ready")
                shifted = s_("shifted")
                exp_done = s_("exp_done")
                part_sum = s_("part_sum")
                sum_ready = s_("sum_ready")
                recip_ready = s_("recip_ready")
                rx_ready = s_("rx_ready")
                rT_done = s_("rT_done")
                rT_ready = s_("rT_ready")
                pT_done = s_("pT_done")
                pT_ready = s_("pT_ready")
                pv_done = s_("pv_done")
                oT_ready = s_("oT_ready")
                out_done = s_("out_done")
                scaled_out = s_("scaled_out")
                res_done = s_("res_done")
                stats = s_("stats")
                stats_step = s_("stats_step")
                eps_added = s_("eps_added")

                tile_xs = xs[:].rearrange("p (g u) d -> p g u d", u=2)
                tile_mv = mv[:].rearrange("p (g u) s -> p g u s", u=2)
                tile_bns = bns[:].rearrange("p (g u) a s -> p g u (a s)", u=2)
                tile_rstd = rstd[:].rearrange("p (g u) -> p g u", u=2)
                tile_valid = valid[:].rearrange("p (g u) -> p g u", u=2)
                tile_kT = kT[:, layer].rearrange("p (g u) k -> p g u k", u=2)
                tile_vc = vc[:].rearrange("p (g u) a l d -> p g u a l d", u=2)

                xn_ps = bank[0][:, 0:P]
                rT_ps = bank[0][:, P:2 * P]
                q_ps = bank[0][:, 2 * P:3 * P]
                o_ps = bank[1][:, 0:P]
                out_ps = bank[4][:, 3 * P:4 * P]
                GROUPS = [(0, 4), (4, 8), (8, CH)]
                sc_main = scores_ps[:, 0:MAIN].rearrange("p (h k) -> p h k", h=H)
                sc_rest = scores_ps[:, MAIN:COLS].rearrange("p (h k) -> p h k", h=H)[:, :, 0:NR]

                def slots(eng, body):
                    for t in range(2):
                        body(0, t, t, True, False)
                    with eng.Fori(1, B // 2) as g:
                        for u in range(2):
                            body(g, u, 2 * g + u, True, True)
                    for t in range(2):
                        body(B // 2, t, B + t, False, True)

                with nc.Block() as block:
                    @block.gpsimd
                    def _(pool):
                        for u in range(2):
                            pool.memset(vbd[:, u, :], 0.0).then_inc(cleared, 1)
                            pool.memset(kbd[:, u, :], 0.0).then_inc(cleared, 1)
                            pool.memset(pr[:, u, :], 0.0).then_inc(cleared, 1)
                        pool.wait_ge(cleared, 6)

                        def body(g, u, t, front, back):
                            if front:
                                if back:
                                    pool.wait_ge(scored, t - 1)
                                src = tile_kT[:, g, u, :]
                                pool.tensor_tensor(
                                    kbd[:, u, 0:MAIN].rearrange("p (h k) -> p h k", h=H),
                                    src[:, 0:KM].unsqueeze(1).to_broadcast([P, H, KM]),
                                    head_mask[:].unsqueeze(2).to_broadcast([P, H, KM]), ALU.mult).then_inc(kbd_ready, 1)
                                pool.tensor_tensor(
                                    kbd[:, u, MAIN:COLS].rearrange("p (h k) -> p h k", h=H)[:, :, 0:NR],
                                    src[:, KM:S2].unsqueeze(1).to_broadcast([P, H, NR]),
                                    head_mask[:].unsqueeze(2).to_broadcast([P, H, NR]), ALU.mult).then_inc(kbd_ready, 1)
                                if back:
                                    pool.wait_ge(pv_done, t - 1)
                                v = tile_vc[:, g, u, :, layer, :]
                                pool.tensor_tensor(
                                    vbd[:, u, 0:CM * (P + 2 * DH)].rearrange("p (c w) -> p c w", c=CM)[:, :, 0:2 * DH],
                                    v[:, 0, :].rearrange("p (c r) -> p c r", c=CM),
                                    main_mask[:].unsqueeze(1).to_broadcast([P, CM, 2 * DH]), ALU.mult
                                ).then_inc(vbd_ready, 1)
                                pool.tensor_tensor(
                                    vbd[:, u, MAIN:MAIN + 2 * (P + 8 * DH)].rearrange("p (c w) -> p c w", c=2)[
                                        :, :, 0:8 * DH].rearrange("p c (h d) -> p c h d", h=8),
                                    v[:, 1, :].rearrange("p (c h d) -> p c h d", c=2, h=8),
                                    rest_mask[:].unsqueeze(1).unsqueeze(3).to_broadcast([P, 2, 8, DH]), ALU.mult
                                ).then_inc(vbd_ready, 1)
                                if layer == 0:
                                    pool.wait_ge(xn_ready, t + 1)
                                    pool.tensor_tensor(tile_xs[:, g, u, :], tile_xs[:, g, u, :], bias_bc[:],
                                                       ALU.add).then_inc(bias_added, 1)
                            if back and layer == 1:
                                pool.wait_ge(scaled_out, t - 1)
                                xt = tile_xs[:, g - 1, u, :]
                                pool.tensor_tensor(xt, xt, tmp[:, u, :], ALU.add).then_inc(res_done, 1)

                        slots(pool, body)
                        finish_rstd(pool, stats_step, eps_added)

                    @block.tensor
                    def _(pe):
                        def body(g, u, t, front, back):
                            if front:
                                pe.wait_ge(xn_ready, t + 1)
                                if not (isinstance(t, int) and t == 0):
                                    pe.wait_ge(q_ready, t)
                                pe.transpose(xn_ps, xn[:, u, :], ident[:]).then_inc(xnT_done, 1)
                            if back:
                                if layer == 0:
                                    pe.wait_ge(rx_ready, t - 1)
                                    pe.transpose(rT_ps, rx[:, u, :], ident[:]).then_inc(rT_done, 1)
                                pe.wait_ge(exp_done, 2 * (t - 1))
                                for n, (c0, c1) in enumerate(GROUPS):
                                    if n == 2 and not (isinstance(t, int) and t == 2):
                                        pe.wait_ge(bank4_read, t - 2)
                                    for c in range(c0, c1):
                                        mm = pe.transpose(bank[2 + n][:, P * (c - c0):P * (c - c0) + P],
                                                          pr[:, u, P * c:P * c + P], ident[:])
                                    mm.then_inc(pT_done, 1)
                            if front:
                                pe.wait_ge(xnT_ready, t + 1)
                                if back and layer == 0:
                                    pe.wait_ge(rT_ready, t - 1)
                                pe.matmul(q_ps, wq0_sb[:] if layer == 0 else wq1T[:], xnT[:, u, :],
                                          start=True, stop=True).then_inc(q_done, 1)
                            if back:
                                pe.wait_ge(vbd_ready, 2 * (t - 1))
                                if not (isinstance(t, int) and t == 2):
                                    pe.wait_ge(oT_ready, t - 2)
                                for n, (c0, c1) in enumerate(GROUPS):
                                    pe.wait_ge(pT_ready, 3 * (t - 2) + n + 1)
                                    for c in range(c0, c1):
                                        mm = pe.matmul(o_ps, vbd[:, u, P * c:P * c + P], pT[:, P * c:P * c + P],
                                                       start=(c == 0), stop=(c == CH - 1))
                                mm.then_inc(pv_done, 1)
                            if front:
                                pe.wait_ge(q_ready, t + 1)
                                pe.wait_ge(kbd_ready, 2 * (t + 1))
                                if not (isinstance(t, int) and t == 0):
                                    pe.wait_ge(shifted, 2 * t)
                                for c0 in range(0, COLS, 512):
                                    c1 = min(c0 + 512, COLS)
                                    mm = pe.matmul(scores_ps[:, c0:c1], qT[:, u, :], kbd[:, u, c0:c1],
                                                   start=True, stop=True)
                                mm.then_inc(scored, 1)
                            if back:
                                pe.wait_ge(oT_ready, t - 1)
                                pe.wait_ge(pT_ready, 3 * (t - 1))
                                if layer == 0:
                                    pe.matmul(out_ps, oT[:, u, :], wo_tg[:], start=True, stop=True
                                              ).then_inc(out_done, 1)
                                else:
                                    pe.transpose(out_ps, oT[:, u, :], ident[:]).then_inc(out_done, 1)

                        bank4_read = res_done if layer == 0 else scaled_out
                        slots(pe, body)

                    @block.scalar
                    def _(act):
                        def body(g, u, t, front, back):
                            if front:
                                act.wait_ge(xnT_done, t + 1)
                                if back and layer == 0:
                                    act.wait_ge(rT_done, t - 1)
                                act.copy(xnT[:, u, :], xn_ps).then_inc(xnT_ready, 1)
                            if back:
                                if layer == 0:
                                    if not front:
                                        act.wait_ge(rT_done, t - 1)
                                    act.copy(rT[:, u, :], rT_ps).then_inc(rT_ready, 1)
                                if not (isinstance(t, int) and t == 2):
                                    act.wait_ge(pv_done, t - 2)
                                for n, (c0, c1) in enumerate(GROUPS):
                                    act.wait_ge(pT_done, 3 * (t - 2) + n + 1)
                                    act.copy(pT[:, P * c0:P * c1], bank[2 + n][:, 0:P * (c1 - c0)]).then_inc(pT_ready, 1)
                            if front:
                                act.wait_ge(q_done, t + 1)
                                act.activation(qT[:, u, :], q_ps, ACT.Identity,
                                               bias=bq_col[:] if layer == 0 else 0.0).then_inc(q_ready, 1)
                            if back and layer == 1:
                                act.wait_ge(pv_done, t - 1)
                                act.copy(oT[:, u, :], o_ps).then_inc(oT_ready, 1)
                            if not (isinstance(t, int) and t in (0, B + 1)):
                                v = 1 - u
                                main = pr[:, v, 0:MAIN]
                                rest = pr[:, v, MAIN:COLS].rearrange("p (h k) -> p h k", h=H)[:, :, 0:NR]
                                act.wait_ge(shifted, 2 * t - 1)
                                act.activation(main, main, ACT.Exp, scale=SCALE).then_inc(exp_done, 1)
                                act.wait_ge(shifted, 2 * t)
                                act.activation(rest, rest, ACT.Exp, scale=SCALE).then_inc(exp_done, 1)

                        slots(act, body)

                    @block.vector
                    def _(dve):
                        def body(g, u, t, front, back):
                            v = 1 - u
                            if front:
                                if back:
                                    dve.wait_ge(xnT_done, t - 1)
                                dve.tensor_scalar(xn[:, u, :], tile_xs[:, g, u, :], tile_mv[:, g, u, 0:1],
                                                  tile_rstd[:, g, u:u + 1], ALU.subtract, ALU.mult
                                                  ).then_inc(xn_ready if layer == 0 else xn_plain, 1)
                                if layer == 1:
                                    dve.wait_ge(xn_plain, t + 1)
                                    dve.tensor_scalar(xn[:, u, :], xn[:, u, :], tile_valid[:, g, u:u + 1], None,
                                                      ALU.mult).then_inc(xn_ready, 1)
                            middle = not (isinstance(t, int) and t in (0, B + 1))
                            main = pr[:, v, 0:MAIN].rearrange("p (h k) -> p h k", h=H)
                            rest = pr[:, v, MAIN:COLS].rearrange("p (h k) -> p h k", h=H)[:, :, 0:NR]
                            if middle:
                                dve.wait_ge(scored, t)
                                dve.tensor_reduce(mxm[:, v, :], sc_main, AX.X, ALU.max).then_inc(part_max, 1)
                                dve.tensor_reduce(mxr[:, v, :], sc_rest, AX.X, ALU.max).then_inc(part_max, 1)
                                dve.wait_ge(part_max, 2 * t)
                                dve.tensor_tensor(mx[:, v, :], mxm[:, v, :], mxr[:, v, :], ALU.max
                                                  ).then_inc(max_ready, 1)
                                dve.wait_ge(max_ready, t)
                                if isinstance(t, int) and t in (1, 2):
                                    dve.wait_ge(cleared, 6)
                                if not (isinstance(t, int) and t < 3):
                                    dve.wait_ge(pT_done, 3 * (t - 2))
                                dve.tensor_tensor(main, sc_main, mx[:, v, :].unsqueeze(2).to_broadcast([P, H, KM]),
                                                  ALU.subtract).then_inc(shifted, 1)
                                dve.tensor_tensor(rest, sc_rest, mx[:, v, :].unsqueeze(2).to_broadcast([P, H, NR]),
                                                  ALU.subtract).then_inc(shifted, 1)
                            if back and layer == 0:
                                dve.wait_ge(pv_done, t - 1)
                                dve.wait_ge(rT_ready, t - 1)
                                dve.tensor_tensor(oT[:, u, :], o_ps, rT[:, u, :], ALU.mult).then_inc(oT_ready, 1)
                            if middle:
                                dve.wait_ge(exp_done, 2 * t)
                                dve.tensor_reduce(smm[:, v, :], main, AX.X, ALU.add).then_inc(part_sum, 1)
                                dve.tensor_reduce(smr[:, v, :], rest, AX.X, ALU.add).then_inc(part_sum, 1)
                                dve.wait_ge(part_sum, 2 * t)
                                dve.tensor_tensor(sm[:, v, :], smm[:, v, :], smr[:, v, :], ALU.add).then_inc(sum_ready, 1)
                                dve.wait_ge(sum_ready, t)
                                dve.reciprocal(rc[:, v, :], sm[:, v, :]).then_inc(recip_ready, 1)
                                dve.wait_ge(recip_ready, t)
                                if layer == 0:
                                    if not (isinstance(t, int) and t < 3):
                                        dve.wait_ge(rT_done, t - 2)
                                    scale = 1.0
                                else:
                                    scale = tg[:, 1:2]
                                dve.tensor_scalar(rx[:, v, :].rearrange("p (h d) -> p h d", h=H),
                                                  rc[:, v, :].unsqueeze(2).to_broadcast([P, H, DH]), scale, None,
                                                  ALU.mult).then_inc(rx_ready, 1)
                            if back:
                                xt = tile_xs[:, g - 1, u, :]
                                dve.wait_ge(out_done, t - 1)
                                if layer == 0:
                                    dve.wait_ge(bias_added, t - 1)
                                    dve.tensor_tensor(xt, xt, out_ps, ALU.add).then_inc(res_done, 1)
                                else:
                                    dve.wait_ge(rx_ready, t - 1)
                                    dve.tensor_tensor(tmp[:, u, :], out_ps, rx[:, u, :], ALU.mult
                                                      ).then_inc(scaled_out, 1)
                                dve.wait_ge(res_done, t - 1)
                                dve.wait_ge(pT_ready, 3)
                                dve.bn_stats(tile_bns[:, g - 1, u, :], xt).then_inc(stats, 1)

                        xn_plain = s_("xn_plain")
                        slots(dve, body)
                        dve.wait_ge(stats, B)
                        finish_stats(dve, stats_step)

        attention(0)

        with ExitStack() as mo:
            xn = sb("xn_m", [P, 4, D], stack=mo)
            xTf = sb("xTf", [P, 512], stack=mo)
            xTh = sb("xTh", [P, NQ, 512], F32R, stack=mo)
            xTl = sb("xTl", [P, NQ, 512], F32R, stack=mo)
            tri = sb("tri", [P, E, E], stack=mo)
            lg = sb("lg", [P, B, E], stack=mo)
            lm = sb("lm", [P, B], stack=mo)
            ex = sb("ex", [P, B, E], stack=mo)
            es = sb("es", [P, B], stack=mo)
            er = sb("er", [P, B], stack=mo)
            gt = sb("gt", [P, B, E, E], stack=mo)
            ge = sb("ge", [P, B, E, E], stack=mo)
            rank = sb("rank", [P, B, E], stack=mo)
            comb = sb("comb", [P, B, E], stack=mo)
            comb2 = sb("comb2", [P, B, 2 * E], stack=mo)
            combT = sb("combT", [P, NQ, 512], F32R, stack=mo)
            self_ = sb("self_", [P, E, P], stack=mo)
            sel = sb("sel", [P, E, P], F32R, stack=mo)
            sg = sb("sg", [P, 2, 512], stack=mo)
            au = sb("au", [P, 2, 512], stack=mo)
            yv = sb("yv", [P, 2, 512], stack=mo)
            yh = sb("yh", [P, 2, 512], F32R, stack=mo)
            yl = sb("yl", [P, 2, 512], F32R, stack=mo)
            oT = sb("oT_m", [P, 512], stack=mo)

            xn_ready = sem("m_xn_ready", mo)
            xT_done = sem("m_xT_done", mo)
            xT_full = sem("m_xT_full", mo)
            xT_high = sem("m_xT_high", mo)
            xT_low = sem("m_xT_low", mo)
            routed = sem("m_routed", mo)
            const_set = sem("m_const_set", mo)
            const_ready = sem("m_const_ready", mo)
            sel_ready = sem("m_sel_ready", mo)
            route_step = sem("m_route_step", mo)
            exp_ready = sem("m_exp_ready", mo)
            comb_ready = sem("m_comb_ready", mo)
            combT_done = sem("m_combT_done", mo)
            combT_ready = sem("m_combT_ready", mo)
            h_done = sem("m_h_done", mo)
            silu_done = sem("m_silu_done", mo)
            up_done = sem("m_up_done", mo)
            weight_spread = sem("m_weight_spread", mo)
            y_done = sem("m_y_done", mo)
            y_high = sem("m_y_high", mo)
            y_low = sem("m_y_low", mo)
            down_done = sem("m_down_done", mo)
            oT_ready = sem("m_oT_ready", mo)
            o_done = sem("m_o_done", mo)
            res_done = sem("m_res_done", mo)
            stats = sem("m_stats", mo)
            stats_step = sem("m_stats_step", mo)
            eps_added = sem("m_eps_added", mo)

            UNITS = 2 * E
            mo_ps = pbank(6)
            lg_ps = pbank(7)

            def gate_ps(j):
                return pbank(2 * (j % 2))

            def up_ps(j):
                return pbank(2 * (j % 2) + 1)

            def cb_ps(j):
                return pbank(4 + j // 2 % 2)

            with nc.Block() as block:
                @block.gpsimd
                def _(pool):
                    pool.memset(tri[:], 1.0).then_inc(const_set, 1)
                    pool.memset(self_[:], 0.0).then_inc(const_set, 1)
                    pool.memset(combT[:].bitcast(F32), 0.0).then_inc(const_set, 1)
                    pool.wait_ge(const_set, 3)
                    pool.affine_select(out=tri[:], in_=tri[:], compare_op=ALU.is_gt, fill=0.0, base=0,
                                       pattern=[[1, E], [-1, E]], channel_multiplier=0).then_inc(const_ready, 1)
                    for n, base in enumerate((0, -E)):
                        pool.affine_select(out=self_[:], in_=self_[:], compare_op=ALU.not_equal, fill=1.0, base=base,
                                           pattern=[[-1, E], [0, P]], channel_multiplier=1).then_inc(const_ready, 1)
                        pool.wait_ge(const_ready, n + 2)
                    pool.tensor_copy(sel[:], self_[:]).then_inc(sel_ready, 1)

                @block.vector
                def _(dve):
                    for q in range(NQ):
                        for i in range(4):
                            b = 4 * q + i
                            if q:
                                dve.wait_ge(xT_done, q)
                            dve.tensor_scalar(xn[:, i, :], xs[:, b, :], mv[:, b, 0:1], rstd[:, b:b + 1],
                                              ALU.subtract, ALU.mult).then_inc(xn_ready, 1)
                        dve.wait_ge(xT_high, q + 1)
                        dve.tensor_tensor(xTl[:, q, :], pbank(q % 2), xTh[:, q, :].bitcast(F32),
                                          ALU.subtract).then_inc(xT_low, 1)
                    n = 0

                    def step(ins):
                        nonlocal n
                        n += 1
                        ins.then_inc(route_step, 1)
                        dve.wait_ge(route_step, n)

                    dve.wait_ge(routed, NQ)
                    step(dve.tensor_copy(lg[:], lg_ps[:, 0:B * E].rearrange("p (b e) -> p b e", e=E)))
                    step(dve.tensor_reduce(lm[:], lg[:], AX.X, ALU.max))
                    step(dve.tensor_tensor(ex[:], lg[:], lm[:].unsqueeze(2).to_broadcast([P, B, E]), ALU.subtract))
                    mine = lg[:].unsqueeze(3).to_broadcast([P, B, E, E])
                    other = lg[:].unsqueeze(2).to_broadcast([P, B, E, E])
                    dve.tensor_tensor(gt[:], other, mine, ALU.is_gt)
                    step(dve.tensor_tensor(ge[:], other, mine, ALU.is_equal))
                    dve.wait_ge(const_ready, 1)
                    step(dve.tensor_tensor(ge[:], ge[:], tri[:].unsqueeze(1).to_broadcast([P, B, E, E]), ALU.mult))
                    step(dve.tensor_tensor(gt[:], gt[:], ge[:], ALU.add))
                    step(dve.tensor_reduce(rank[:], gt[:], AX.X, ALU.add))
                    step(dve.tensor_scalar(rank[:], rank[:], 2.0, tg[:, 2:3], ALU.is_lt, ALU.mult))
                    dve.wait_ge(exp_ready, 1)
                    step(dve.tensor_reduce(es[:], ex[:], AX.X, ALU.add))
                    step(dve.reciprocal(er[:], es[:]))
                    step(dve.tensor_tensor(comb[:], ex[:], er[:].unsqueeze(2).to_broadcast([P, B, E]), ALU.mult))
                    step(dve.tensor_tensor(comb[:], comb[:], rank[:], ALU.mult))
                    step(dve.tensor_copy(comb2[:, :, 0:E].bitcast(F32R), comb[:]))
                    dve.tensor_tensor(comb2[:, :, E:2 * E], comb[:], comb2[:, :, 0:E], ALU.subtract
                                      ).then_inc(comb_ready, 1)

                @block.tensor
                def _(pe):
                    for q in range(NQ):
                        if q >= 2:
                            pe.wait_ge(xT_low, q - 1)
                        for i in range(4):
                            pe.wait_ge(xn_ready, 4 * q + i + 1)
                            mm = pe.transpose(pbank(q % 2)[:, P * i:P * i + P], xn[:, i, :], ident[:])
                        mm.then_inc(xT_done, 1)
                        pe.wait_ge(xT_full, q + 1)
                        for i in range(4):
                            b = 4 * q + i
                            mm = pe.matmul(lg_ps[:, E * b:E * b + E], xTf[:, P * i:P * i + P], routerT[:],
                                           start=True, stop=True)
                        mm.then_inc(routed, 1)
                    pe.wait_ge(comb_ready, 1)
                    for q in range(NQ):
                        for i in range(4):
                            mm = pe.transpose(pbank(q)[0:2 * E, P * i:P * i + P], comb2[:, 4 * q + i, :], ident[:])
                        mm.then_inc(combT_done, 1)

                @block.scalar
                def _(act):
                    for q in range(NQ):
                        act.wait_ge(xT_done, q + 1)
                        if q:
                            act.wait_ge(routed, q)
                        act.copy(xTf[:], pbank(q % 2)).then_inc(xT_full, 1)
                        act.copy(xTh[:, q, :], pbank(q % 2)).then_inc(xT_high, 1)
                    act.wait_ge(route_step, 3)
                    act.activation(ex[:], ex[:], ACT.Exp).then_inc(exp_ready, 1)
                    act.wait_ge(const_set, 3)
                    for q in range(NQ):
                        act.wait_ge(combT_done, q + 1)
                        act.copy(combT[0:2 * E, q, :], pbank(q)[0:2 * E, :]).then_inc(combT_ready, 1)

            with nc.Block() as block:
                @block.tensor
                def _(pe):
                    def inner(q, j, n):
                        e, half = j // 2, j % 2
                        if not (isinstance(n, int) and n < 2):
                            pe.wait_ge(up_done, n - 1)
                        for ps, off in ((gate_ps(j), half * P), (up_ps(j), I + half * P)):
                            wh, wl = w1h[:, e, off:off + P], w1l[:, e, off:off + P]
                            pe.matmul(ps, wl, xTh[:, q, :], start=True, stop=False)
                            pe.matmul(ps, wh, xTl[:, q, :], start=False, stop=False)
                            mm = pe.matmul(ps, wh, xTh[:, q, :], start=False, stop=True)
                        mm.then_inc(h_done, 1)

                    def spread(q, j, n):
                        if not (isinstance(n, int) and n < 4):
                            pe.wait_ge(y_done, n - 2)
                        pe.matmul(cb_ps(j), sel[:, j // 2, :], combT[:, q, :], start=True, stop=True
                                  ).then_inc(weight_spread, 1)

                    def outer(q, j, n):
                        e, half, u = j // 2, j % 2, j % 2
                        pe.wait_ge(y_high, n + 1)
                        pe.wait_ge(y_low, n + 3)
                        if j == 0 and not (isinstance(q, int) and q == 0):
                            pe.wait_ge(oT_ready, q)
                        pe.matmul(mo_ps, w2l[:, e, half, :], yh[:, u, :], start=(j == 0), stop=False)
                        pe.matmul(mo_ps, w2h[:, e, half, :], yl[:, u, :], start=False, stop=False)
                        pe.matmul(mo_ps, w2h[:, e, half, :], yh[:, u, :], start=False, stop=(j == UNITS - 1)
                                  ).then_inc(down_done, 1)

                    def group(q, last):
                        for j in range(2, UNITS + 2):
                            n = q * UNITS + j
                            if j < UNITS:
                                inner(q, j, n)
                            elif not last:
                                inner(q + 1, j - UNITS, n)
                            outer(q, j - 2, n - 2)
                            if j % 2 == 0 and j < UNITS:
                                spread(q, j, n)
                            elif j == UNITS and not last:
                                spread(q + 1, 0, n)

                    def back(q):
                        pe.wait_ge(oT_ready, q + 1)
                        pe.wait_ge(res_done, q)
                        for i in range(4):
                            mm = pe.transpose(lg_ps[:, P * i:P * i + P], oT[:, P * i:P * i + P], ident[:])
                        mm.then_inc(o_done, 1)

                    inner(0, 0, 0)
                    spread(0, 0, 0)
                    inner(0, 1, 1)
                    with pe.Fori(0, NQ - 1) as q:
                        group(q, False)
                        back(q)
                    group(NQ - 1, True)
                    back(NQ - 1)

                @block.scalar
                def _(act):
                    act.sem_inc(down_done, 2)
                    with act.Fori(0, NQ) as q:
                        for j in range(UNITS + 1):
                            n = q * UNITS + j
                            u = j % 2
                            if j < UNITS:
                                act.wait_ge(h_done, n + 1)
                                act.activation(sg[:, u, :], gate_ps(j), ACT.Silu).then_inc(silu_done, 1)
                            if j > 0:
                                act.wait_ge(down_done, n)
                                act.wait_ge(y_done, n)
                                act.copy(yh[:, 1 - u, :], yv[:, 1 - u, :]).then_inc(y_high, 1)
                        act.wait_ge(down_done, q * UNITS + UNITS + 2)
                        act.copy(oT[:], mo_ps).then_inc(oT_ready, 1)

                @block.gpsimd
                def _(pool):
                    pool.sem_inc(y_low, 2)
                    with pool.Fori(0, NQ) as q:
                        for j in range(UNITS):
                            n = q * UNITS + j
                            pool.wait_ge(y_high, n + 1)
                            pool.tensor_tensor(yl[:, j % 2, :], yv[:, j % 2, :], yh[:, j % 2, :].bitcast(F32),
                                               ALU.subtract).then_inc(y_low, 1)

                @block.vector
                def _(dve):
                    with dve.Fori(0, NQ) as q:
                        for j in range(UNITS):
                            n = q * UNITS + j
                            u = j % 2
                            dve.wait_ge(silu_done, n + 1)
                            dve.tensor_tensor(au[:, u, :], sg[:, u, :], up_ps(j), ALU.mult).then_inc(up_done, 1)
                            dve.wait_ge(up_done, n + 1)
                            dve.wait_ge(weight_spread, q * E + j // 2 + 1)
                            dve.wait_ge(y_low, n + 1)
                            dve.tensor_tensor(yv[:, u, :], au[:, u, :], cb_ps(j), ALU.mult).then_inc(y_done, 1)
                        xq = xs[:].rearrange("p (q i) d -> p q i d", i=4)[:, q]
                        bq = bns[:].rearrange("p (q i) a s -> p q i (a s)", i=4)[:, q]
                        dve.wait_ge(o_done, q + 1)
                        dve.tensor_tensor(xq, xq, lg_ps.rearrange("p (i d) -> p i d", i=4), ALU.add
                                          ).then_inc(res_done, 1)
                        dve.wait_ge(res_done, q + 1)
                        dve.wait_ge(silu_done, UNITS)
                        for i in range(4):
                            dve.bn_stats(bq[:, i, :], xq[:, i, :]).then_inc(stats, 1)
                    dve.wait_ge(stats, B)
                    finish_stats(dve, stats_step)

            with nc.Block() as block:
                @block.gpsimd
                def _(pool):
                    finish_rstd(pool, stats_step, eps_added)

        attention(1)

        with ExitStack() as ff:
            xn = sb("xn_f", [P, 2, 4, D], stack=ff)
            xT = sb("xT_f", [P, 2, 4, P + 1], stack=ff)
            pr = sb("prev_r", [P, 2, 512], stack=ff)
            pk = sb("prev_k", [P, 2, 512], stack=ff)
            xr = sb("xr", [P, 2, 512], stack=ff)
            xk = sb("xk", [P, 2, 512], stack=ff)
            rs = sb("rs", [P, 2, 512], stack=ff)
            kr = sb("kr", [P, 2, 512], stack=ff)
            kk = sb("kk", [P, 2, 512], stack=ff)
            ov = sb("ov", [P, 2, 512], stack=ff)

            cleared = sem("f_cleared", ff)
            xn_ready = sem("f_xn_ready", ff)
            xT_done = sem("f_xT_done", ff)
            xT_ready = sem("f_xT_ready", ff)
            prev_ready = sem("f_prev_ready", ff)
            mix_ready = sem("f_mix_ready", ff)
            rk_done = sem("f_rk_done", ff)
            r_ready = sem("f_r_ready", ff)
            relu_ready = sem("f_relu_ready", ff)
            kk_ready = sem("f_kk_ready", ff)
            v_done = sem("f_v_done", ff)
            ov_ready = sem("f_ov_ready", ff)
            o_done = sem("f_o_done", ff)
            res_done = sem("f_res_done", ff)

            with nc.Block() as block:
                @block.gpsimd
                def _(pool):
                    pool.memset(xT[:, :, :, 0:1], 0.0).then_inc(cleared, 1)

                @block.vector
                def _(dve):
                    def mix(n):
                        u = n % 2
                        if n >= 2:
                            dve.wait_ge(xT_done, n - 1)
                        for i in range(4):
                            b = 4 * n + i
                            dve.tensor_scalar(xn[:, u, i, :], xs[:, b, :], mv[:, b, 0:1], rstd[:, b:b + 1],
                                              ALU.subtract, ALU.mult).then_inc(xn_ready, 1)
                        cur, prev = xT[:, u, :, 1:P + 1], xT[:, u, :, 0:P]
                        dve.wait_ge(xT_ready, n + 1)
                        dve.wait_ge(cleared, 1)
                        for dst, col in ((pr, 2), (pk, 3)):
                            dve.tensor_scalar(dst[:, u, :].rearrange("p (i t) -> p i t", i=4), prev,
                                              mus[:, col:col + 1], None, ALU.mult).then_inc(prev_ready, 1)
                        dve.wait_ge(prev_ready, 2 * n + 2)
                        if n >= 2:
                            dve.wait_ge(rk_done, 2 * (n - 1))
                        for dst, add, col in ((xr, pr, 0), (xk, pk, 1)):
                            dve.scalar_tensor_tensor(dst[:, u, :].rearrange("p (i t) -> p i t", i=4), cur,
                                                     mus[:, col:col + 1],
                                                     add[:, u, :].rearrange("p (i t) -> p i t", i=4),
                                                     ALU.mult, ALU.add).then_inc(mix_ready, 1)

                    def square(n):
                        u = n % 2
                        dve.wait_ge(relu_ready, n + 1)
                        if n >= 2:
                            dve.wait_ge(v_done, n - 1)
                        dve.tensor_tensor(kk[:, u, :], kr[:, u, :], pbank(4 + u), ALU.mult).then_inc(kk_ready, 1)

                    def finish(n):
                        u = n % 2
                        dve.wait_ge(v_done, n + 1)
                        dve.wait_ge(r_ready, n + 1)
                        if n >= 2:
                            dve.wait_ge(o_done, n - 1)
                        dve.scalar_tensor_tensor(ov[:, u, :], pbank(6 + u), tg[:, 3:4], rs[:, u, :],
                                                 ALU.mult, ALU.mult).then_inc(ov_ready, 1)
                        dve.wait_ge(o_done, n + 1)
                        xq = xs[:, 4 * n:4 * n + 4, :]
                        dve.tensor_tensor(xq, xq, pbank(u).rearrange("p (i d) -> p i d", i=4), ALU.add
                                          ).then_inc(res_done, 1)

                    mix(0)
                    for n in range(NQ):
                        if n + 1 < NQ:
                            mix(n + 1)
                        square(n)
                        finish(n)

                @block.tensor
                def _(pe):
                    def first(n):
                        u = n % 2
                        if n >= 2:
                            pe.wait_ge(res_done, n - 1)
                        for i in range(4):
                            pe.wait_ge(xn_ready, 4 * n + i + 1)
                            mm = pe.transpose(pbank(u)[:, P * i:P * i + P], xn[:, u, i, :], ident[:])
                        mm.then_inc(xT_done, 1)
                        pe.wait_ge(mix_ready, 2 * n + 2)
                        if n >= 2:
                            pe.wait_ge(r_ready, n - 1)
                        pe.matmul(pbank(2 + u), w_rT[:], xr[:, u, :], start=True, stop=True).then_inc(rk_done, 1)
                        if n >= 2:
                            pe.wait_ge(kk_ready, n - 1)
                        pe.matmul(pbank(4 + u), w_kT[:], xk[:, u, :], start=True, stop=True).then_inc(rk_done, 1)

                    def second(n):
                        u = n % 2
                        pe.wait_ge(kk_ready, n + 1)
                        if n >= 2:
                            pe.wait_ge(ov_ready, n - 1)
                        pe.matmul(pbank(6 + u), w_vT[:], kk[:, u, :], start=True, stop=True).then_inc(v_done, 1)
                        pe.wait_ge(ov_ready, n + 1)
                        pe.wait_ge(xT_ready, n + 1)
                        for i in range(4):
                            mm = pe.transpose(pbank(u)[:, P * i:P * i + P], ov[:, u, P * i:P * i + P], ident[:])
                        mm.then_inc(o_done, 1)

                    first(0)
                    for n in range(NQ):
                        if n + 1 < NQ:
                            first(n + 1)
                        second(n)

                @block.scalar
                def _(act):
                    def gather(n):
                        u = n % 2
                        act.wait_ge(xT_done, n + 1)
                        if n >= 2:
                            act.wait_ge(mix_ready, 2 * (n - 1))
                        act.copy(xT[:, u, :, 1:P + 1], pbank(u).rearrange("p (i t) -> p i t", i=4)
                                 ).then_inc(xT_ready, 1)

                    gather(0)
                    for n in range(NQ):
                        u = n % 2
                        if n + 1 < NQ:
                            gather(n + 1)
                        act.wait_ge(rk_done, 2 * n + 2)
                        if n >= 2:
                            act.wait_ge(kk_ready, n - 1)
                            act.wait_ge(ov_ready, n - 1)
                        act.activation(kr[:, u, :], pbank(4 + u), ACT.Relu).then_inc(relu_ready, 1)
                        act.activation(rs[:, u, :], pbank(2 + u), ACT.Sigmoid).then_inc(r_ready, 1)

                @block.sync
                def _(sp):
                    for n in range(NQ):
                        sp.wait_ge(res_done, n + 1)
                        sp.dma_start(out_dram[:, 4 * n:4 * n + 4, :], xs[:, 4 * n:4 * n + 4, :]).then_inc(out_stored, 16)
                    sp.wait_ge(out_stored, 16 * NQ)


_INS = ['x', 'ctx_768', 'mask_BxS_bk0', 'g_xattn', 'g_ffn', 'L0_xattn_wq', 'L0_xattn_bq', 'L0_xattn_wk',
        'L0_xattn_bk', 'L0_xattn_wv', 'L0_xattn_bv', 'L0_xattn_wo', 'L0_xattn_bo', 'L0_ffn_w1', 'L0_ffn_w2',
        'L0_ffn_router_w', 'L1_xattn_Wq', 'L1_xattn_Wkv', 'L1_ffn_W_r', 'L1_ffn_W_k', 'L1_ffn_W_v', 'L1_ffn_mu_r',
        'L1_ffn_mu_k']


def kernel(**inputs):
    import numpy as _np
    import concourse.bacc as _bacc
    from concourse import mybir as _mybir
    from concourse.bass_utils import run_bass_kernel_spmd as _run

    nc = _bacc.Bacc("TRN2", target_bir_lowering=False, num_devices=1)
    arrays, args = {}, []
    for name in _INS:
        a = _np.ascontiguousarray(inputs[name])
        arrays[f"in_{name}_dram"] = a
        args.append(nc.dram_tensor(f"in_{name}_dram", a.shape, _mybir.dt.from_np(a.dtype), kind="ExternalInput").ap())
    shape = inputs["x"].shape
    out = nc.dram_tensor("out_dram", shape, _mybir.dt.float32, kind="ExternalOutput").ap()
    flamingo_kernel(nc, *args, out)
    r = _run(nc, [arrays], core_ids=[0])
    return r.results[0]["out_dram"]
```

```python
from contextlib import ExitStack

import concourse.bass as bass
from concourse import mybir

F32 = mybir.dt.float32
F32R = mybir.dt.float32r
U8 = mybir.dt.uint8
ALU = mybir.AluOpType
ACT = mybir.ActivationFunctionType
AX = mybir.AxisListType

P = 128
KM = 64
KR = 16
LN_EPS = 1e-5


def flamingo_kernel(nc, x, ctx_768, mask_BxS_bk0, g_xattn, g_ffn, wq0, bq0, wk0, bk0, wv0, bv0, wo0, bo0,
                    w1, w2, router_w, wq1, wkv1, w_r, w_k, w_v, mu_r, mu_k, out):
    B, S, D = x.shape
    _, S2, DC = ctx_768.shape
    E, I2, _ = w1.shape
    I = I2 // 2
    H = 16
    DH = D // H
    SCALE = float(DH) ** -0.5
    NR = S2 - KM
    MAIN, REST = H * KM, H * KR
    COLS = MAIN + REST
    CH = COLS // P
    CM = MAIN // P
    NQ = B // 4
    assert S == P and D == P and H * DH == P and 0 < NR <= KR and B % 4 == 0 and E == 8 and I == 2 * P

    with ExitStack() as ctx:
        def sb(name, shape, dt=F32, stack=ctx):
            return stack.enter_context(nc.sbuf_tensor(name, shape, dt))

        def sem(name, stack=ctx):
            return stack.enter_context(nc.semaphore(name))

        bank = [ctx.enter_context(nc.psum_tensor(f"bank{i}", [P, 512], F32)) for i in range(5)]
        scores_ps = ctx.enter_context(nc.psum_tensor("scores_ps", [P, 3 * 512], F32))

        def pbank(i):
            return bank[i][:, :] if i < 5 else scores_ps[:, (i - 5) * 512:(i - 4) * 512]

        xs = sb("xs", [P, B, D])
        mv = sb("mv", [P, B, 2])
        rstd = sb("rstd", [P, B])
        veps = sb("veps", [P, B])
        rstd_valid = sb("rstd_valid", [P, B])
        neg_half = sb("neg_half", [P, B])
        bns = sb("bns", [P, B, 2, 3])
        st = sb("st", [P, 3, B])
        ident = sb("ident", [P, P])
        tg = sb("tg", [P, 4])
        kT = sb("kT", [P, 2, B, S2])
        vc = sb("vc", [P, B, 2, 2, D])
        head_mask = sb("head_mask", [P, H])
        main_mask = sb("main_mask", [P, 2 * DH])
        rest_mask = sb("rest_mask", [P, 8])
        wq0_sb = sb("wq0_sb", [P, D])
        bq_col = sb("bq_col", [P, 1])
        wo_tg = sb("wo_tg", [P, D])
        bias_bc = sb("bias_bc", [P, D])
        wq1T = sb("wq1T", [P, D])
        valid = sb("valid", [P, B])
        w_rT = sb("w_rT", [P, D])
        w_kT = sb("w_kT", [P, D])
        w_vT = sb("w_vT", [P, D])
        mus = sb("mus", [P, 4])
        routerh = sb("routerh", [P, P], F32R)
        routerl = sb("routerl", [P, P], F32R)
        tri = sb("tri", [P, E, E])
        sel = sb("sel", [P, E, P], F32R)
        combT = sb("combT", [P, NQ, 512], F32R)
        w1h = sb("w1h", [P, E, I2], F32R)
        w1l = sb("w1l", [P, E, I2], F32R)
        w2h = sb("w2h", [P, E, 2, D], F32R)
        w2l = sb("w2l", [P, E, 2, D], F32R)

        x_loaded = [sem(f"x_loaded{q}") for q in range(NQ)]
        out_stored = sem("out_stored")

        def finish_stats(dve, stats_step):
            even, odd = bns[:, :, 0, :], bns[:, :, 1, :]
            dve.tensor_tensor(st[:, 0, :], even[:, :, 1], odd[:, :, 1], ALU.subtract).then_inc(stats_step, 1)
            dve.tensor_tensor(st[:, 1, :], even[:, :, 1], odd[:, :, 1], ALU.add).then_inc(stats_step, 1)
            dve.tensor_tensor(st[:, 2, :], even[:, :, 2], odd[:, :, 2], ALU.add).then_inc(stats_step, 1)
            dve.wait_ge(stats_step, 3)
            dve.tensor_scalar(mv[:, :, 0], st[:, 1, :], 0.5, None, ALU.mult).then_inc(stats_step, 1)
            dve.scalar_tensor_tensor(st[:, 0, :], st[:, 0, :], 0.25, st[:, 0, :], ALU.mult, ALU.mult
                                     ).then_inc(stats_step, 1)
            dve.wait_ge(stats_step, 5)
            dve.scalar_tensor_tensor(mv[:, :, 1], st[:, 2, :], 1.0 / D, st[:, 0, :], ALU.mult, ALU.add
                                     ).then_inc(stats_step, 1)

        def finish_rstd(pool, stats_step, eps_added):
            pool.wait_ge(stats_step, 6)
            pool.tensor_scalar(veps[:], mv[:, :, 1], LN_EPS, 1.0, ALU.add, ALU.mult).then_inc(eps_added, 1)
            pool.wait_ge(eps_added, 1)
            pool.tensor_tensor(rstd[:], veps[:], neg_half[:], ALU.pow)

        x_dram = x.rearrange("b t d -> t b d")
        out_dram = out.rearrange("b t d -> t b d")

        kbd = sb("kbd", [P, 2, COLS])
        vbd = sb("vbd", [P, 2, COLS + P])
        pr = sb("pr", [P, 2, COLS])
        pT = sb("pT", [P, COLS])
        work = sb("work", [P, 4, 2, D])
        xn, xnT, qT, tmp = (work[:, i] for i in range(4))
        oT = sb("oT", [P, 2, P])
        rT = sb("rT", [P, 2, P])
        mxm = sb("mxm", [P, 2, H])
        mxr = sb("mxr", [P, 2, H])
        mx = sb("mx", [P, 2, H])
        smm = sb("smm", [P, 2, H])
        smr = sb("smr", [P, 2, H])
        sm = sb("sm", [P, 2, H])
        rc = sb("rc", [P, 2, H])
        rx = sb("rx", [P, 2, P])

        with ExitStack() as su:
            yrep = sb("yrep", [DC, B, 2, P], stack=su)
            w1_sb = sb("w1_sb", [P, E, 4, P], stack=su)
            wk01 = sb("wk01", [DC, 2, D], stack=su)
            wv01 = sb("wv01", [DC, 2, D], stack=su)
            w2_sb = sb("w2_sb", [P, E, I], stack=su)
            wq1_sb = sb("wq1_sb", [P, D], stack=su)
            wkv_sb = sb("wkv_sb", [P, 2, DC], stack=su)
            ffn_sb = sb("ffn_sb", [P, 3, D], stack=su)
            router_sb = sb("router_sb", [E, D], stack=su)
            wo_sb = sb("wo_sb", [P, D], stack=su)
            bk_col = sb("bk_col", [P, 1], stack=su)
            bv_col = sb("bv_col", [P, 1], stack=su)
            bo_row = sb("bo_row", [1, D], stack=su)
            bo_tg = sb("bo_tg", [1, D], stack=su)
            ones_row = sb("ones_row", [1, P], stack=su)
            g_sb = sb("g_sb", [P, 4], stack=su)
            mask_u8 = sb("mask_u8", [B, P], U8, stack=su)
            yT = pr[0:DC, 0, 0:B * S2].rearrange("p (b k) -> p b k", b=B)
            mask_f = tmp[0:B, 0, :]
            bv_bc, ones_pp = rx[:, 0, :], rx[:, 1, :]
            y_sb = kbd[0:S2].rearrange("p u c -> p (u c)")[:, 0:B * DC].rearrange("p (b c) -> p b c", b=B)
            sel_f = pT[:, 0:E * P].rearrange("p (e t) -> p e t", e=E)

            y_loaded = sem("y_loaded", su)
            small_loaded = sem("small_loaded", su)
            w_loaded = [sem(f"w_loaded{i}", su) for i in range(E // 2)]
            zeroed = sem("zeroed", su)
            ident_ready = sem("ident_ready", su)
            masks_step = sem("masks_step", su)
            yT_done = sem("yT_done", su)
            yT_copied = sem("yT_copied", su)
            yrep_ready = sem("yrep_ready", su)
            small_T = sem("small_T", su)
            small_copied = sem("small_copied", su)
            tg_ready = sem("tg_ready", su)
            scaled = sem("scaled", su)
            mask_float = sem("mask_float", su)
            router_high = sem("router_high", su)
            router_low = sem("router_low", su)
            k_done = sem("k_done", su)
            k_copied = sem("k_copied", su)
            v_done = sem("v_done", su)
            v_copied_act = sem("v_copied_act", su)
            v_copied_dve = sem("v_copied_dve", su)
            wT_done = sem("wT_done", su)
            wT_high = sem("wT_high", su)
            wT_low = sem("wT_low", su)
            stats = sem("stats", su)
            stats_step = sem("stats_step", su)
            eps_added = sem("eps_added", su)
            bias_done = sem("bias_done", su)

            SMALL = 19
            YG = [range(0, 6), range(6, 12), range(12, B)]

            with nc.Block() as block:
                @block.sync
                def _(sp):
                    sp.dma_start(y_sb, ctx_768.rearrange("b k c -> k b c")).then_inc(y_loaded, 16)
                    for dst, src in (
                        (wk01[:, 0, :], wk0), (wv01[:, 0, :], wv0), (wq0_sb[:], wq0), (wo_sb[:], wo0),
                        (wq1_sb[:], wq1), (wkv_sb[:], wkv1.rearrange("(l o) c -> o l c", l=2)),
                        (ffn_sb[:, 0, :], w_r), (ffn_sb[:, 1, :], w_k), (ffn_sb[:, 2, :], w_v),
                        (router_sb[:], router_w), (mask_u8[:], mask_BxS_bk0),
                        (bq_col[:], bq0.rearrange("(d o) -> d o", o=1)),
                        (bk_col[:], bk0.rearrange("(d o) -> d o", o=1)),
                        (bv_col[:], bv0.rearrange("(d o) -> d o", o=1)),
                        (bo_row[:], bo0.rearrange("(o d) -> o d", o=1)),
                        (mus[:, 0:1], mu_r.rearrange("(d o) -> d o", o=1)),
                        (mus[:, 1:2], mu_k.rearrange("(d o) -> d o", o=1)),
                        (g_sb[:, 0:2], g_xattn.partition_broadcast(P)), (g_sb[:, 2:4], g_ffn.partition_broadcast(P)),
                    ):
                        sp.dma_start(dst, src).then_inc(small_loaded, 16)
                    for q in range(NQ):
                        sp.dma_start(xs[:, 4 * q:4 * q + 4, :], x_dram[:, 4 * q:4 * q + 4, :]).then_inc(x_loaded[q], 16)
                    for pair in range(E // 2):
                        es = slice(2 * pair, 2 * pair + 2)
                        sp.dma_start(w1_sb[:, es], w1[es].rearrange("e (k o) i -> o e k i", o=P)
                                     ).then_inc(w_loaded[pair], 16)
                        sp.dma_start(w2_sb[:, es], w2[es].rearrange("e h i -> h e i")).then_inc(w_loaded[pair], 16)

                @block.gpsimd
                def _(pool):
                    pool.memset(ident[:], 0.0).then_inc(zeroed, 1)
                    pool.memset(head_mask[:], 1.0).then_inc(zeroed, 1)
                    pool.memset(main_mask[:], 1.0).then_inc(zeroed, 1)
                    pool.memset(rest_mask[:], 1.0).then_inc(zeroed, 1)
                    pool.memset(yrep[:], 0.0).then_inc(zeroed, 1)
                    pool.memset(ones_pp, 1.0).then_inc(zeroed, 1)
                    pool.memset(ones_row[:], 1.0).then_inc(zeroed, 1)
                    pool.memset(neg_half[:], -0.5).then_inc(zeroed, 1)
                    pool.memset(routerh[:].bitcast(F32), 0.0).then_inc(zeroed, 1)
                    pool.memset(routerl[:].bitcast(F32), 0.0).then_inc(zeroed, 1)
                    pool.memset(tri[:], 1.0).then_inc(zeroed, 1)
                    pool.memset(sel_f, 0.0).then_inc(zeroed, 1)
                    pool.wait_ge(zeroed, 12)
                    pool.affine_select(out=ident[:], in_=ident[:], compare_op=ALU.not_equal, fill=1.0, base=0,
                                       pattern=[[-1, P]], channel_multiplier=1).then_inc(ident_ready, 1)
                    n = 0
                    for mask, step, pat in ((head_mask, DH, [[-DH, H]]), (main_mask, P // 2, [[-P // 2, 2], [0, DH]]),
                                            (rest_mask, KR, [[-KR, 8]])):
                        pool.affine_select(out=mask[:], in_=mask[:], compare_op=ALU.is_ge, fill=0.0, base=0,
                                           pattern=pat, channel_multiplier=1).then_inc(masks_step, 1)
                        n += 1
                        pool.wait_ge(masks_step, n)
                        pool.affine_select(out=mask[:], in_=mask[:], compare_op=ALU.is_ge, fill=0.0, base=step - 1,
                                           pattern=[[-s, c] for s, c in pat], channel_multiplier=-1
                                           ).then_inc(masks_step, 1)
                        n += 1
                    pool.affine_select(out=tri[:], in_=tri[:], compare_op=ALU.is_gt, fill=0.0, base=0,
                                       pattern=[[1, E], [-1, E]], channel_multiplier=0)
                    for base in (0, -E):
                        pool.affine_select(out=sel_f, in_=sel_f, compare_op=ALU.not_equal, fill=1.0, base=base,
                                           pattern=[[-1, E], [0, P]], channel_multiplier=1).then_inc(masks_step, 1)
                        n += 1
                        pool.wait_ge(masks_step, n)
                    pool.tensor_copy(sel[:], sel_f)
                    pool.memset(combT[:].bitcast(F32), 0.0)
                    pool.memset(vbd[:], 0.0)
                    pool.wait_ge(yT_done, 3)
                    pool.memset(kbd[:], 0.0)
                    pool.wait_ge(yrep_ready, 2)
                    pool.wait_ge(k_done, 6)
                    pool.memset(pr[:], 0.0)
                    finish_rstd(pool, stats_step, eps_added)

                @block.tensor
                def _(pe):
                    pe.wait_ge(ident_ready, 1)
                    pe.wait_ge(y_loaded, 16)
                    for n, group in enumerate(YG):
                        for i, b in enumerate(group):
                            mm = pe.transpose(pbank(n)[0:DC, i * S2:(i + 1) * S2], y_sb[:, b, :], ident[0:S2, 0:S2])
                        mm.then_inc(yT_done, 1)
                    pe.wait_ge(small_loaded, 16 * SMALL)
                    pe.wait_ge(mask_float, 1)
                    pe.transpose(pbank(3)[:, 0:128], wq1_sb[:], ident[:])
                    for i in range(2):
                        pe.transpose(pbank(3)[0:DC, 128 + 128 * i:256 + 128 * i], wkv_sb[:, i, :], ident[:])
                    pe.transpose(pbank(3)[:, 384:384 + B], mask_f, ident[0:B, 0:B])
                    pe.transpose(pbank(3)[:, 400:400 + E], router_sb[:], ident[0:E, 0:E]).then_inc(small_T, 1)
                    for i in range(3):
                        mm = pe.transpose(pbank(4)[:, 128 * i:128 * i + 128], ffn_sb[:, i, :], ident[:])
                    mm.then_inc(small_T, 1)
                    pe.wait_ge(yT_copied, 3)
                    pe.wait_ge(small_copied, 2)
                    n = 0
                    for layer in range(2):
                        for group in YG:
                            if n >= 3:
                                pe.wait_ge(k_copied, n - 2)
                            w = len(group) * S2
                            pe.matmul(pbank(5 + n % 3)[:, 0:w], wk01[:, layer, :],
                                      yT[:, group[0]:group[-1] + 1, :], start=True, stop=True).then_inc(k_done, 1)
                            n += 1
                    pe.wait_ge(yrep_ready, 2)
                    for b in range(B):
                        if b >= 2:
                            pe.wait_ge(v_copied_dve if b % 2 else v_copied_act, b // 2)
                        for part in range(2):
                            mm = pe.matmul(pbank(b % 2)[:, 256 * part:256 * part + 256], yrep[:, b, part, :],
                                           wv01[:], start=True, stop=True)
                        mm.then_inc(v_done, 1)
                    pe.wait_ge(scaled, 3)
                    pe.matmul(pbank(2)[:, 0:D], bv_bc, wo_tg[:], start=True, stop=False)
                    pe.matmul(pbank(2)[:, 0:D], ones_row[:], bo_tg[:], start=False, stop=True).then_inc(bias_done, 1)
                    n = 0
                    for pair in range(E // 2):
                        pe.wait_ge(w_loaded[pair], 32)
                        for g in range(3):
                            if n >= 2:
                                pe.wait_ge(wT_low, n - 1)
                            else:
                                pe.wait_ge(small_copied, 4)
                                pe.wait_ge(router_low, 1)
                            for i in range(4):
                                src = (w1_sb[:, 2 * pair + g, i, :] if g < 2 else
                                       w2_sb[:, 2 * pair + i // 2, P * (i % 2):P * (i % 2) + P])
                                mm = pe.transpose(pbank(3 + n % 2)[:, P * i:P * i + P], src, ident[:])
                            mm.then_inc(wT_done, 1)
                            n += 1

                @block.scalar
                def _(act):
                    act.wait_ge(small_loaded, 16 * SMALL)
                    act.activation(tg[:], g_sb[:], ACT.Tanh).then_inc(tg_ready, 1)
                    for n, group in enumerate(YG):
                        act.wait_ge(yT_done, n + 1)
                        act.copy(yT[:, group[0]:group[-1] + 1, :],
                                 pbank(n)[0:DC, 0:len(group) * S2]).then_inc(yT_copied, 1)
                    act.wait_ge(small_T, 1)
                    act.copy(wk01[:, 1, :], pbank(3)[0:DC, 128:256]).then_inc(small_copied, 1)
                    act.copy(wv01[:, 1, :], pbank(3)[0:DC, 256:384]).then_inc(small_copied, 1)
                    act.copy(wq1T[:], pbank(3)[:, 0:128]).then_inc(small_copied, 1)
                    act.copy(valid[:], pbank(3)[:, 384:384 + B])
                    act.wait_ge(zeroed, 12)
                    act.copy(routerh[:, 0:E], pbank(3)[:, 400:400 + E]).then_inc(router_high, 1)
                    act.wait_ge(small_T, 2)
                    act.copy(w_rT[:], pbank(4)[:, 0:128])
                    act.copy(w_kT[:], pbank(4)[:, 128:256])
                    act.copy(w_vT[:], pbank(4)[:, 256:384]).then_inc(small_copied, 1)
                    n = 0
                    for layer in range(2):
                        for group in YG:
                            act.wait_ge(k_done, n + 1)
                            act.activation(kT[:, layer, group[0]:group[-1] + 1, :],
                                           pbank(5 + n % 3)[:, 0:len(group) * S2], ACT.Identity,
                                           bias=bk_col[:] if layer == 0 else 0.0).then_inc(k_copied, 1)
                            n += 1
                    for b in range(0, B, 2):
                        act.wait_ge(v_done, b + 1)
                        act.copy(vc[:, b].rearrange("p a l d -> p (a l d)"), pbank(0)).then_inc(v_copied_act, 1)
                    act.wait_ge(bias_done, 1)
                    act.copy(bias_bc[:], pbank(2)[:, 0:D])
                    for n in range(3 * E // 2):
                        pair, g = n // 3, n % 3
                        act.wait_ge(wT_done, n + 1)
                        act.copy(w1h[:, 2 * pair + g, :] if g < 2 else
                                 w2h[:, 2 * pair:2 * pair + 2].rearrange("p e k d -> p (e k d)"),
                                 pbank(3 + n % 2)).then_inc(wT_high, 1)

                @block.vector
                def _(dve):
                    dve.wait_ge(small_loaded, 16 * SMALL)
                    dve.tensor_copy(mask_f, mask_u8[:]).then_inc(mask_float, 1)
                    dve.tensor_scalar(mus[:, 2:4], mus[:, 0:2], -1.0, 1.0, ALU.mult, ALU.add)
                    dve.wait_ge(tg_ready, 1)
                    dve.wait_ge(zeroed, 12)
                    dve.tensor_scalar(wo_tg[:], wo_sb[:], tg[:, 0:1], None, ALU.mult).then_inc(scaled, 1)
                    dve.tensor_scalar(bo_tg[:], bo_row[:], tg[0:1, 0:1], None, ALU.mult).then_inc(scaled, 1)
                    dve.tensor_scalar(bv_bc, ones_pp, bv_col[:, 0:1], None, ALU.mult).then_inc(scaled, 1)
                    dve.wait_ge(yT_copied, 3)
                    dve.tensor_copy(yrep[:, :, 0, :].rearrange("c b (r k) -> c b r k", r=2),
                                    yT[:, :, 0:KM].unsqueeze(2).to_broadcast([DC, B, 2, KM])).then_inc(yrep_ready, 1)
                    dve.tensor_copy(yrep[:, :, 1, :].rearrange("c b (r k) -> c b r k", r=8)[:, :, :, 0:NR],
                                    yT[:, :, KM:S2].unsqueeze(2).to_broadcast([DC, B, 8, NR])).then_inc(yrep_ready, 1)
                    dve.wait_ge(router_high, 1)
                    dve.tensor_tensor(routerl[:, 0:E], pbank(3)[:, 400:400 + E], routerh[:, 0:E].bitcast(F32),
                                      ALU.subtract).then_inc(router_low, 1)
                    for b in range(B):
                        if b % 4 == 0:
                            dve.wait_ge(x_loaded[b // 4], 16)
                        if b % 2:
                            dve.wait_ge(v_done, b + 1)
                            dve.tensor_copy(vc[:, b].rearrange("p a l d -> p (a l d)"),
                                            pbank(1)).then_inc(v_copied_dve, 1)
                        dve.bn_stats(bns[:, b].rearrange("p a s -> p (a s)"), xs[:, b, :]).then_inc(stats, 1)
                    dve.wait_ge(stats, B)
                    finish_stats(dve, stats_step)
                    for n in range(3 * E // 2):
                        pair, g = n // 3, n % 3
                        dve.wait_ge(wT_high, n + 1)
                        hi, lo = ((w1h[:, 2 * pair + g, :], w1l[:, 2 * pair + g, :]) if g < 2 else
                                  [w[:, 2 * pair:2 * pair + 2].rearrange("p e k d -> p (e k d)") for w in (w2h, w2l)])
                        dve.tensor_tensor(lo, pbank(3 + n % 2), hi.bitcast(F32), ALU.subtract).then_inc(wT_low, 1)

        def attention(layer):
            with ExitStack() as at:
                def s_(name):
                    return sem(f"{name}{layer}", at)

                xn_ready = s_("xn_ready")
                bias_added = s_("bias_added")
                xnT_done = s_("xnT_done")
                xnT_ready = s_("xnT_ready")
                q_done = s_("q_done")
                q_ready = s_("q_ready")
                kbd_ready = s_("kbd_ready")
                vbd_ready = s_("vbd_ready")
                scored = s_("scored")
                part_max = s_("part_max")
                max_ready = s_("max_ready")
                shifted = s_("shifted")
                exp_done = s_("exp_done")
                part_sum = s_("part_sum")
                sum_ready = s_("sum_ready")
                recip_ready = s_("recip_ready")
                rx_ready = s_("rx_ready")
                rT_done = s_("rT_done")
                rT_ready = s_("rT_ready")
                pT_done = s_("pT_done")
                pT_ready = s_("pT_ready")
                pv_done = s_("pv_done")
                oT_ready = s_("oT_ready")
                out_done = s_("out_done")
                scaled_out = s_("scaled_out")
                factor_ready = s_("factor_ready")
                res_done = s_("res_done")
                stats = s_("stats")
                stats_step = s_("stats_step")
                eps_added = s_("eps_added")

                tile_xs = xs[:].rearrange("p (g u) d -> p g u d", u=2)
                tile_mv = mv[:].rearrange("p (g u) s -> p g u s", u=2)
                tile_bns = bns[:].rearrange("p (g u) a s -> p g u (a s)", u=2)
                tile_rstd = rstd[:].rearrange("p (g u) -> p g u", u=2)
                tile_rstd_valid = rstd_valid[:].rearrange("p (g u) -> p g u", u=2)
                tile_kT = kT[:, layer].rearrange("p (g u) k -> p g u k", u=2)
                tile_vc = vc[:].rearrange("p (g u) a l d -> p g u a l d", u=2)

                xn_ps = bank[0][:, 0:P]
                rT_ps = bank[0][:, P:2 * P]
                q_ps = bank[0][:, 2 * P:3 * P]
                o_ps = bank[1][:, 0:P]
                out_ps = bank[1][:, P:2 * P]
                GROUPS = [(0, 4), (4, 8), (8, CH)]

                def pr_main(u):
                    return pr[:, u, 0:MAIN].rearrange("p (h k) -> p h k", h=H)

                def pr_rest(u):
                    return pr[:, u, MAIN:COLS].rearrange("p (h k) -> p h k", h=H)[:, :, 0:NR]

                def parts(u):
                    return pr_main(u)[:, 0:H // 2], pr_main(u)[:, H // 2:H], pr_rest(u)

                def parts_by_head(m, u):
                    return m[:, u, 0:H // 2], m[:, u, H // 2:H], m[:, u, :]

                sc_main = scores_ps[:, 0:MAIN].rearrange("p (h k) -> p h k", h=H)
                sc_rest = scores_ps[:, MAIN:COLS].rearrange("p (h k) -> p h k", h=H)[:, :, 0:NR]

                def slots(eng, body):
                    for t in range(4):
                        body(t // 2, t % 2, t)
                    with eng.Fori(2, B // 2 - 1) as g:
                        for u in range(2):
                            body(g, u, 2 * g + u)
                    for t in range(B - 2, B + 3):
                        body(t // 2, t % 2, t)

                def stage(t, k):
                    return not isinstance(t, int) or k <= t < B + k

                with nc.Block() as block:
                    @block.gpsimd
                    def _(pool):
                        def body(g, u, t):
                            if stage(t, 0):
                                if stage(t, 2):
                                    pool.wait_ge(scored, t - 1)
                                src = tile_kT[:, g, u, :]
                                pool.tensor_tensor(
                                    kbd[:, u, 0:MAIN].rearrange("p (h k) -> p h k", h=H),
                                    src[:, 0:KM].unsqueeze(1).to_broadcast([P, H, KM]),
                                    head_mask[:].unsqueeze(2).to_broadcast([P, H, KM]), ALU.mult).then_inc(kbd_ready, 1)
                                pool.tensor_tensor(
                                    kbd[:, u, MAIN:COLS].rearrange("p (h k) -> p h k", h=H)[:, :, 0:NR],
                                    src[:, KM:S2].unsqueeze(1).to_broadcast([P, H, NR]),
                                    head_mask[:].unsqueeze(2).to_broadcast([P, H, NR]), ALU.mult).then_inc(kbd_ready, 1)
                                if stage(t, 2):
                                    pool.wait_ge(pv_done, t - 1)
                                v = tile_vc[:, g, u, :, layer, :]
                                pool.tensor_tensor(
                                    vbd[:, u, 0:CM * (P + 2 * DH)].rearrange("p (c w) -> p c w", c=CM)[:, :, 0:2 * DH],
                                    v[:, 0, :].rearrange("p (c r) -> p c r", c=CM),
                                    main_mask[:].unsqueeze(1).to_broadcast([P, CM, 2 * DH]), ALU.mult
                                ).then_inc(vbd_ready, 1)
                                pool.tensor_tensor(
                                    vbd[:, u, MAIN:MAIN + 2 * (P + 8 * DH)].rearrange("p (c w) -> p c w", c=2)[
                                        :, :, 0:8 * DH].rearrange("p c (h d) -> p c h d", h=8),
                                    v[:, 1, :].rearrange("p (c h d) -> p c h d", c=2, h=8),
                                    rest_mask[:].unsqueeze(1).unsqueeze(3).to_broadcast([P, 2, 8, DH]), ALU.mult
                                ).then_inc(vbd_ready, 1)
                                if layer == 0:
                                    pool.wait_ge(xn_ready, t + 1)
                                    pool.tensor_tensor(tile_xs[:, g, u, :], tile_xs[:, g, u, :], bias_bc[:],
                                                       ALU.add).then_inc(bias_added, 1)

                        slots(pool, body)
                        finish_rstd(pool, stats_step, eps_added)

                    @block.tensor
                    def _(pe):
                        def body(g, u, t):
                            if stage(t, 0):
                                pe.wait_ge(xn_ready, t + 1)
                                if stage(t, 1):
                                    pe.wait_ge(q_ready, t)
                                if stage(t, 3) and layer == 0:
                                    pe.wait_ge(rT_ready, t - 2)
                                pe.transpose(xn_ps, xn[:, u, :], ident[:]).then_inc(xnT_done, 1)
                            if stage(t, 2):
                                pe.wait_ge(exp_done, 3 * (t - 1))
                                if stage(t, 3):
                                    pe.wait_ge(pT_ready, 3 * (t - 2))
                                for n, (c0, c1) in enumerate(GROUPS):
                                    for c in range(c0, c1):
                                        mm = pe.transpose(bank[2 + n][:, P * (c - c0):P * (c - c0) + P],
                                                          pr[:, u, P * c:P * c + P], ident[:])
                                    mm.then_inc(pT_done, 1)
                            if stage(t, 0):
                                pe.wait_ge(xnT_ready, t + 1)
                            if stage(t, 2) and layer == 0:
                                pe.wait_ge(rx_ready, t - 1)
                                if not stage(t, 0):
                                    pe.wait_ge(q_ready, B)
                                pe.transpose(rT_ps, rx[:, u, :], ident[:]).then_inc(rT_done, 1)
                            if stage(t, 0):
                                pe.matmul(q_ps, wq0_sb[:] if layer == 0 else wq1T[:], xnT[:, u, :],
                                          start=True, stop=True).then_inc(q_done, 1)
                            if stage(t, 2):
                                pe.wait_ge(vbd_ready, 2 * (t - 1))
                                if stage(t, 3):
                                    pe.wait_ge(out_read, t - 2)
                                for n, (c0, c1) in enumerate(GROUPS):
                                    pe.wait_ge(pT_ready, 3 * (t - 2) + n + 1)
                                    for c in range(c0, c1):
                                        mm = pe.matmul(o_ps, vbd[:, u, P * c:P * c + P], pT[:, P * c:P * c + P],
                                                       start=(c == 0), stop=(c == CH - 1))
                                mm.then_inc(pv_done, 1)
                            if stage(t, 0):
                                pe.wait_ge(q_ready, t + 1)
                                pe.wait_ge(kbd_ready, 2 * (t + 1))
                                if stage(t, 1):
                                    pe.wait_ge(shifted, 3 * t)
                                for c0 in range(0, COLS, 512):
                                    c1 = min(c0 + 512, COLS)
                                    mm = pe.matmul(scores_ps[:, c0:c1], qT[:, u, :], kbd[:, u, c0:c1],
                                                   start=True, stop=True)
                                mm.then_inc(scored, 1)
                            if stage(t, 2):
                                pe.wait_ge(oT_ready, t - 1)
                                if layer == 0:
                                    pe.matmul(out_ps, oT[:, u, :], wo_tg[:], start=True, stop=True
                                              ).then_inc(out_done, 1)
                                else:
                                    pe.transpose(out_ps, oT[:, u, :], ident[:]).then_inc(out_done, 1)

                        out_read = res_done if layer == 0 else scaled_out
                        slots(pe, body)

                    @block.scalar
                    def _(act):
                        def body(g, u, t):
                            if stage(t, 0):
                                act.wait_ge(xnT_done, t + 1)
                                act.copy(xnT[:, u, :], xn_ps).then_inc(xnT_ready, 1)
                            if stage(t, 2):
                                if stage(t, 3):
                                    act.wait_ge(pv_done, t - 2)
                                for n, (c0, c1) in enumerate(GROUPS):
                                    act.wait_ge(pT_done, 3 * (t - 2) + n + 1)
                                    act.copy(pT[:, P * c0:P * c1], bank[2 + n][:, 0:P * (c1 - c0)]).then_inc(pT_ready, 1)
                            if stage(t, 0):
                                act.wait_ge(q_done, t + 1)
                                act.activation(qT[:, u, :], q_ps, ACT.Identity,
                                               bias=bq_col[:] if layer == 0 else 0.0).then_inc(q_ready, 1)
                            if stage(t, 2) and layer == 0:
                                act.wait_ge(rT_done, t - 1)
                                act.copy(rT[:, u, :], rT_ps).then_inc(rT_ready, 1)
                            if stage(t, 1):
                                for n, part in enumerate(parts(1 - u)):
                                    act.wait_ge(shifted, 3 * (t - 1) + n + 1)
                                    act.activation(part, part, ACT.Exp, scale=SCALE).then_inc(exp_done, 1)
                                    if n == 1 and stage(t, 2) and layer == 1:
                                        act.wait_ge(pv_done, t - 1)
                                        act.copy(oT[:, u, :], o_ps).then_inc(oT_ready, 1)
                            elif stage(t, 2) and layer == 1:
                                act.wait_ge(pv_done, t - 1)
                                act.copy(oT[:, u, :], o_ps).then_inc(oT_ready, 1)

                        slots(act, body)

                    @block.vector
                    def _(dve):
                        def normalise(g, u, t):
                            factor = tile_rstd if layer == 0 else tile_rstd_valid
                            dve.tensor_scalar(xn[:, u, :], tile_xs[:, g, u, :], tile_mv[:, g, u, 0:1],
                                              factor[:, g, u:u + 1], ALU.subtract, ALU.mult).then_inc(xn_ready, 1)

                        def body(g, u, t):
                            v = 1 - u
                            if stage(t, 1):
                                dve.wait_ge(scored, t)
                                dve.tensor_reduce(mxm[:, v, :], sc_main, AX.X, ALU.max).then_inc(part_max, 1)
                                dve.tensor_reduce(mxr[:, v, :], sc_rest, AX.X, ALU.max).then_inc(part_max, 1)
                            if stage(t, 3):
                                xt = tile_xs[:, g - 2 + u, v, :]
                                dve.wait_ge(out_done, t - 2)
                                if layer == 0:
                                    dve.wait_ge(bias_added, t - 2)
                                    dve.tensor_tensor(xt, xt, out_ps, ALU.add).then_inc(res_done, 1)
                                else:
                                    dve.tensor_tensor(tmp[:, v, :], out_ps, rx[:, v, :], ALU.mult
                                                      ).then_inc(scaled_out, 1)
                            if stage(t, 1):
                                dve.wait_ge(part_max, 2 * t)
                                dve.tensor_tensor(mx[:, v, :], mxm[:, v, :], mxr[:, v, :], ALU.max
                                                  ).then_inc(max_ready, 1)
                            if stage(t, 3):
                                if layer == 0:
                                    dve.wait_ge(res_done, t - 2)
                                    dve.wait_ge(pT_ready, 3)
                                    dve.bn_stats(tile_bns[:, g - 2 + u, v, :], xt).then_inc(stats, 1)
                                else:
                                    dve.wait_ge(scaled_out, t - 2)
                                    dve.tensor_tensor(xt, xt, tmp[:, v, :], ALU.add).then_inc(res_done, 1)
                            if stage(t, 1):
                                dve.wait_ge(max_ready, t)
                                if stage(t, 3):
                                    dve.wait_ge(pT_done, 3 * (t - 2))
                                for part, ps, m in zip(parts(v), (sc_main[:, 0:H // 2], sc_main[:, H // 2:H], sc_rest),
                                                       parts_by_head(mx, v)):
                                    dve.tensor_tensor(part, ps, m.unsqueeze(2).to_broadcast([P, *part.shape[1:]]),
                                                      ALU.subtract).then_inc(shifted, 1)
                            if stage(t, 3) and layer == 1:
                                dve.wait_ge(res_done, t - 2)
                                dve.wait_ge(pT_ready, 3)
                                dve.bn_stats(tile_bns[:, g - 2 + u, v, :], xt).then_inc(stats, 1)
                            if stage(t, -1) and stage(t, 0):
                                if stage(t, 1):
                                    dve.wait_ge(xnT_done, t)
                                normalise(g + u, v, t + 1)
                            if stage(t, 1):
                                dve.wait_ge(exp_done, 3 * t)
                                dve.tensor_reduce(smm[:, v, :], pr_main(v), AX.X, ALU.add).then_inc(part_sum, 1)
                                dve.tensor_reduce(smr[:, v, :], pr_rest(v), AX.X, ALU.add).then_inc(part_sum, 1)
                            if stage(t, 2) and layer == 0:
                                dve.wait_ge(pv_done, t - 1)
                                dve.wait_ge(rT_ready, t - 1)
                                dve.tensor_tensor(oT[:, u, :], o_ps, rT[:, u, :], ALU.mult).then_inc(oT_ready, 1)
                            if stage(t, 1):
                                dve.wait_ge(part_sum, 2 * t)
                                dve.tensor_tensor(sm[:, v, :], smm[:, v, :], smr[:, v, :], ALU.add).then_inc(sum_ready, 1)
                                dve.wait_ge(sum_ready, t)
                                dve.reciprocal(rc[:, v, :], sm[:, v, :]).then_inc(recip_ready, 1)
                                dve.wait_ge(recip_ready, t)
                                if layer == 0 and stage(t, 3):
                                    dve.wait_ge(rT_done, t - 2)
                                dve.tensor_scalar(rx[:, v, :].rearrange("p (h d) -> p h d", h=H),
                                                  rc[:, v, :].unsqueeze(2).to_broadcast([P, H, DH]),
                                                  1.0 if layer == 0 else tg[:, 1:2], None, ALU.mult
                                                  ).then_inc(rx_ready, 1)

                        if layer == 1:
                            dve.tensor_tensor(rstd_valid[:], rstd[:], valid[:], ALU.mult).then_inc(factor_ready, 1)
                            dve.wait_ge(factor_ready, 1)
                        normalise(0, 0, 0)
                        slots(dve, body)
                        dve.wait_ge(stats, B)
                        finish_stats(dve, stats_step)

        attention(0)

        with ExitStack() as mo:
            UNITS = 2 * E
            LAG = 3
            HEAD = 6
            xm = work[:, 0:2].rearrange("p k u d -> p (k u) d")
            om = work[:, 2:4].rearrange("p k u d -> p (k u d)")
            sg = pT[:, 0:1024].rearrange("p (u n) -> p u n", u=2)
            xTh = sb("xTh", [P, NQ, 512], F32R, stack=mo)
            xTl = sb("xTl", [P, NQ, 512], F32R, stack=mo)
            lgT = sb("lgT", [P, 512], stack=mo)
            lg = sb("lg", [P, 4, E], stack=mo)
            lm = sb("lm", [P, 4], stack=mo)
            ex = sb("ex", [P, 4, E], stack=mo)
            es = sb("es", [P, 4], stack=mo)
            er = sb("er", [P, 4], stack=mo)
            gt = sb("gt", [P, 4, E, E], stack=mo)
            ge = sb("ge", [P, 4, E, E], stack=mo)
            rank = sb("rank", [P, 4, E], stack=mo)
            comb = sb("comb", [P, 4, E], stack=mo)
            comb2 = sb("comb2", [P, 4, 2 * E], stack=mo)
            au = sb("au", [P, 2, 512], stack=mo)
            yv = sb("yv", [P, 2, 512], stack=mo)
            yh = sb("yh", [P, 4, 512], F32R, stack=mo)
            yl = sb("yl", [P, 4, 512], F32R, stack=mo)

            xn_ready = sem("m_xn_ready", mo)
            xT_done = sem("m_xT_done", mo)
            xT_high = sem("m_xT_high", mo)
            xT_low = sem("m_xT_low", mo)
            lgT_done = sem("m_lgT_done", mo)
            lgT_ready = sem("m_lgT_ready", mo)
            routed = sem("m_routed", mo)
            route_step = sem("m_route_step", mo)
            exp_ready = sem("m_exp_ready", mo)
            comb_ready = sem("m_comb_ready", mo)
            combT_done = sem("m_combT_done", mo)
            combT_ready = sem("m_combT_ready", mo)
            h_done = sem("m_h_done", mo)
            silu_done = sem("m_silu_done", mo)
            up_done = sem("m_up_done", mo)
            weight_spread = sem("m_weight_spread", mo)
            y_done = sem("m_y_done", mo)
            y_high = sem("m_y_high", mo)
            y_low = sem("m_y_low", mo)
            down_done = sem("m_down_done", mo)
            oT_ready = sem("m_oT_ready", mo)
            o_done = sem("m_o_done", mo)
            res_done = sem("m_res_done", mo)
            stats = sem("m_stats", mo)
            stats_step = sem("m_stats_step", mo)
            eps_added = sem("m_eps_added", mo)

            STEPS = 13
            cb_ps, row_ps, mo_ps, col_ps = pbank(4), pbank(5), pbank(6), pbank(7)
            q_xs = xs[:].rearrange("p (q i) d -> p q i d", i=4)
            q_mv = mv[:].rearrange("p (q i) s -> p q i s", i=4)
            q_rstd = rstd[:].rearrange("p (q i) -> p q i", i=4)
            q_bns = bns[:].rearrange("p (q i) a s -> p q i (a s)", i=4)

            def gate_ps(j):
                return pbank(2 * (j % 2))

            def up_ps(j):
                return pbank(2 * (j % 2) + 1)

            def program(eng, unit, prepare, finish):
                for piece in range(11):
                    prepare(0, piece)
                for j in range(HEAD):
                    unit(0, j, j)
                with eng.Fori(0, NQ - 1) as q:
                    for j in range(HEAD, UNITS):
                        unit(q, j, q * UNITS + j)
                        prepare(q + 1, j - HEAD)
                    for j in range(HEAD):
                        unit(q + 1, j, q * UNITS + UNITS + j)
                        if j == 0:
                            prepare(q + 1, 10)
                        finish(q, j)
                for j in range(HEAD, UNITS):
                    unit(NQ - 1, j, (NQ - 1) * UNITS + j)
                for j in range(HEAD):
                    finish(NQ - 1, j)

            with nc.Block() as block:
                @block.tensor
                def _(pe):
                    def inner(q, j, n):
                        e, half = j // 2, j % 2
                        if not (isinstance(n, int) and n < 2):
                            pe.wait_ge(up_done, n - 1)
                        if j == 0:
                            pe.wait_ge(xT_low, q + 1)
                        for ps, off in ((gate_ps(j), half * P), (up_ps(j), I + half * P)):
                            wh, wl = w1h[:, e, off:off + P], w1l[:, e, off:off + P]
                            pe.matmul(ps, wl, xTh[:, q, :], start=True, stop=False)
                            pe.matmul(ps, wh, xTl[:, q, :], start=False, stop=False)
                            mm = pe.matmul(ps, wh, xTh[:, q, :], start=False, stop=True)
                        mm.then_inc(h_done, 1)

                    def spread(q, j, n):
                        if not (isinstance(n, int) and n < 2):
                            pe.wait_ge(y_done, n)
                        if j == 0:
                            pe.wait_ge(combT_ready, q + 1)
                        pe.matmul(cb_ps, sel[:, j // 2, :], combT[:, q, :], start=True, stop=True
                                  ).then_inc(weight_spread, 1)

                    def outer(q, j, n):
                        e, half, u = j // 2, j % 2, j % 4
                        pe.wait_ge(y_low, n + 1)
                        if j == 0 and not (isinstance(q, int) and q == 0):
                            pe.wait_ge(oT_ready, q)
                        pe.matmul(mo_ps, w2l[:, e, half, :], yh[:, u, :], start=(j == 0), stop=False)
                        pe.matmul(mo_ps, w2h[:, e, half, :], yl[:, u, :], start=False, stop=False)
                        pe.matmul(mo_ps, w2h[:, e, half, :], yh[:, u, :], start=False, stop=(j == UNITS - 1)
                                  ).then_inc(down_done, 1)

                    def unit(q, j, n):
                        inner(q, j, n)
                        if j >= LAG:
                            outer(q, j - LAG, n - LAG)
                        elif not isinstance(n, int):
                            outer(q - 1, j - LAG + UNITS, n - LAG)
                        if j % 2 == 0:
                            spread(q, j, n)

                    def prepare(g, piece):
                        if piece == 1:
                            pe.wait_ge(xn_ready, 4 * g + 4)
                            if not isinstance(g, int):
                                pe.wait_ge(res_done, g - 1)
                            for i in range(4):
                                mm = pe.transpose(col_ps[:, P * i:P * i + P], xm[:, i, :], ident[:])
                            mm.then_inc(xT_done, 1)
                        if piece == 3:
                            pe.wait_ge(xT_low, g + 1)
                            if not isinstance(g, int):
                                pe.wait_ge(combT_ready, g)
                            pe.matmul(row_ps, routerl[:], xTh[:, g, :], start=True, stop=False)
                            pe.matmul(row_ps, routerh[:], xTl[:, g, :], start=False, stop=False)
                            pe.matmul(row_ps, routerh[:], xTh[:, g, :], start=False, stop=True
                                      ).then_inc(lgT_done, 1)
                        if piece == 4:
                            pe.wait_ge(lgT_ready, g + 1)
                            for i in range(4):
                                mm = pe.transpose(col_ps[:, P * i:P * i + P], lgT[:, P * i:P * i + P], ident[:])
                            mm.then_inc(routed, 1)
                        if piece == 9:
                            pe.wait_ge(comb_ready, g + 1)
                            for i in range(4):
                                mm = pe.transpose(row_ps[0:2 * E, P * i:P * i + P], comb2[:, i, :], ident[:])
                            mm.then_inc(combT_done, 1)

                    def finish(q, j):
                        if isinstance(q, int) and j < LAG:
                            outer(q, UNITS - LAG + j, q * UNITS + UNITS - LAG + j)
                        if j == 4:
                            pe.wait_ge(oT_ready, q + 1)
                            pe.wait_ge(route_step, STEPS * q + STEPS)
                            for i in range(4):
                                mm = pe.transpose(col_ps[:, P * i:P * i + P], om[:, P * i:P * i + P], ident[:])
                            mm.then_inc(o_done, 1)

                    program(pe, unit, prepare, finish)

                @block.scalar
                def _(act):
                    def high(j, n):
                        act.wait_ge(y_done, n + 1)
                        if not (isinstance(n, int) and n < 4):
                            act.wait_ge(down_done, n - 3)
                        act.copy(yh[:, j % 4, :], yv[:, j % 2, :]).then_inc(y_high, 1)

                    def unit(q, j, n):
                        act.wait_ge(h_done, n + 1)
                        act.activation(sg[:, j % 2, :], gate_ps(j), ACT.Silu).then_inc(silu_done, 1)
                        if not (isinstance(n, int) and n == 0):
                            high((j - 1) % UNITS, n - 1)

                    def prepare(g, piece):
                        if piece == 1:
                            act.wait_ge(xT_done, g + 1)
                            act.copy(xTh[:, g, :], col_ps).then_inc(xT_high, 1)
                        if piece == 3:
                            act.wait_ge(lgT_done, g + 1)
                            act.copy(lgT[:], row_ps).then_inc(lgT_ready, 1)
                        if piece == 6:
                            act.wait_ge(route_step, STEPS * g + 3)
                            act.activation(ex[:], ex[:], ACT.Exp).then_inc(exp_ready, 1)
                        if piece == 9:
                            act.wait_ge(combT_done, g + 1)
                            act.copy(combT[0:2 * E, g, :], row_ps[0:2 * E, :]).then_inc(combT_ready, 1)

                    def finish(q, j):
                        if isinstance(q, int) and j == 0:
                            high(UNITS - 1, q * UNITS + UNITS - 1)
                        if j == 2:
                            act.wait_ge(down_done, q * UNITS + UNITS)
                            act.copy(om, mo_ps).then_inc(oT_ready, 1)

                    program(act, unit, prepare, finish)

                @block.gpsimd
                def _(pool):
                    def unit(q, j, n):
                        pool.wait_ge(y_high, n + 1)
                        pool.tensor_tensor(yl[:, j % 4, :], yv[:, j % 2, :], yh[:, j % 4, :].bitcast(F32),
                                           ALU.subtract).then_inc(y_low, 1)

                    def nothing(*_):
                        pass

                    program(pool, unit, nothing, nothing)
                    finish_rstd(pool, stats_step, eps_added)

                @block.vector
                def _(dve):
                    def unit(q, j, n):
                        u = j % 2
                        dve.wait_ge(silu_done, n + 1)
                        dve.tensor_tensor(au[:, u, :], sg[:, u, :], up_ps(j), ALU.mult).then_inc(up_done, 1)
                        dve.wait_ge(up_done, n + 1)
                        dve.wait_ge(weight_spread, q * E + j // 2 + 1)
                        if not (isinstance(n, int) and n < 2):
                            dve.wait_ge(y_low, n - 1)
                        dve.tensor_tensor(yv[:, u, :], au[:, u, :], cb_ps, ALU.mult).then_inc(y_done, 1)

                    def prepare(g, piece):
                        def step(k, ins):
                            ins.then_inc(route_step, 1)
                            dve.wait_ge(route_step, STEPS * g + k)

                        mine = lg[:].unsqueeze(3).to_broadcast([P, 4, E, E])
                        other = lg[:].unsqueeze(2).to_broadcast([P, 4, E, E])
                        if piece == 0:
                            for i in range(4):
                                dve.tensor_scalar(xm[:, i, :], q_xs[:, g, i, :], q_mv[:, g, i, 0:1],
                                                  q_rstd[:, g, i:i + 1], ALU.subtract, ALU.mult).then_inc(xn_ready, 1)
                        if piece == 2:
                            dve.wait_ge(xT_high, g + 1)
                            dve.tensor_tensor(xTl[:, g, :], col_ps, xTh[:, g, :].bitcast(F32), ALU.subtract
                                              ).then_inc(xT_low, 1)
                        if piece == 5:
                            dve.wait_ge(routed, g + 1)
                            step(1, dve.tensor_copy(lg[:], col_ps.rearrange("p (i e) -> p i e", i=4)[:, :, 0:E]))
                            step(2, dve.tensor_reduce(lm[:], lg[:], AX.X, ALU.max))
                            step(3, dve.tensor_tensor(ex[:], lg[:], lm[:].unsqueeze(2).to_broadcast([P, 4, E]),
                                                      ALU.subtract))
                        if piece == 6:
                            dve.tensor_tensor(gt[:], other, mine, ALU.is_gt)
                            step(4, dve.tensor_tensor(ge[:], other, mine, ALU.is_equal))
                            step(5, dve.tensor_tensor(ge[:], ge[:], tri[:].unsqueeze(1).to_broadcast([P, 4, E, E]),
                                                      ALU.mult))
                        if piece == 7:
                            step(6, dve.tensor_tensor(gt[:], gt[:], ge[:], ALU.add))
                            step(7, dve.tensor_reduce(rank[:], gt[:], AX.X, ALU.add))
                            step(8, dve.tensor_scalar(rank[:], rank[:], 2.0, tg[:, 2:3], ALU.is_lt, ALU.mult))
                            dve.wait_ge(exp_ready, g + 1)
                            step(9, dve.tensor_reduce(es[:], ex[:], AX.X, ALU.add))
                        if piece == 8:
                            step(10, dve.reciprocal(er[:], es[:]))
                            step(11, dve.tensor_tensor(comb[:], ex[:], er[:].unsqueeze(2).to_broadcast([P, 4, E]),
                                                       ALU.mult))
                            step(12, dve.tensor_tensor(comb[:], comb[:], rank[:], ALU.mult))
                            step(13, dve.tensor_copy(comb2[:, :, 0:E].bitcast(F32R), comb[:]))
                            dve.tensor_tensor(comb2[:, :, E:2 * E], comb[:], comb2[:, :, 0:E], ALU.subtract
                                              ).then_inc(comb_ready, 1)

                    def finish(q, j):
                        if j == 5:
                            dve.wait_ge(o_done, q + 1)
                            dve.tensor_tensor(q_xs[:, q], q_xs[:, q], col_ps.rearrange("p (i d) -> p i d", i=4),
                                              ALU.add).then_inc(res_done, 1)
                            dve.wait_ge(res_done, q + 1)
                            dve.wait_ge(silu_done, UNITS)
                            for i in range(4):
                                dve.bn_stats(q_bns[:, q, i, :], q_xs[:, q, i, :]).then_inc(stats, 1)

                    program(dve, unit, prepare, finish)
                    dve.wait_ge(stats, B)
                    finish_stats(dve, stats_step)

        attention(1)

        with ExitStack() as ff:
            xn = sb("xn_f", [P, 2, 4, D], stack=ff)
            xT = sb("xT_f", [P, 2, 4, P + 1], stack=ff)
            pr = sb("prev_r", [P, 2, 512], stack=ff)
            pk = sb("prev_k", [P, 2, 512], stack=ff)
            xr = sb("xr", [P, 2, 512], stack=ff)
            xk = sb("xk", [P, 2, 512], stack=ff)
            rs = sb("rs", [P, 2, 512], stack=ff)
            kr = sb("kr", [P, 2, 512], stack=ff)
            kk = sb("kk", [P, 2, 512], stack=ff)
            ov = sb("ov", [P, 2, 512], stack=ff)

            cleared = sem("f_cleared", ff)
            xn_ready = sem("f_xn_ready", ff)
            xT_done = sem("f_xT_done", ff)
            xT_ready = sem("f_xT_ready", ff)
            prev_ready = sem("f_prev_ready", ff)
            mix_ready = sem("f_mix_ready", ff)
            rk_done = sem("f_rk_done", ff)
            r_ready = sem("f_r_ready", ff)
            relu_ready = sem("f_relu_ready", ff)
            kk_ready = sem("f_kk_ready", ff)
            v_done = sem("f_v_done", ff)
            ov_ready = sem("f_ov_ready", ff)
            o_done = sem("f_o_done", ff)
            res_done = sem("f_res_done", ff)

            with nc.Block() as block:
                @block.gpsimd
                def _(pool):
                    pool.memset(xT[:, :, :, 0:1], 0.0).then_inc(cleared, 1)

                @block.vector
                def _(dve):
                    def mix(n):
                        u = n % 2
                        if n >= 2:
                            dve.wait_ge(xT_done, n - 1)
                        for i in range(4):
                            b = 4 * n + i
                            dve.tensor_scalar(xn[:, u, i, :], xs[:, b, :], mv[:, b, 0:1], rstd[:, b:b + 1],
                                              ALU.subtract, ALU.mult).then_inc(xn_ready, 1)
                        cur, prev = xT[:, u, :, 1:P + 1], xT[:, u, :, 0:P]
                        dve.wait_ge(xT_ready, n + 1)
                        dve.wait_ge(cleared, 1)
                        for dst, col in ((pr, 2), (pk, 3)):
                            dve.tensor_scalar(dst[:, u, :].rearrange("p (i t) -> p i t", i=4), prev,
                                              mus[:, col:col + 1], None, ALU.mult).then_inc(prev_ready, 1)
                        dve.wait_ge(prev_ready, 2 * n + 2)
                        if n >= 2:
                            dve.wait_ge(rk_done, 2 * (n - 1))
                        for dst, add, col in ((xr, pr, 0), (xk, pk, 1)):
                            dve.scalar_tensor_tensor(dst[:, u, :].rearrange("p (i t) -> p i t", i=4), cur,
                                                     mus[:, col:col + 1],
                                                     add[:, u, :].rearrange("p (i t) -> p i t", i=4),
                                                     ALU.mult, ALU.add).then_inc(mix_ready, 1)

                    def square(n):
                        u = n % 2
                        dve.wait_ge(relu_ready, n + 1)
                        if n >= 2:
                            dve.wait_ge(v_done, n - 1)
                        dve.tensor_tensor(kk[:, u, :], kr[:, u, :], pbank(4 + u), ALU.mult).then_inc(kk_ready, 1)

                    def finish(n):
                        u = n % 2
                        dve.wait_ge(v_done, n + 1)
                        dve.wait_ge(r_ready, n + 1)
                        if n >= 2:
                            dve.wait_ge(o_done, n - 1)
                        dve.scalar_tensor_tensor(ov[:, u, :], pbank(6 + u), tg[:, 3:4], rs[:, u, :],
                                                 ALU.mult, ALU.mult).then_inc(ov_ready, 1)
                        dve.wait_ge(o_done, n + 1)
                        xq = xs[:, 4 * n:4 * n + 4, :]
                        dve.tensor_tensor(xq, xq, pbank(u).rearrange("p (i d) -> p i d", i=4), ALU.add
                                          ).then_inc(res_done, 1)

                    mix(0)
                    for n in range(NQ):
                        if n + 1 < NQ:
                            mix(n + 1)
                        square(n)
                        finish(n)

                @block.tensor
                def _(pe):
                    def first(n):
                        u = n % 2
                        if n >= 2:
                            pe.wait_ge(res_done, n - 1)
                        for i in range(4):
                            pe.wait_ge(xn_ready, 4 * n + i + 1)
                            mm = pe.transpose(pbank(u)[:, P * i:P * i + P], xn[:, u, i, :], ident[:])
                        mm.then_inc(xT_done, 1)
                        pe.wait_ge(mix_ready, 2 * n + 2)
                        if n >= 2:
                            pe.wait_ge(r_ready, n - 1)
                        pe.matmul(pbank(2 + u), w_rT[:], xr[:, u, :], start=True, stop=True).then_inc(rk_done, 1)
                        if n >= 2:
                            pe.wait_ge(kk_ready, n - 1)
                        pe.matmul(pbank(4 + u), w_kT[:], xk[:, u, :], start=True, stop=True).then_inc(rk_done, 1)

                    def second(n):
                        u = n % 2
                        pe.wait_ge(kk_ready, n + 1)
                        if n >= 2:
                            pe.wait_ge(ov_ready, n - 1)
                        pe.matmul(pbank(6 + u), w_vT[:], kk[:, u, :], start=True, stop=True).then_inc(v_done, 1)
                        pe.wait_ge(ov_ready, n + 1)
                        pe.wait_ge(xT_ready, n + 1)
                        for i in range(4):
                            mm = pe.transpose(pbank(u)[:, P * i:P * i + P], ov[:, u, P * i:P * i + P], ident[:])
                        mm.then_inc(o_done, 1)

                    first(0)
                    for n in range(NQ):
                        if n + 1 < NQ:
                            first(n + 1)
                        second(n)

                @block.scalar
                def _(act):
                    def gather(n):
                        u = n % 2
                        act.wait_ge(xT_done, n + 1)
                        if n >= 2:
                            act.wait_ge(mix_ready, 2 * (n - 1))
                        act.copy(xT[:, u, :, 1:P + 1], pbank(u).rearrange("p (i t) -> p i t", i=4)
                                 ).then_inc(xT_ready, 1)

                    gather(0)
                    for n in range(NQ):
                        u = n % 2
                        if n + 1 < NQ:
                            gather(n + 1)
                        act.wait_ge(rk_done, 2 * n + 2)
                        if n >= 2:
                            act.wait_ge(kk_ready, n - 1)
                            act.wait_ge(ov_ready, n - 1)
                        act.activation(kr[:, u, :], pbank(4 + u), ACT.Relu).then_inc(relu_ready, 1)
                        act.activation(rs[:, u, :], pbank(2 + u), ACT.Sigmoid).then_inc(r_ready, 1)

                @block.sync
                def _(sp):
                    for n in range(NQ):
                        sp.wait_ge(res_done, n + 1)
                        sp.dma_start(out_dram[:, 4 * n:4 * n + 4, :], xs[:, 4 * n:4 * n + 4, :]).then_inc(out_stored, 16)
                    sp.wait_ge(out_stored, 16 * NQ)


_INS = ['x', 'ctx_768', 'mask_BxS_bk0', 'g_xattn', 'g_ffn', 'L0_xattn_wq', 'L0_xattn_bq', 'L0_xattn_wk',
        'L0_xattn_bk', 'L0_xattn_wv', 'L0_xattn_bv', 'L0_xattn_wo', 'L0_xattn_bo', 'L0_ffn_w1', 'L0_ffn_w2',
        'L0_ffn_router_w', 'L1_xattn_Wq', 'L1_xattn_Wkv', 'L1_ffn_W_r', 'L1_ffn_W_k', 'L1_ffn_W_v', 'L1_ffn_mu_r',
        'L1_ffn_mu_k']


def kernel(**inputs):
    import numpy as _np
    import concourse.bacc as _bacc
    from concourse import mybir as _mybir
    from concourse.bass_utils import run_bass_kernel_spmd as _run

    nc = _bacc.Bacc("TRN2", target_bir_lowering=False, num_devices=1)
    arrays, args = {}, []
    for name in _INS:
        a = _np.ascontiguousarray(inputs[name])
        arrays[f"in_{name}_dram"] = a
        args.append(nc.dram_tensor(f"in_{name}_dram", a.shape, _mybir.dt.from_np(a.dtype), kind="ExternalInput").ap())
    shape = inputs["x"].shape
    out = nc.dram_tensor("out_dram", shape, _mybir.dt.float32, kind="ExternalOutput").ap()
    flamingo_kernel(nc, *args, out)
    r = _run(nc, [arrays], core_ids=[0])
    return r.results[0]["out_dram"]
```

```python
from contextlib import ExitStack

import concourse.bass as bass
from concourse import mybir

F32 = mybir.dt.float32
F32R = mybir.dt.float32r
U8 = mybir.dt.uint8
ALU = mybir.AluOpType
ACT = mybir.ActivationFunctionType
AX = mybir.AxisListType

P = 128
KM = 64
KR = 16
LN_EPS = 1e-5


def flamingo_kernel(nc, x, ctx_768, mask_BxS_bk0, g_xattn, g_ffn, wq0, bq0, wk0, bk0, wv0, bv0, wo0, bo0,
                    w1, w2, router_w, wq1, wkv1, w_r, w_k, w_v, mu_r, mu_k, out):
    B, S, D = x.shape
    _, S2, DC = ctx_768.shape
    E, I2, _ = w1.shape
    I = I2 // 2
    H = 16
    DH = D // H
    SCALE = float(DH) ** -0.5
    NR = S2 - KM
    MAIN, REST = H * KM, H * KR
    COLS = MAIN + REST
    CH = COLS // P
    RG = P // 32
    HG = H // RG
    CM = MAIN // P
    NQ = B // 4
    assert S == P and D == P and H * DH == P and 0 < NR <= KR and B % 4 == 0 and E == 8 and I == 2 * P

    with ExitStack() as ctx:
        def sb(name, shape, dt=F32, stack=ctx):
            return stack.enter_context(nc.sbuf_tensor(name, shape, dt))

        def sem(name, stack=ctx):
            return stack.enter_context(nc.semaphore(name))

        bank = [ctx.enter_context(nc.psum_tensor(f"bank{i}", [P, 512], F32)) for i in range(4)]
        scores_ps = ctx.enter_context(nc.psum_tensor("scores_ps", [P, 4 * 512], F32))

        def pbank(i):
            return bank[i][:, :] if i < 4 else scores_ps[:, (i - 4) * 512:(i - 3) * 512]

        xs = sb("xs", [P, B, D])
        mean = sb("mean", [P, B])
        rstd = sb("rstd", [P, B])
        veps = sb("veps", [P, B])
        minus_mean = sb("minus_mean", [P, B])
        shift = sb("shift", [P, B])
        ones_col = sb("ones_col", [P, 1])
        rstd_valid = sb("rstd_valid", [P, B])
        neg_half = sb("neg_half", [P, B])
        bns = sb("bns", [P, B, 2, 3])
        st = sb("st", [P, 3, B])
        ident = sb("ident", [P, P])
        tg = sb("tg", [P, 4])
        kT = sb("kT", [P, 2, B, S2])
        vc = sb("vc", [P, B, 2, 2, D])
        head_mask = sb("head_mask", [P, H])
        main_mask = sb("main_mask", [P, 2 * DH])
        rest_mask = sb("rest_mask", [P, 8])
        wq0_sb = sb("wq0_sb", [P, D])
        bq_col = sb("bq_col", [P, 1])
        wo_tg = sb("wo_tg", [P, D])
        bias_bc = sb("bias_bc", [P, D])
        wq1T = sb("wq1T", [P, D])
        valid = sb("valid", [P, B])
        w_rT = sb("w_rT", [P, D])
        w_kT = sb("w_kT", [P, D])
        w_vT = sb("w_vT", [P, D])
        mus = sb("mus", [P, 4])
        routerh = sb("routerh", [P, P], F32R)
        routerl = sb("routerl", [P, P], F32R)
        tri = sb("tri", [P, E, E])
        sel = sb("sel", [P, E, P], F32R)
        combT = sb("combT", [P, NQ, 512], F32R)
        w1h = sb("w1h", [P, E, I2], F32R)
        w1l = sb("w1l", [P, E, I2], F32R)
        w2h = sb("w2h", [P, E, 2, D], F32R)
        w2l = sb("w2l", [P, E, 2, D], F32R)

        x_loaded = [sem(f"x_loaded{q}") for q in range(NQ)]
        out_stored = sem("out_stored")

        idle = sb("idle", [P, 1])

        def load_functions(act, function):
            act.activation(idle[:], ident[:, 0:1], function)

        def join_stats(dve, stats_step, done, b, m, mm, s, v):
            even, odd = b[:, :, 0, :], b[:, :, 1, :]
            dve.tensor_tensor(s[:, 0, :], even[:, :, 1], odd[:, :, 1], ALU.subtract).then_inc(stats_step, 1)
            dve.tensor_tensor(s[:, 1, :], even[:, :, 1], odd[:, :, 1], ALU.add).then_inc(stats_step, 1)
            dve.tensor_tensor(s[:, 2, :], even[:, :, 2], odd[:, :, 2], ALU.add).then_inc(stats_step, 1)
            dve.wait_ge(stats_step, done + 3)
            dve.tensor_scalar(m, s[:, 1, :], 0.5, None, ALU.mult).then_inc(stats_step, 1)
            dve.scalar_tensor_tensor(s[:, 0, :], s[:, 0, :], 0.25, s[:, 0, :], ALU.mult, ALU.mult
                                     ).then_inc(stats_step, 1)
            dve.wait_ge(stats_step, done + 5)
            dve.scalar_tensor_tensor(v, s[:, 2, :], 1.0 / D, s[:, 0, :], ALU.mult, ALU.add).then_inc(stats_step, 1)
            dve.wait_ge(stats_step, done + 6)
            dve.tensor_scalar(v, v, LN_EPS, None, ALU.add).then_inc(stats_step, 1)
            dve.tensor_scalar(mm, s[:, 1, :], -0.5, None, ALU.mult).then_inc(stats_step, 1)

        STATS_STEPS = 8

        def join_tiles(dve, stats_step, done, lo, hi):
            join_stats(dve, stats_step, done, bns[:, lo:hi], mean[:, lo:hi], minus_mean[:, lo:hi], st[:, :, lo:hi], veps[:, lo:hi])

        def rstd_tiles(pool, rstd_ready, lo, hi):
            pool.tensor_tensor(rstd[:, lo:hi], veps[:, lo:hi], neg_half[:, lo:hi], ALU.pow).then_inc(rstd_ready, 1)

        x_dram = x.rearrange("b t d -> t b d")
        out_dram = out.rearrange("b t d -> t b d")

        kbd = sb("kbd", [P, 2, H * S2])
        vbd = sb("vbd", [P, 2, (CM + RG) * 32])
        pr = sb("pr", [P, 2, COLS])
        pT = sb("pT", [P, COLS])
        work = sb("work", [P, 4, 2, D])
        xn, xnT, qT, tmp = (work[:, i] for i in range(4))
        oT = sb("oT", [P, 2, P])
        rT = sb("rT", [P, 2, P])
        mx = sb("mx", [P, 2, H])
        smm = sb("smm", [P, 2, H])
        smr = sb("smr", [P, 2, H])
        sm = sb("sm", [P, 2, H])
        rc = sb("rc", [P, 2, H])
        rx = sb("rx", [P, 2, P])

        def attention(layer, experts_rstd=None):
            def s_(name):
                return sem(f"{name}{layer}")

            xn_ready = s_("xn_ready")
            bias_added = s_("bias_added")
            xnT_done = s_("xnT_done")
            xnT_ready = s_("xnT_ready")
            q_done = s_("q_done")
            q_ready = s_("q_ready")
            kbd_ready = s_("kbd_ready")
            vbd_ready = s_("vbd_ready")
            scored = s_("scored")
            max_ready = s_("max_ready")
            shifted = s_("shifted")
            exp_done = s_("exp_done")
            part_sum = s_("part_sum")
            sum_ready = s_("sum_ready")
            recip_ready = s_("recip_ready")
            rx_ready = s_("rx_ready")
            rT_done = s_("rT_done")
            rT_ready = s_("rT_ready")
            pT_done = s_("pT_done")
            pT_ready = s_("pT_ready")
            pv_done = s_("pv_done")
            oT_ready = s_("oT_ready")
            out_done = s_("out_done")
            out_read = s_("out_read")
            out_scaled = s_("out_scaled")
            res_done = s_("res_done")
            stats = s_("stats")
            stats_step = s_("stats_step")
            rstd_ready = s_("rstd_ready")

            tile_xs = xs[:].rearrange("p (g u) d -> p g u d", u=2)
            tile_shift = shift[:].rearrange("p (g u) -> p g u", u=2)
            tile_bns = bns[:].rearrange("p (g u) a s -> p g u (a s)", u=2)
            tile_rstd = rstd[:].rearrange("p (g u) -> p g u", u=2)
            tile_rstd_valid = rstd_valid[:].rearrange("p (g u) -> p g u", u=2)
            tile_kT = kT[:, layer].rearrange("p (g u) k -> p g u k", u=2)
            tile_vc = vc[:].rearrange("p (g u) a l d -> p g u a l d", u=2)

            xn_ps, rT_ps = bank[0][:, 0:P], bank[0][:, P:2 * P]
            o_ps, out_ps = bank[1][:, 0:P], bank[1][:, P:2 * P]
            q_ps = xn_ps if layer == 0 else rT_ps
            GROUPS = [(bank[2], 0, range(0, CM, 2)), (bank[3], 0, range(1, CM, 2)), (bank[0], 2 * P, range(CM, CH))]
            def t_after(t, n):
                return not isinstance(t, int) or t >= n

            sc = scores_ps[:].rearrange("p (g c) -> p g c", g=RG)[:, :, 0:HG * S2].rearrange(
                "p g (h k) -> p g h k", h=HG)

            def pr_main(u):
                return pr[:, u, 0:MAIN].rearrange("p (g h k) -> p g h k", g=RG, h=HG)

            def pr_rest(u):
                return pr[:, u, MAIN:COLS].rearrange("p (g h k) -> p g h k", g=RG, h=HG)[:, :, :, 0:NR]

            def parts(u):
                return pr_rest(u), pr_main(u)[:, 0:RG // 2], pr_main(u)[:, RG // 2:RG]

            def score_parts():
                return sc[:, :, :, KM:S2], sc[:, 0:RG // 2, :, 0:KM], sc[:, RG // 2:RG, :, 0:KM]

            def max_parts(u):
                m = mx[:, u, :].rearrange("p (g h) -> p g h", g=RG)
                return m, m[:, 0:RG // 2], m[:, RG // 2:RG]

            def slots(eng, body, after):
                for t in range(4):
                    body(t // 2, t % 2, t)
                with eng.Fori(2, B // 2 - 1) as g:
                    for u in range(2):
                        body(g, u, 2 * g + u)
                for t in range(B - 2, B + 3):
                    body(t // 2, t % 2, t)
                    after(t)

            def stage(t, k):
                return not isinstance(t, int) or k <= t < B + k

            def build_keys(pool, g, u):
                pool.tensor_tensor(
                    kbd[:, u, :].rearrange("p (h k) -> p h k", h=H),
                    tile_kT[:, g, u, :].unsqueeze(1).to_broadcast([P, H, S2]),
                    head_mask[:].unsqueeze(2).to_broadcast([P, H, S2]), ALU.mult).then_inc(kbd_ready, 1)

            def build_values(pool, g, u):
                v = tile_vc[:, g, u, :, layer, :]
                pool.tensor_tensor(
                    vbd[:, u, 0:CM * 32].rearrange("p (j a w) -> p j a w", j=RG, w=2 * DH)[:, :, 0:4:3, :],
                    v[:, 0, :].rearrange("p (j a w) -> p j a w", j=RG, w=2 * DH),
                    main_mask[:].unsqueeze(1).unsqueeze(1).to_broadcast([P, RG, 2, 2 * DH]), ALU.mult
                ).then_inc(vbd_ready, 1)
                pool.tensor_tensor(
                    vbd[:, u, CM * 32:(CM + RG) * 32].rearrange("p (c h d) -> p c h d", c=2, h=8),
                    v[:, 1, :].rearrange("p (c h d) -> p c h d", c=2, h=8),
                    rest_mask[:].unsqueeze(1).unsqueeze(3).to_broadcast([P, 2, 8, DH]), ALU.mult
                ).then_inc(vbd_ready, 1)

            def build_first_keys(pool):
                for u in range(2):
                    build_keys(pool, 0, u)

            def build_first_values(pool):
                for u in range(2):
                    build_values(pool, 0, u)

            def gpsimd(pool, meanwhile, at_end):
                def spread(u, t):
                    pool.wait_ge(recip_ready, t - 1)
                    if t_after(t, 4):
                        pool.wait_ge(rT_done if layer == 0 else out_scaled, t - 3)
                    scale = ones_col[:, 0:1] if layer == 0 else tg[:, 1:2]
                    pool.tensor_tensor(rx[:, u, :].rearrange("p (h d) -> p h d", h=H),
                                       rc[:, u, :].unsqueeze(2).to_broadcast([P, H, DH]),
                                       scale.unsqueeze(2).to_broadcast([P, H, DH]), ALU.mult).then_inc(rx_ready, 1)

                def body(g, u, t):
                    if stage(t, 3):
                        xt = tile_xs[:, g - 2 + u, 1 - u, :]
                        pool.wait_ge(out_read, t - 2)
                        if layer == 0:
                            pool.wait_ge(bias_added, t - 2)
                        else:
                            pool.wait_ge(rx_ready, t - 2)
                            pool.tensor_tensor(tmp[:, 1 - u, :], tmp[:, 1 - u, :], rx[:, 1 - u, :],
                                               ALU.mult).then_inc(out_scaled, 1)
                            pool.wait_ge(out_scaled, t - 2)
                        pool.tensor_tensor(xt, xt, tmp[:, 1 - u, :], ALU.add).then_inc(res_done, 1)
                    if stage(t, 2) and layer == 0:
                        spread(u, t)
                    if stage(t, 0):
                        if layer == 0:
                            pool.wait_ge(xn_ready, t + 1)
                            pool.tensor_tensor(tile_xs[:, g, u, :], tile_xs[:, g, u, :], bias_bc[:],
                                               ALU.add).then_inc(bias_added, 1)
                        if stage(t, 2):
                            pool.wait_ge(pv_done, t - 1)
                            build_values(pool, g, u)
                    if stage(t, 1) and stage(t, -1):
                        pool.wait_ge(scored, 2 * t)
                        build_keys(pool, g + u, 1 - u)
                    if stage(t, 2) and layer == 1:
                        spread(u, t)

                def after(t):
                    if t == B - 2:
                        pool.wait_ge(stats_step, STATS_STEPS)
                        rstd_tiles(pool, rstd_ready, 0, 4)
                    if t == B:
                        for lo in range(4, B - 4, 4):
                            rstd_tiles(pool, rstd_ready, lo, lo + 4)
                        meanwhile()

                slots(pool, body, after)
                at_end()
                pool.wait_ge(stats_step, 2 * STATS_STEPS)
                rstd_tiles(pool, rstd_ready, B - 4, B)

            def tensor(pe, before, scores_free, after):
                def transpose_chunks(u, n):
                    ps, c0, chunks = GROUPS[n]
                    for i, c in enumerate(chunks):
                        mm = pe.transpose(ps[:, c0 + P * i:c0 + P * i + P], pr[:, u, P * c:P * c + P], ident[:])
                    mm.then_inc(pT_done, 1)

                def body(g, u, t):
                    if stage(t, 0):
                        pe.wait_ge(xn_ready, t + 1)
                        if stage(t, 3):
                            pe.wait_ge(pT_ready, 3 * (t - 2))
                            if layer == 0:
                                pe.wait_ge(rT_ready, t - 2)
                        if stage(t, 1) and layer == 1:
                            pe.wait_ge(q_ready, t)
                        pe.transpose(xn_ps, xn[:, u, :], ident[:]).then_inc(xnT_done, 1)
                    if stage(t, 2):
                        pe.wait_ge(exp_done, 3 * (t - 1))
                        if stage(t, 3):
                            pe.wait_ge(pT_ready, 3 * (t - 2))
                        transpose_chunks(u, 0)
                    if stage(t, 0):
                        pe.wait_ge(xnT_ready, t + 1)
                        pe.matmul(q_ps, wq0_sb[:] if layer == 0 else wq1T[:], xnT[:, u, :],
                                  start=True, stop=True).then_inc(q_done, 1)
                    if stage(t, 2):
                        transpose_chunks(u, 1)
                        if layer == 1:
                            if stage(t, 0):
                                pe.wait_ge(q_ready, t + 1)
                            transpose_chunks(u, 2)
                        pe.wait_ge(vbd_ready, 2 * (t - 1))
                        if stage(t, 3):
                            pe.wait_ge(out_read, t - 2)
                        for n in range(3):
                            if n == 1 and layer == 0:
                                if stage(t, 0):
                                    pe.wait_ge(q_ready, t + 1)
                                else:
                                    pe.wait_ge(rT_ready, t - 2)
                                transpose_chunks(u, 2)
                            pe.wait_ge(pT_ready, 3 * (t - 2) + n + 1)
                            if n == 2 and layer == 0:
                                pe.wait_ge(rx_ready, t - 1)
                                pe.transpose(rT_ps, rx[:, u, :], ident[:]).then_inc(rT_done, 1)
                            for j in range(RG):
                                w = 2 * j + n if n < 2 else CM + j
                                c = 4 * n + j if n < 2 else CM + j // 2
                                mm = pe.matmul(o_ps[32 * j:32 * j + 32, :], vbd[:, u, 32 * w:32 * w + 32],
                                               pT[:, P * c:P * c + P], start=(n == 0), stop=(n == 2))
                        mm.then_inc(pv_done, 1)
                    if stage(t, 0):
                        pe.wait_ge(q_ready, t + 1)
                        pe.wait_ge(kbd_ready, t + 1)
                        if isinstance(t, int) and t == 0:
                            scores_free()
                        for r in range(RG):
                            if r % 2 == 0 and stage(t, 1):
                                pe.wait_ge(shifted, 3 * (t - 1) + 2 + r // 2)
                            mm = pe.matmul(scores_ps[:, 512 * r:512 * r + HG * S2], qT[:, u, :],
                                           kbd[:, u, HG * S2 * r:HG * S2 * (r + 1)], start=True, stop=True)
                            if r % 2 == 1:
                                mm.then_inc(scored, 1)
                    if stage(t, 2):
                        pe.wait_ge(oT_ready, t - 1)
                        if layer == 0:
                            pe.matmul(out_ps, oT[:, u, :], wo_tg[:], start=True, stop=True
                                      ).then_inc(out_done, 1)
                        else:
                            pe.transpose(out_ps, oT[:, u, :], ident[:]).then_inc(out_done, 1)

                before(pe)
                slots(pe, body, after)

            def normalise(act, g, u):
                factor = tile_rstd if layer == 0 else tile_rstd_valid
                act.activation(xn[:, u, :], tile_xs[:, g, u, :], ACT.Identity, bias=tile_shift[:, g, u:u + 1],
                               scale=factor[:, g, u:u + 1]).then_inc(xn_ready, 1)

            def scalar(act, before, after):
                def gather(t, n):
                    ps, c0, chunks = GROUPS[n]
                    act.wait_ge(pT_done, 3 * (t - 2) + n + 1)
                    act.copy(pT[:, 4 * P * n:4 * P * n + P * len(chunks)], ps[:, c0:c0 + P * len(chunks)]
                             ).then_inc(pT_ready, 1)

                def between(u, t):
                    if layer == 0:
                        act.wait_ge(rT_done, t - 1)
                        act.copy(rT[:, u, :], rT_ps).then_inc(rT_ready, 1)
                    else:
                        act.wait_ge(pv_done, t - 1)
                        act.copy(oT[:, u, :], o_ps).then_inc(oT_ready, 1)

                def body(g, u, t):
                    if stage(t, 0):
                        act.wait_ge(xnT_done, t + 1)
                        act.copy(xnT[:, u, :], xn_ps).then_inc(xnT_ready, 1)
                    if stage(t, 3):
                        act.wait_ge(out_done, t - 2)
                        if t_after(t, 5):
                            act.wait_ge(res_done, t - 4)
                        act.copy(tmp[:, 1 - u, :], out_ps).then_inc(out_read, 1)
                    if stage(t, 2):
                        if stage(t, 3):
                            act.wait_ge(pv_done, t - 2)
                        gather(t, 0)
                    if stage(t, 0):
                        act.wait_ge(q_done, t + 1)
                        act.activation(qT[:, u, :], q_ps, ACT.Identity,
                                       bias=bq_col[:] if layer == 0 else 0.0).then_inc(q_ready, 1)
                    if stage(t, 2):
                        gather(t, 1)
                        gather(t, 2)
                    if stage(t, 1):
                        for n, part in enumerate(parts(1 - u)):
                            act.wait_ge(shifted, 3 * (t - 1) + n + 1)
                            act.activation(part, part, ACT.Exp, scale=SCALE).then_inc(exp_done, 1)
                            if n == 1 and layer == 0 and stage(t, 2):
                                between(u, t)
                    if stage(t, 2) and not (layer == 0 and stage(t, 1)):
                        between(u, t)
                    if stage(t, -1) and stage(t, 0):
                        if layer == 1 and isinstance(t, int) and t == 3:
                            act.wait_ge(experts_rstd, NQ)
                        if stage(t, 1):
                            act.wait_ge(xnT_done, t)
                            act.wait_ge(scored, 1)
                        normalise(act, g + u, 1 - u)

                before(act)
                slots(act, body, after)

            def vector(dve, after):
                def max_half(t, v, half):
                    dve.wait_ge(scored, 2 * (t - 1) + half + 1)
                    dve.tensor_reduce(max_parts(v)[1 + half], sc[:, RG // 2 * half:RG // 2 * half + RG // 2],
                                      AX.X, ALU.max).then_inc(max_ready, 1)

                def statistics(g, u, t):
                    dve.wait_ge(res_done, t - 2)
                    dve.wait_ge(pT_ready, 3)
                    dve.bn_stats(tile_bns[:, g - 2 + u, 1 - u, :], tile_xs[:, g - 2 + u, 1 - u, :]
                                 ).then_inc(stats, 1)

                def body(g, u, t):
                    v = 1 - u
                    if stage(t, 1):
                        max_half(t, v, 0)
                    if stage(t, 2) and layer == 0:
                        dve.wait_ge(part_sum, 2 * (t - 1))
                        dve.tensor_tensor(sm[:, u, :], smm[:, u, :], smr[:, u, :], ALU.add).then_inc(sum_ready, 1)
                    if stage(t, 1):
                        max_half(t, v, 1)
                    if stage(t, 2) and layer == 1:
                        dve.wait_ge(part_sum, 2 * (t - 1))
                        dve.tensor_tensor(sm[:, u, :], smm[:, u, :], smr[:, u, :], ALU.add).then_inc(sum_ready, 1)
                    if stage(t, 2) and layer == 0:
                        dve.wait_ge(sum_ready, t - 1)
                        dve.reciprocal(rc[:, u, :], sm[:, u, :]).then_inc(recip_ready, 1)
                    if stage(t, 1):
                        dve.wait_ge(max_ready, 2 * t)
                        if stage(t, 3):
                            dve.wait_ge(pT_done, 3 * (t - 2))
                        for part, ps, m in zip(parts(v), score_parts(), max_parts(v)):
                            dve.tensor_tensor(part, ps, m.unsqueeze(3).to_broadcast(list(part.shape)),
                                              ALU.subtract).then_inc(shifted, 1)
                    if stage(t, 1):
                        dve.wait_ge(exp_done, 3 * (t - 1) + 1)
                        dve.tensor_reduce(smr[:, v, :].rearrange("p (g h) -> p g h", g=RG), pr_rest(v), AX.X,
                                          ALU.add).then_inc(part_sum, 1)
                    if stage(t, 2) and layer == 1:
                        dve.wait_ge(sum_ready, t - 1)
                        dve.reciprocal(rc[:, u, :], sm[:, u, :]).then_inc(recip_ready, 1)
                    if stage(t, 2) and layer == 0:
                        dve.wait_ge(pv_done, t - 1)
                        dve.wait_ge(rT_ready, t - 1)
                        dve.tensor_tensor(oT[:, u, :], o_ps, rT[:, u, :], ALU.mult).then_inc(oT_ready, 1)
                    if stage(t, 3):
                        statistics(g, u, t)
                    if stage(t, 1):
                        dve.wait_ge(exp_done, 3 * t)
                        dve.tensor_reduce(smm[:, v, :].rearrange("p (g h) -> p g h", g=RG), pr_main(v), AX.X,
                                          ALU.add).then_inc(part_sum, 1)

                def after_vector(t):
                    if t == B - 2:
                        dve.wait_ge(stats, B - 4)
                        join_tiles(dve, stats_step, 0, 0, B - 4)
                    after(t)

                slots(dve, body, after_vector)
                dve.wait_ge(stats, B)
                join_tiles(dve, stats_step, STATS_STEPS, B - 4, B)

            return dict(build_first_keys=build_first_keys, build_first_values=build_first_values,
                                   normalise=normalise, gpsimd=gpsimd, tensor=tensor, scalar=scalar, vector=vector,
                                   xnT_done=xnT_done, q_done=q_done, q_ready=q_ready, scored=scored, shifted=shifted,
                                   pT_ready=pT_ready, rT_ready=rT_ready, pv_done=pv_done, vbd_ready=vbd_ready, oT_ready=oT_ready,
                                   out_read=out_read, res_done=res_done, rstd_ready=rstd_ready)

        experts_rstd = sem("experts_rstd")
        att0, att1 = attention(0), attention(1, experts_rstd)

        with ExitStack() as su:
            yrep = sb("yrep", [DC, B, 2, P], stack=su)
            w1_sb = sb("w1_sb", [P, E, 4, P], stack=su)
            wk01 = sb("wk01", [DC, 2, D], stack=su)
            wv01 = sb("wv01", [DC, 2, D], stack=su)
            w2_sb = sb("w2_sb", [P, E, I], stack=su)
            wq1_sb = sb("wq1_sb", [P, D], stack=su)
            wkv_sb = sb("wkv_sb", [P, 2, DC], stack=su)
            ffn_sb = sb("ffn_sb", [P, 3, D], stack=su)
            router_sb = sb("router_sb", [E, D], stack=su)
            wo_sb = sb("wo_sb", [P, D], stack=su)
            bk_col = sb("bk_col", [P, 1], stack=su)
            bv_col = sb("bv_col", [P, 1], stack=su)
            bo_row = sb("bo_row", [1, D], stack=su)
            bo_tg = sb("bo_tg", [1, D], stack=su)
            ones_row = sb("ones_row", [1, P], stack=su)
            g_sb = sb("g_sb", [P, 4], stack=su)
            mask_u8 = sb("mask_u8", [B, P], U8, stack=su)
            yT = pr[0:DC, 0, 0:B * S2].rearrange("p (b k) -> p b k", b=B)
            mask_f = tmp[0:B, 0, :]
            bv_bc, ones_pp = rx[:, 0, :], rx[:, 1, :]
            y_sb = kbd[0:S2].rearrange("p u c -> p (u c)")[:, 0:B * DC].rearrange("p (b c) -> p b c", b=B)
            sel_f = pT[:, 0:E * P].rearrange("p (e t) -> p e t", e=E)

            y_loaded = sem("y_loaded", su)
            kv_loaded = sem("kv_loaded", su)
            small_loaded = sem("small_loaded", su)
            kv_T = sem("kv_T", su)
            kv_copied = sem("kv_copied", su)
            w_loaded = [sem(f"w_loaded{i}", su) for i in range(E // 2)]
            zeroed = sem("zeroed", su)
            ident_ready = sem("ident_ready", su)
            masks_step = sem("masks_step", su)
            yT_done = sem("yT_done", su)
            yT_copied = sem("yT_copied", su)
            yrep_ready = sem("yrep_ready", su)
            small_T = sem("small_T", su)
            tg_ready = sem("tg_ready", su)
            scaled = sem("scaled", su)
            mask_float = sem("mask_float", su)
            router_high = sem("router_high", su)
            k_done = sem("k_done", su)
            k_copied = sem("k_copied", su)
            v_done = sem("v_done", su)
            v_copied_act = sem("v_copied_act", su)
            v_copied_dve = sem("v_copied_dve", su)
            wT_done = sem("wT_done", su)
            wT_high = sem("wT_high", su)
            wT_low = sem("wT_low", su)
            stats = sem("stats", su)
            stats_step = sem("stats_step", su)
            setup_rstd = sem("setup_rstd", su)
            vbd_zeroed = sem("vbd_zeroed", su)
            bias_done = sem("bias_done", su)

            YG = [range(0, 6), range(6, 12), range(12, B)]
            WEIGHTS = 3 * E // 2
            LEAD = B - WEIGHTS
            kv_loads = (
                (wk01[:, 0, :], wk0), (wkv_sb[:], wkv1.rearrange("(l o) c -> o l c", l=2)), (wv01[:, 0, :], wv0),
                (bk_col[:], bk0.rearrange("(d o) -> d o", o=1)),
            )
            small_loads = (
                (g_sb[:, 0:2], g_xattn.partition_broadcast(P)), (g_sb[:, 2:4], g_ffn.partition_broadcast(P)),
                (mask_u8[:], mask_BxS_bk0), (wo_sb[:], wo0), (wq1_sb[:], wq1), (router_sb[:], router_w),
                (ffn_sb[:, 0, :], w_r), (ffn_sb[:, 1, :], w_k), (ffn_sb[:, 2, :], w_v), (wq0_sb[:], wq0),
                (bq_col[:], bq0.rearrange("(d o) -> d o", o=1)), (bv_col[:], bv0.rearrange("(d o) -> d o", o=1)),
                (bo_row[:], bo0.rearrange("(o d) -> o d", o=1)),
                (mus[:, 0:1], mu_r.rearrange("(d o) -> d o", o=1)), (mus[:, 1:2], mu_k.rearrange("(d o) -> d o", o=1)),
            )

            with nc.Block() as block:
                @block.sync
                def _(sp):
                    sp.dma_start(y_sb, ctx_768.rearrange("b k c -> k b c")).then_inc(y_loaded, 16)
                    for dst, src in kv_loads:
                        sp.dma_start(dst, src).then_inc(kv_loaded, 16)
                    for dst, src in small_loads:
                        sp.dma_start(dst, src).then_inc(small_loaded, 16)
                    for q in range(NQ):
                        sp.dma_start(xs[:, 4 * q:4 * q + 4, :], x_dram[:, 4 * q:4 * q + 4, :]).then_inc(x_loaded[q], 16)
                    for pair in range(E // 2):
                        es = slice(2 * pair, 2 * pair + 2)
                        sp.dma_start(w1_sb[:, es], w1[es].rearrange("e (k o) i -> o e k i", o=P)
                                     ).then_inc(w_loaded[pair], 16)
                        sp.dma_start(w2_sb[:, es], w2[es].rearrange("e h i -> h e i")).then_inc(w_loaded[pair], 16)

                @block.gpsimd
                def _(pool):
                    pool.memset(ident[:], 0.0).then_inc(zeroed, 1)
                    pool.memset(head_mask[:], 1.0).then_inc(zeroed, 1)
                    pool.memset(main_mask[:], 1.0).then_inc(zeroed, 1)
                    pool.memset(rest_mask[:], 1.0).then_inc(zeroed, 1)
                    pool.memset(yrep[:], 0.0).then_inc(zeroed, 1)
                    pool.memset(ones_pp, 1.0).then_inc(zeroed, 1)
                    pool.memset(ones_row[:], 1.0).then_inc(zeroed, 1)
                    pool.memset(neg_half[:], -0.5).then_inc(zeroed, 1)
                    pool.memset(routerh[:].bitcast(F32), 0.0).then_inc(zeroed, 1)
                    pool.memset(routerl[:].bitcast(F32), 0.0).then_inc(zeroed, 1)
                    pool.memset(tri[:], 1.0).then_inc(zeroed, 1)
                    pool.memset(sel_f, 0.0).then_inc(zeroed, 1)
                    pool.wait_ge(zeroed, 12)
                    pool.affine_select(out=ident[:], in_=ident[:], compare_op=ALU.not_equal, fill=1.0, base=0,
                                       pattern=[[-1, P]], channel_multiplier=1).then_inc(ident_ready, 1)
                    n = 0
                    for mask, step, pat in ((head_mask, DH, [[-DH, H]]), (main_mask, P // 2, [[-P // 2, 2], [0, DH]]),
                                            (rest_mask, KR, [[-KR, 8]])):
                        pool.affine_select(out=mask[:], in_=mask[:], compare_op=ALU.is_ge, fill=0.0, base=0,
                                           pattern=pat, channel_multiplier=1).then_inc(masks_step, 1)
                        n += 1
                        pool.wait_ge(masks_step, n)
                        pool.affine_select(out=mask[:], in_=mask[:], compare_op=ALU.is_ge, fill=0.0, base=step - 1,
                                           pattern=[[-s, c] for s, c in pat], channel_multiplier=-1
                                           ).then_inc(masks_step, 1)
                        n += 1
                    pool.affine_select(out=tri[:], in_=tri[:], compare_op=ALU.is_gt, fill=0.0, base=0,
                                       pattern=[[1, E], [-1, E]], channel_multiplier=0)
                    for base in (0, -E):
                        pool.affine_select(out=sel_f, in_=sel_f, compare_op=ALU.not_equal, fill=1.0, base=base,
                                           pattern=[[-1, E], [0, P]], channel_multiplier=1).then_inc(masks_step, 1)
                        n += 1
                        pool.wait_ge(masks_step, n)
                    pool.tensor_copy(sel[:], sel_f)
                    pool.memset(combT[:].bitcast(F32), 0.0)
                    pool.memset(vbd[:], 0.0).then_inc(vbd_zeroed, 1)
                    pool.wait_ge(yrep_ready, 2)
                    pool.wait_ge(k_done, 6)
                    pool.memset(pr[:], 0.0)
                    pool.wait_ge(stats_step, STATS_STEPS)
                    rstd_tiles(pool, setup_rstd, 0, B)
                    pool.wait_ge(setup_rstd, 1)
                    pool.tensor_tensor(shift[:], minus_mean[:], rstd[:], ALU.mult)
                    pool.memset(ones_col[:], 1.0)
                    pool.wait_ge(k_copied, 6)
                    pool.wait_ge(v_copied_act, 1)
                    pool.wait_ge(v_copied_dve, 1)
                    pool.wait_ge(vbd_zeroed, 1)
                    att0["build_first_keys"](pool)
                    att0["build_first_values"](pool)

                @block.tensor
                def _(pe):
                    def values(b):
                        if b >= 2:
                            pe.wait_ge(v_copied_dve if b % 2 else v_copied_act, b // 2)
                        for part in range(2):
                            mm = pe.matmul(pbank(b % 2)[:, 256 * part:256 * part + 256], yrep[:, b, part, :],
                                           wv01[:], start=True, stop=True)
                        mm.then_inc(v_done, 1)

                    def expert_weights(n):
                        pair, g = n // 3, n % 3
                        pe.wait_ge(w_loaded[pair], 32)
                        if n >= 3:
                            pe.wait_ge(wT_low, n - 2)
                        else:
                            pe.wait_ge(k_copied, 6)
                        for i in range(4):
                            src = (w1_sb[:, 2 * pair + g, i, :] if g < 2 else
                                   w2_sb[:, 2 * pair + i // 2, P * (i % 2):P * (i % 2) + P])
                            mm = pe.transpose(pbank(5 + n % 3)[:, P * i:P * i + P], src, ident[:])
                        mm.then_inc(wT_done, 1)

                    pe.wait_ge(ident_ready, 1)
                    pe.wait_ge(y_loaded, 16)
                    for n, group in enumerate(YG):
                        for i, b in enumerate(group):
                            mm = pe.transpose(pbank(n)[0:DC, i * S2:(i + 1) * S2], y_sb[:, b, :], ident[0:S2, 0:S2])
                        mm.then_inc(yT_done, 1)
                    pe.wait_ge(kv_loaded, 16 * len(kv_loads))
                    for i in range(2):
                        mm = pe.transpose(pbank(3)[0:DC, 128 * i:128 + 128 * i], wkv_sb[:, i, :], ident[:])
                    mm.then_inc(kv_T, 1)
                    n = 0
                    for layer in range(2):
                        if layer == 1:
                            pe.wait_ge(kv_copied, 2)
                        for i, group in enumerate(YG):
                            pe.wait_ge(yT_copied, i + 1)
                            if n >= 3:
                                pe.wait_ge(k_copied, n - 2)
                            w = len(group) * S2
                            pe.matmul(pbank(5 + n % 3)[:, 0:w], wk01[:, layer, :],
                                      yT[:, group[0]:group[-1] + 1, :], start=True, stop=True).then_inc(k_done, 1)
                            n += 1
                    pe.wait_ge(yrep_ready, 2)
                    for b in range(B):
                        values(b)
                        if b == 1:
                            pe.wait_ge(small_loaded, 16 * len(small_loads))
                            pe.wait_ge(mask_float, 1)
                            pe.transpose(pbank(4)[:, 0:128], wq1_sb[:], ident[:])
                            pe.transpose(pbank(4)[:, 384:384 + B], mask_f, ident[0:B, 0:B])
                            pe.transpose(pbank(4)[:, 400:400 + E], router_sb[:], ident[0:E, 0:E]).then_inc(small_T, 1)
                            for i in range(3):
                                mm = pe.transpose(pbank(2)[:, 128 * i:128 * i + 128], ffn_sb[:, i, :], ident[:])
                            mm.then_inc(small_T, 1)
                        if b == 2:
                            pe.wait_ge(scaled, 3)
                            pe.matmul(pbank(3)[:, 0:D], bv_bc, wo_tg[:], start=True, stop=False)
                            pe.matmul(pbank(3)[:, 0:D], ones_row[:], bo_tg[:], start=False, stop=True
                                      ).then_inc(bias_done, 1)
                        if b >= LEAD:
                            expert_weights(b - LEAD)

                @block.scalar
                def _(act):
                    for n, group in enumerate(YG):
                        act.wait_ge(yT_done, n + 1)
                        act.copy(yT[:, group[0]:group[-1] + 1, :],
                                 pbank(n)[0:DC, 0:len(group) * S2]).then_inc(yT_copied, 1)
                    act.wait_ge(kv_T, 1)
                    act.copy(wk01[:, 1, :], pbank(3)[0:DC, 0:128]).then_inc(kv_copied, 1)
                    act.copy(wv01[:, 1, :], pbank(3)[0:DC, 128:256]).then_inc(kv_copied, 1)
                    n = 0
                    for layer in range(2):
                        for group in YG:
                            act.wait_ge(k_done, n + 1)
                            act.activation(kT[:, layer, group[0]:group[-1] + 1, :],
                                           pbank(5 + n % 3)[:, 0:len(group) * S2], ACT.Identity,
                                           bias=bk_col[:] if layer == 0 else 0.0).then_inc(k_copied, 1)
                            n += 1
                        if layer == 0:
                            act.wait_ge(small_loaded, 16 * len(small_loads))
                            act.activation(tg[:], g_sb[:], ACT.Tanh).then_inc(tg_ready, 1)
                    for b in range(B):
                        if b % 2 == 0:
                            act.wait_ge(v_done, b + 1)
                            act.copy(vc[:, b].rearrange("p a l d -> p (a l d)"), pbank(0)).then_inc(v_copied_act, 1)
                        if b == 1:
                            act.wait_ge(small_T, 1)
                            act.copy(wq1T[:], pbank(4)[:, 0:128])
                            act.copy(valid[:], pbank(4)[:, 384:384 + B])
                            act.wait_ge(zeroed, 12)
                            act.copy(routerh[:, 0:E], pbank(4)[:, 400:400 + E]).then_inc(router_high, 1)
                            act.wait_ge(small_T, 2)
                            act.copy(w_rT[:], pbank(2)[:, 0:128])
                            act.copy(w_kT[:], pbank(2)[:, 128:256])
                            act.copy(w_vT[:], pbank(2)[:, 256:384])
                        if b == 2:
                            act.wait_ge(bias_done, 1)
                            act.copy(bias_bc[:], pbank(3)[:, 0:D])
                        if b >= LEAD:
                            n = b - LEAD
                            pair, g = n // 3, n % 3
                            act.wait_ge(wT_done, n + 1)
                            act.copy(w1h[:, 2 * pair + g, :] if g < 2 else
                                     w2h[:, 2 * pair:2 * pair + 2].rearrange("p e k d -> p (e k d)"),
                                     pbank(5 + n % 3)).then_inc(wT_high, 1)

                @block.vector
                def _(dve):
                    dve.wait_ge(zeroed, 12)
                    dve.wait_ge(yT_copied, 3)
                    dve.tensor_copy(yrep[:, :, 0, :].rearrange("c b (r k) -> c b r k", r=2),
                                    yT[:, :, 0:KM].unsqueeze(2).to_broadcast([DC, B, 2, KM])).then_inc(yrep_ready, 1)
                    dve.tensor_copy(yrep[:, :, 1, :].rearrange("c b (r k) -> c b r k", r=8)[:, :, :, 0:NR],
                                    yT[:, :, KM:S2].unsqueeze(2).to_broadcast([DC, B, 8, NR])).then_inc(yrep_ready, 1)
                    dve.wait_ge(small_loaded, 16 * len(small_loads))
                    dve.tensor_copy(mask_f, mask_u8[:]).then_inc(mask_float, 1)
                    dve.tensor_scalar(mus[:, 2:4], mus[:, 0:2], -1.0, 1.0, ALU.mult, ALU.add)
                    dve.wait_ge(tg_ready, 1)
                    dve.tensor_scalar(wo_tg[:], wo_sb[:], tg[:, 0:1], None, ALU.mult).then_inc(scaled, 1)
                    dve.tensor_scalar(bo_tg[:], bo_row[:], tg[0:1, 0:1], None, ALU.mult).then_inc(scaled, 1)
                    dve.tensor_scalar(bv_bc, ones_pp, bv_col[:, 0:1], None, ALU.mult).then_inc(scaled, 1)
                    for b in range(B):
                        if b % 2:
                            dve.wait_ge(v_done, b + 1)
                            dve.tensor_copy(vc[:, b].rearrange("p a l d -> p (a l d)"),
                                            pbank(1)).then_inc(v_copied_dve, 1)
                        if b == 1:
                            dve.wait_ge(router_high, 1)
                            dve.tensor_tensor(routerl[:, 0:E], pbank(4)[:, 400:400 + E], routerh[:, 0:E].bitcast(F32),
                                              ALU.subtract)
                        if b % 2 == 0 and b // 2 < NQ:
                            dve.wait_ge(x_loaded[b // 2], 16)
                            for i in range(2 * b, 2 * b + 4):
                                dve.bn_stats(bns[:, i].rearrange("p a s -> p (a s)"), xs[:, i, :]).then_inc(stats, 1)
                        if b == 2 * NQ:
                            dve.wait_ge(stats, B)
                            join_tiles(dve, stats_step, 0, 0, B)
                        if b >= LEAD:
                            n = b - LEAD
                            pair, g = n // 3, n % 3
                            dve.wait_ge(wT_high, n + 1)
                            hi, lo = ((w1h[:, 2 * pair + g, :], w1l[:, 2 * pair + g, :]) if g < 2 else
                                      [w[:, 2 * pair:2 * pair + 2].rearrange("p e k d -> p (e k d)")
                                       for w in (w2h, w2l)])
                            dve.tensor_tensor(lo, pbank(5 + n % 3), hi.bitcast(F32), ALU.subtract).then_inc(wT_low, 1)

        UNITS = 2 * E
        LAG = 3
        HEAD = 6
        xm = work[:, 0:2].rearrange("p k u d -> p (k u) d")
        om = work[:, 2:4].rearrange("p k u d -> p (k u d)")
        sg = pT[:, 0:1024].rearrange("p (u n) -> p u n", u=2)
        xTh = sb("xTh", [P, NQ, 512], F32R)
        xTl = sb("xTl", [P, NQ, 512], F32R)
        lgT = sb("lgT", [P, 512])
        lg = sb("lg", [P, 4, E])
        lm = sb("lm", [P, 4])
        ex = sb("ex", [P, 4, E])
        ep = sb("ep", [P, 4, E])
        en = sb("en", [P, 4, E])
        es = sb("es", [P, 4])
        er = sb("er", [P, 4])
        gt = sb("gt", [P, 4, E, E])
        ge = sb("ge", [P, 4, E, E])
        rank = sb("rank", [P, 4, E])
        comb = sb("comb", [P, 4, E])
        comb2 = sb("comb2", [P, 4, 2 * E])
        au = sb("au", [P, 2, 512])
        yv = sb("yv", [P, 2, 512])
        yh = sb("yh", [P, 4, 512], F32R)
        yl = sb("yl", [P, 4, 512], F32R)

        def experts():
            xn_ready = sem("m_xn_ready")
            xT_done = sem("m_xT_done")
            xT_high = sem("m_xT_high")
            xT_low = sem("m_xT_low")
            lgT_done = sem("m_lgT_done")
            lgT_ready = sem("m_lgT_ready")
            routed = sem("m_routed")
            route_step = sem("m_route_step")
            tanh_ready = sem("m_tanh_ready")
            comb_ready = sem("m_comb_ready")
            combT_done = sem("m_combT_done")
            combT_ready = sem("m_combT_ready")
            h_done = sem("m_h_done")
            silu_done = sem("m_silu_done")
            up_done = sem("m_up_done")
            weight_spread = sem("m_weight_spread")
            y_done = sem("m_y_done")
            y_high = sem("m_y_high")
            y_low = sem("m_y_low")
            down_done = sem("m_down_done")
            oT_ready = sem("m_oT_ready")
            o_done = sem("m_o_done")
            res_done = sem("m_res_done")
            stats = sem("m_stats")
            stats_step = sem("m_stats_step")
            powered = sem("m_powered")

            STEPS = 18
            PIECES = [range(0, 1), range(1, 8), range(8, 10), range(0)]
            cb_ps, row_ps, mo_ps, col_ps = pbank(4), pbank(5), pbank(6), pbank(7)
            q_xs = xs[:].rearrange("p (q i) d -> p q i d", i=4)
            q_mean = mean[:].rearrange("p (q i) -> p q i", i=4)
            q_minus_mean = minus_mean[:].rearrange("p (q i) -> p q i", i=4)
            q_shift = shift[:].rearrange("p (q i) -> p q i", i=4)
            q_veps = veps[:].rearrange("p (q i) -> p q i", i=4)
            q_st = st[:].rearrange("p s (q i) -> p q s i", i=4)
            q_valid = valid[:].rearrange("p (q i) -> p q i", i=4)
            q_rstd_valid = rstd_valid[:].rearrange("p (q i) -> p q i", i=4)
            q_rstd = rstd[:].rearrange("p (q i) -> p q i", i=4)
            q_bns = bns[:].rearrange("p (q i) a s -> p q i a s", i=4)

            def gate_ps(j):
                return pbank(2 - 2 * (j % 2))

            def up_ps(j):
                return pbank(3 - 2 * (j % 2))

            def program(eng, unit, prepare, finish, meanwhile=lambda: None):
                for j in range(HEAD):
                    unit(0, j, j)
                with eng.Fori(0, NQ - 1) as q:
                    for j in range(HEAD, UNITS):
                        unit(q, j, q * UNITS + j)
                        prepare(q + 1, j - HEAD)
                    for j in range(HEAD):
                        unit(q + 1, j, q * UNITS + UNITS + j)
                        finish(q, j)
                for j in range(HEAD, UNITS):
                    unit(NQ - 1, j, (NQ - 1) * UNITS + j)
                meanwhile()
                for j in range(HEAD):
                    finish(NQ - 1, j)

            def prepare_first(prepare, t):
                if t >= B - 1:
                    for piece in PIECES[t - B + 1]:
                        prepare(0, piece)

            def tensor(pe):
                def inner(q, j, n):
                    e, half = j // 2, j % 2
                    if not (isinstance(n, int) and n < 2):
                        pe.wait_ge(up_done, n - 1)
                    elif n == 0:
                        pe.wait_ge(att0["pT_ready"], 3 * B)
                    else:
                        pe.wait_ge(att0["rT_ready"], B)
                        pe.wait_ge(att0["oT_ready"], B)
                        pe.wait_ge(att0["out_read"], B)
                    if j == 0:
                        pe.wait_ge(xT_low, q + 1)
                    for ps, off in ((gate_ps(j), half * P), (up_ps(j), I + half * P)):
                        wh, wl = w1h[:, e, off:off + P], w1l[:, e, off:off + P]
                        pe.matmul(ps, wl, xTh[:, q, :], start=True, stop=False)
                        pe.matmul(ps, wh, xTl[:, q, :], start=False, stop=False)
                        mm = pe.matmul(ps, wh, xTh[:, q, :], start=False, stop=True)
                    mm.then_inc(h_done, 1)

                def spread(q, j, n):
                    if not (isinstance(n, int) and n < 2):
                        pe.wait_ge(y_done, n)
                    if j == 0:
                        pe.wait_ge(combT_ready, q + 1)
                    pe.matmul(cb_ps, sel[:, j // 2, :], combT[:, q, :], start=True, stop=True
                              ).then_inc(weight_spread, 1)

                def outer(q, j, n):
                    e, half, u = j // 2, j % 2, j % 4
                    pe.wait_ge(y_low, n + 1)
                    if j == 0 and not (isinstance(q, int) and q == 0):
                        pe.wait_ge(oT_ready, q)
                    pe.matmul(mo_ps, w2l[:, e, half, :], yh[:, u, :], start=(j == 0), stop=False)
                    pe.matmul(mo_ps, w2h[:, e, half, :], yl[:, u, :], start=False, stop=False)
                    pe.matmul(mo_ps, w2h[:, e, half, :], yh[:, u, :], start=False, stop=(j == UNITS - 1)
                              ).then_inc(down_done, 1)

                def unit(q, j, n):
                    inner(q, j, n)
                    if j >= LAG:
                        outer(q, j - LAG, n - LAG)
                    elif not isinstance(n, int):
                        outer(q - 1, j - LAG + UNITS, n - LAG)
                    if j % 2 == 0:
                        spread(q, j, n)

                def prepare(g, piece):
                    if piece == 1:
                        if isinstance(g, int):
                            pe.wait_ge(att0["shifted"], 3 * B)
                        pe.wait_ge(xn_ready, 4 * g + 4)
                        if not isinstance(g, int):
                            pe.wait_ge(res_done, g - 1)
                        for i in range(4):
                            mm = pe.transpose(col_ps[:, P * i:P * i + P], xm[:, i, :], ident[:])
                        mm.then_inc(xT_done, 1)
                    if piece == 3:
                        pe.wait_ge(xT_low, g + 1)
                        if not isinstance(g, int):
                            pe.wait_ge(combT_ready, g)
                        pe.matmul(row_ps, routerl[:], xTh[:, g, :], start=True, stop=False)
                        pe.matmul(row_ps, routerh[:], xTl[:, g, :], start=False, stop=False)
                        pe.matmul(row_ps, routerh[:], xTh[:, g, :], start=False, stop=True
                                  ).then_inc(lgT_done, 1)
                    if piece == 4:
                        pe.wait_ge(lgT_ready, g + 1)
                        for i in range(4):
                            mm = pe.transpose(col_ps[:, P * i:P * i + P], lgT[:, P * i:P * i + P], ident[:])
                        mm.then_inc(routed, 1)
                    if piece == 9:
                        pe.wait_ge(comb_ready, g + 1)
                        for i in range(4):
                            mm = pe.transpose(row_ps[0:2 * E, P * i:P * i + P], comb2[:, i, :], ident[:])
                        mm.then_inc(combT_done, 1)

                def finish(q, j):
                    if isinstance(q, int) and j < LAG:
                        outer(q, UNITS - LAG + j, q * UNITS + UNITS - LAG + j)
                    if j == 3:
                        pe.wait_ge(oT_ready, q + 1)
                        pe.wait_ge(route_step, STEPS * q + STEPS)
                        for i in range(4):
                            mm = pe.transpose(col_ps[:, P * i:P * i + P], om[:, P * i:P * i + P], ident[:])
                        mm.then_inc(o_done, 1)

                def run():
                    program(pe, unit, prepare, finish)

                return lambda t: prepare_first(prepare, t), run

            def scalar(act):
                def high(j, n):
                    act.wait_ge(y_done, n + 1)
                    if not (isinstance(n, int) and n < 4):
                        act.wait_ge(down_done, n - 3)
                    act.copy(yh[:, j % 4, :], yv[:, j % 2, :]).then_inc(y_high, 1)

                def unit(q, j, n):
                    act.wait_ge(h_done, n + 1)
                    act.activation(sg[:, j % 2, :], gate_ps(j), ACT.Silu).then_inc(silu_done, 1)
                    if not (isinstance(n, int) and n == 0):
                        high((j - 1) % UNITS, n - 1)

                def prepare(g, piece):
                    if piece == 1:
                        act.wait_ge(xT_done, g + 1)
                        act.copy(xTh[:, g, :], col_ps).then_inc(xT_high, 1)
                    if piece == 3:
                        act.wait_ge(lgT_done, g + 1)
                        act.copy(lgT[:], row_ps).then_inc(lgT_ready, 1)
                    if piece == 5:
                        act.wait_ge(route_step, STEPS * g + 4)
                        act.activation(ex[:], ex[:], ACT.Tanh, scale=0.5).then_inc(tanh_ready, 1)
                        if isinstance(g, int):
                            load_functions(act, ACT.Silu)
                    if piece == 9:
                        act.wait_ge(combT_done, g + 1)
                        act.copy(combT[0:2 * E, g, :], row_ps[0:2 * E, :]).then_inc(combT_ready, 1)

                def finish(q, j):
                    if isinstance(q, int) and j == 0:
                        high(UNITS - 1, q * UNITS + UNITS - 1)
                    if j == 2:
                        act.wait_ge(down_done, q * UNITS + UNITS)
                        act.copy(om, mo_ps).then_inc(oT_ready, 1)

                def run(meanwhile):
                    act.wait_ge(att0["pv_done"], B)
                    program(act, unit, prepare, finish, meanwhile)

                return lambda t: prepare_first(prepare, t), run

            def gpsimd(pool):
                def unit(q, j, n):
                    pool.wait_ge(y_high, n + 1)
                    pool.tensor_tensor(yl[:, j % 4, :], yv[:, j % 2, :], yh[:, j % 4, :].bitcast(F32),
                                       ALU.subtract).then_inc(y_low, 1)

                def prepare(g, piece):
                    pass

                def finish(q, j):
                    if j == 5:
                        pool.wait_ge(stats_step, STATS_STEPS * q + STATS_STEPS)
                        pool.tensor_tensor(q_rstd[:, q, :], q_veps[:, q, :], neg_half[:, 0:4], ALU.pow
                                           ).then_inc(powered, 1)
                        pool.wait_ge(powered, 2 * q + 1)
                        pool.tensor_tensor(q_rstd_valid[:, q, :], q_rstd[:, q, :], q_valid[:, q, :], ALU.mult
                                           ).then_inc(powered, 1)
                        pool.wait_ge(powered, 2 * q + 2)
                        pool.tensor_tensor(q_shift[:, q, :], q_minus_mean[:, q, :], q_rstd_valid[:, q, :], ALU.mult
                                           ).then_inc(experts_rstd, 1)

                program(pool, unit, prepare, finish)

            def vector(dve):
                def weigh(q, j, n):
                    dve.wait_ge(up_done, n + 1)
                    dve.wait_ge(weight_spread, q * E + j // 2 + 1)
                    if not (isinstance(n, int) and n < 2):
                        dve.wait_ge(y_low, n - 1)
                    dve.tensor_tensor(yv[:, j % 2, :], au[:, j % 2, :], cb_ps, ALU.mult).then_inc(y_done, 1)

                def unit(q, j, n):
                    if j > 0:
                        weigh(q, j - 1, n - 1)
                    elif not isinstance(n, int):
                        weigh(q - 1, UNITS - 1, n - 1)
                    dve.wait_ge(silu_done, n + 1)
                    dve.tensor_tensor(au[:, j % 2, :], sg[:, j % 2, :], up_ps(j), ALU.mult).then_inc(up_done, 1)

                def prepare(g, piece):
                    def step(ins):
                        ins.then_inc(route_step, 1)

                    def done(k):
                        dve.wait_ge(route_step, STEPS * g + k)

                    mine = lg[:].unsqueeze(3).to_broadcast([P, 4, E, E])
                    other = lg[:].unsqueeze(2).to_broadcast([P, 4, E, E])
                    if piece == 0:
                        if isinstance(g, int):
                            dve.wait_ge(att0["q_done"], B)
                        dve.wait_ge(att0["rstd_ready"], g + 1)
                        for i in range(4):
                            dve.tensor_scalar(xm[:, i, :], q_xs[:, g, i, :], q_mean[:, g, i:i + 1],
                                              q_rstd[:, g, i:i + 1], ALU.subtract, ALU.mult).then_inc(xn_ready, 1)
                    if piece == 2:
                        dve.wait_ge(xT_high, g + 1)
                        dve.tensor_tensor(xTl[:, g, :], col_ps, xTh[:, g, :].bitcast(F32), ALU.subtract
                                          ).then_inc(xT_low, 1)
                    if piece == 5:
                        dve.wait_ge(routed, g + 1)
                        step(dve.tensor_copy(lg[:], col_ps.rearrange("p (i e) -> p i e", i=4)[:, :, 0:E]))
                        done(1)
                        step(dve.tensor_reduce(lm[:], lg[:], AX.X, ALU.max))
                        step(dve.tensor_tensor(gt[:], other, mine, ALU.is_gt))
                        done(2)
                        step(dve.tensor_tensor(ex[:], lg[:], lm[:].unsqueeze(2).to_broadcast([P, 4, E]),
                                               ALU.subtract))
                    if piece == 6:
                        step(dve.tensor_tensor(ge[:], other, mine, ALU.is_equal))
                        done(5)
                        step(dve.tensor_tensor(ge[:], ge[:], tri[:].unsqueeze(1).to_broadcast([P, 4, E, E]),
                                               ALU.mult))
                        done(6)
                        step(dve.tensor_tensor(gt[:], gt[:], ge[:], ALU.add))
                    if piece == 7:
                        done(7)
                        step(dve.tensor_reduce(rank[:], gt[:], AX.X, ALU.add))
                        dve.wait_ge(tanh_ready, g + 1)
                        step(dve.tensor_scalar(ep[:], ex[:], 1.0, None, ALU.add))
                        step(dve.tensor_scalar(en[:], ex[:], -1.0, 1.0, ALU.mult, ALU.add))
                        done(8)
                        step(dve.tensor_scalar(rank[:], rank[:], 2.0, tg[:, 2:3], ALU.is_lt, ALU.mult))
                        done(10)
                        step(dve.reciprocal(en[:], en[:]))
                        done(12)
                        step(dve.tensor_tensor(ex[:], ep[:], en[:], ALU.mult))
                        done(13)
                        step(dve.tensor_reduce(es[:], ex[:], AX.X, ALU.add))
                        step(dve.tensor_tensor(comb[:], ex[:], rank[:], ALU.mult))
                    if piece == 8:
                        done(14)
                        step(dve.reciprocal(er[:], es[:]))
                        done(16)
                        step(dve.tensor_tensor(comb[:], comb[:], er[:].unsqueeze(2).to_broadcast([P, 4, E]),
                                               ALU.mult))
                        done(17)
                        step(dve.tensor_copy(comb2[:, :, 0:E].bitcast(F32R), comb[:]))
                        done(18)
                        dve.tensor_tensor(comb2[:, :, E:2 * E], comb[:], comb2[:, :, 0:E], ALU.subtract
                                          ).then_inc(comb_ready, 1)

                def finish(q, j):
                    if j == 3:
                        dve.wait_ge(o_done, q + 1)
                        dve.tensor_tensor(q_xs[:, q], q_xs[:, q], col_ps.rearrange("p (i d) -> p i d", i=4),
                                          ALU.add).then_inc(res_done, 1)
                    if j == 4:
                        dve.wait_ge(res_done, q + 1)
                        dve.wait_ge(silu_done, UNITS)
                        for i in range(4):
                            dve.bn_stats(q_bns[:, q, i].rearrange("p a s -> p (a s)"), q_xs[:, q, i, :]).then_inc(stats, 1)
                    if j == 5:
                        dve.wait_ge(stats, 4 * q + 4)
                        join_stats(dve, stats_step, STATS_STEPS * q, q_bns[:, q], q_mean[:, q, :], q_minus_mean[:, q, :], q_st[:, q],
                                   q_veps[:, q, :])

                def run():
                    program(dve, unit, prepare, finish, lambda: weigh(NQ - 1, UNITS - 1, NQ * UNITS - 1))

                return lambda t: prepare_first(prepare, t), run

            return dict(tensor=tensor, scalar=scalar, gpsimd=gpsimd, vector=vector, xT_done=xT_done,
                                   up_done=up_done, y_done=y_done, combT_ready=combT_ready, oT_ready=oT_ready,
                                   o_done=o_done, res_done=res_done)

        def channel_mixing():
            room = vc[:].rearrange("p b a l d -> p (b a l d)").rearrange("p (n u t) -> p n u t", u=2, t=512)
            xn_f = au[:].rearrange("p u (i d) -> p u i d", i=4)
            xk, xr, rs, kr, kk, ov = (room[:, i] for i in range(6))
            prev_k, prev_r = (room[:, i].rearrange("p u (i t) -> p u i t", i=4) for i in (6, 7))

            cleared = sem("f_cleared")
            xn_ready = sem("f_xn_ready")
            xT_done = sem("f_xT_done")
            prev_ready = sem("f_prev_ready")
            mix_ready = sem("f_mix_ready")
            k_done = sem("f_k_done")
            r_done = sem("f_r_done")
            relu_ready = sem("f_relu_ready")
            sigmoid_ready = sem("f_sigmoid_ready")
            kk_ready = sem("f_kk_ready")
            v_done = sem("f_v_done")
            ov_ready = sem("f_ov_ready")
            o_done = sem("f_o_done")
            res_done = sem("f_res_done")

            xT_ps, k_ps, r_ps = (lambda n: pbank(n % 2)), (lambda n: pbank(2 + n % 2)), (lambda n: pbank(4 + n % 2))
            v_ps, o_ps = pbank(6), pbank(7)

            def gpsimd(pool):
                pool.wait_ge(att1["vbd_ready"], 2 * B)
                pool.memset(prev_k[:, :, :, 0:1], 0.0).then_inc(cleared, 1)
                pool.memset(prev_r[:, :, :, 0:1], 0.0).then_inc(cleared, 1)

            def vector(dve):
                def normalise(n):
                    if n >= 2:
                        dve.wait_ge(xT_done, n - 1)
                    dve.wait_ge(att1["rstd_ready"], n + 1)
                    for i in range(4):
                        b = 4 * n + i
                        dve.tensor_scalar(xn_f[:, n % 2, i, :], xs[:, b, :], mean[:, b:b + 1], rstd[:, b:b + 1],
                                          ALU.subtract, ALU.mult).then_inc(xn_ready, 1)

                def mix(n):
                    u = n % 2
                    for i, (dst, add, mu) in enumerate(((xk, prev_k, mus[:, 1:2]), (xr, prev_r, mus[:, 0:1]))):
                        dve.wait_ge(prev_ready, 2 * n + 2)
                        if n >= 2:
                            dve.wait_ge((k_done, r_done)[i], n - 1)
                        dve.scalar_tensor_tensor(dst[:, u, :], xT_ps(n), mu, add[:, u].rearrange("p i t -> p (i t)"),
                                                 ALU.mult, ALU.add).then_inc(mix_ready, 1)

                def square(n):
                    u = n % 2
                    dve.wait_ge(relu_ready, n + 1)
                    if n >= 2:
                        dve.wait_ge(v_done, n - 1)
                    dve.tensor_tensor(kk[:, u, :], kr[:, u, :], k_ps(n), ALU.mult).then_inc(kk_ready, 1)

                def gate(n):
                    u = n % 2
                    dve.wait_ge(v_done, n + 1)
                    dve.wait_ge(sigmoid_ready, n + 1)
                    if n >= 2:
                        dve.wait_ge(o_done, n - 1)
                    dve.scalar_tensor_tensor(ov[:, u, :], v_ps, tg[:, 3:4], rs[:, u, :], ALU.mult, ALU.mult
                                             ).then_inc(ov_ready, 1)

                def residual(n):
                    dve.wait_ge(o_done, n + 1)
                    xq = xs[:, 4 * n:4 * n + 4, :]
                    dve.tensor_tensor(xq, xq, o_ps.rearrange("p (i d) -> p i d", i=4), ALU.add
                                      ).then_inc(res_done, 1)

                def first(t):
                    if t == B + 1:
                        normalise(0)

                def run():
                    dve.wait_ge(att1["vbd_ready"], 2 * B)
                    for n in range(NQ + 1):
                        if n < NQ:
                            mix(n)
                        if n + 1 < NQ:
                            normalise(n + 1)
                        if n >= 1:
                            gate(n - 1)
                        if n < NQ:
                            square(n)
                        if n >= 1:
                            residual(n - 1)

                return first, run

            def tensor(pe):
                def transpose_in(n):
                    pe.wait_ge(xn_ready, 4 * n + 4)
                    if n >= 2:
                        pe.wait_ge(mix_ready, 2 * n - 2)
                    for i in range(4):
                        mm = pe.transpose(xT_ps(n)[:, P * i:P * i + P], xn_f[:, n % 2, i, :], ident[:])
                    mm.then_inc(xT_done, 1)

                def features(n):
                    u = n % 2
                    pe.wait_ge(mix_ready, 2 * n + 1)
                    if n >= 2:
                        pe.wait_ge(kk_ready, n - 1)
                    pe.matmul(k_ps(n), w_kT[:], xk[:, u, :], start=True, stop=True).then_inc(k_done, 1)
                    pe.wait_ge(mix_ready, 2 * n + 2)
                    if n >= 2:
                        pe.wait_ge(sigmoid_ready, n - 1)
                    pe.matmul(r_ps(n), w_rT[:], xr[:, u, :], start=True, stop=True).then_inc(r_done, 1)

                def values(n):
                    pe.wait_ge(kk_ready, n + 1)
                    if n >= 1:
                        pe.wait_ge(ov_ready, n)
                    pe.matmul(v_ps, w_vT[:], kk[:, n % 2, :], start=True, stop=True).then_inc(v_done, 1)

                def transpose_out(n):
                    pe.wait_ge(ov_ready, n + 1)
                    if n >= 1:
                        pe.wait_ge(res_done, n)
                    for i in range(4):
                        mm = pe.transpose(o_ps[:, P * i:P * i + P], ov[:, n % 2, P * i:P * i + P], ident[:])
                    mm.then_inc(o_done, 1)

                pe.wait_ge(att1["pT_ready"], 3 * B)
                pe.wait_ge(att1["oT_ready"], B)
                pe.wait_ge(att1["out_read"], B)
                pe.wait_ge(att1["shifted"], 3 * B)
                transpose_in(0)
                for n in range(NQ + 1):
                    if n < NQ:
                        features(n)
                    if n + 1 < NQ:
                        transpose_in(n + 1)
                    if n >= 1:
                        transpose_out(n - 1)
                    if n < NQ:
                        values(n)

            def scalar(act):
                def before(n):
                    act.wait_ge(xT_done, n + 1)
                    act.wait_ge(cleared, 2)
                    if n >= 2:
                        act.wait_ge(mix_ready, 2 * n - 2)
                    for dst, col in ((prev_k, 3), (prev_r, 2)):
                        act.activation(dst[:, n % 2, :, 1:P],
                                       xT_ps(n).rearrange("p (i t) -> p i t", i=4)[:, :, 0:P - 1], ACT.Copy,
                                       scale=mus[:, col:col + 1]).then_inc(prev_ready, 1)

                load_functions(act, ACT.Sigmoid)
                before(0)
                for n in range(NQ):
                    u = n % 2
                    act.wait_ge(k_done, n + 1)
                    if n >= 2:
                        act.wait_ge(kk_ready, n - 1)
                    act.activation(kr[:, u, :], k_ps(n), ACT.Relu).then_inc(relu_ready, 1)
                    if n + 1 < NQ:
                        before(n + 1)
                    act.wait_ge(r_done, n + 1)
                    if n >= 2:
                        act.wait_ge(ov_ready, n - 1)
                    act.activation(rs[:, u, :], r_ps(n), ACT.Sigmoid).then_inc(sigmoid_ready, 1)

            def sync(sp):
                for n in range(NQ):
                    sp.wait_ge(res_done, n + 1)
                    sp.dma_start(out_dram[:, 4 * n:4 * n + 4, :], xs[:, 4 * n:4 * n + 4, :]).then_inc(out_stored, 16)
                sp.wait_ge(out_stored, 16 * NQ)

            return dict(gpsimd=gpsimd, tensor=tensor, scalar=scalar, vector=vector, sync=sync)

        moe, mixing = experts(), channel_mixing()

        def at_once(*_):
            pass

        with nc.Block() as block:
            @block.gpsimd
            def _(pool):
                def keys_next():
                    pool.wait_ge(att0["scored"], 2 * B)
                    att1["build_first_keys"](pool)

                def values_next():
                    pool.wait_ge(att0["pv_done"], B)
                    att1["build_first_values"](pool)

                att0["gpsimd"](pool, keys_next, values_next)
                moe["gpsimd"](pool)
                att1["gpsimd"](pool, lambda: mixing["gpsimd"](pool), at_once)

            @block.tensor
            def _(pe):
                def banks_read(pe):
                    pe.wait_ge(moe["up_done"], 2 * E * NQ)

                def score_banks_read():
                    pe.wait_ge(moe["y_done"], 2 * E * NQ)
                    pe.wait_ge(moe["combT_ready"], NQ)
                    pe.wait_ge(moe["oT_ready"], NQ)
                    pe.wait_ge(moe["res_done"], NQ)

                prepare_first, run = moe["tensor"](pe)
                att0["tensor"](pe, at_once, at_once, prepare_first)
                run()
                att1["tensor"](pe, banks_read, score_banks_read, at_once)
                mixing["tensor"](pe)

            @block.scalar
            def _(act):
                def buffers_free(act):
                    load_functions(act, ACT.Exp)
                    act.wait_ge(moe["o_done"], NQ)
                    act.wait_ge(moe["up_done"], 2 * E * NQ)

                def normalise_next():
                    act.wait_ge(moe["xT_done"], NQ)
                    act.wait_ge(experts_rstd, 1)
                    att1["normalise"](act, 0, 0)

                prepare_first, run = moe["scalar"](act)
                att0["normalise"](act, 0, 0)
                att0["scalar"](act, at_once, prepare_first)
                run(normalise_next)
                att1["scalar"](act, buffers_free, at_once)
                mixing["scalar"](act)

            @block.vector
            def _(dve):
                prepare_first, run = moe["vector"](dve)
                att0["vector"](dve, prepare_first)
                run()
                first, mix_all = mixing["vector"](dve)
                att1["vector"](dve, first)
                mix_all()

            @block.sync
            def _(sp):
                mixing["sync"](sp)


_INS = ['x', 'ctx_768', 'mask_BxS_bk0', 'g_xattn', 'g_ffn', 'L0_xattn_wq', 'L0_xattn_bq', 'L0_xattn_wk',
        'L0_xattn_bk', 'L0_xattn_wv', 'L0_xattn_bv', 'L0_xattn_wo', 'L0_xattn_bo', 'L0_ffn_w1', 'L0_ffn_w2',
        'L0_ffn_router_w', 'L1_xattn_Wq', 'L1_xattn_Wkv', 'L1_ffn_W_r', 'L1_ffn_W_k', 'L1_ffn_W_v', 'L1_ffn_mu_r',
        'L1_ffn_mu_k']


def kernel(**inputs):
    import numpy as _np
    import concourse.bacc as _bacc
    from concourse import mybir as _mybir
    from concourse.bass_utils import run_bass_kernel_spmd as _run

    nc = _bacc.Bacc("TRN2", target_bir_lowering=False, num_devices=1)
    arrays, args = {}, []
    for name in _INS:
        a = _np.ascontiguousarray(inputs[name])
        arrays[f"in_{name}_dram"] = a
        args.append(nc.dram_tensor(f"in_{name}_dram", a.shape, _mybir.dt.from_np(a.dtype), kind="ExternalInput").ap())
    shape = inputs["x"].shape
    out = nc.dram_tensor("out_dram", shape, _mybir.dt.float32, kind="ExternalOutput").ap()
    flamingo_kernel(nc, *args, out)
    r = _run(nc, [arrays], core_ids=[0])
    return r.results[0]["out_dram"]
```
